# Optimizing a Trainium2 kernel written in Bass

```python
import numpy as np
import jax
import jax.numpy as jnp

def _softmax(x, axis=-1):
    return jax.nn.softmax(x, axis=axis)

def _gelu(x):
    return jax.nn.gelu(x, approximate=True)

def _silu(x):
    return jax.nn.silu(x)

def _sigmoid(x):
    return jax.nn.sigmoid(x)

def _layernorm(x, axis=-1, eps=1e-05):
    m = jnp.mean(x, axis=axis, keepdims=True)
    v = jnp.var(x, axis=axis, keepdims=True)
    return (x - m) / jnp.sqrt(v + eps)

def _scatter_add(tgt, idx, src, axis=0):
    return tgt.at[idx].add(src)

def _segment_sum(src, seg, n):
    return jax.ops.segment_sum(src, seg, n)
kernel_name = 'mk_decoder_postln_d2_seqx_r4_f9eee0'

def setup_inputs(seed: int=0):
    np.random.seed(seed)
    _w = jnp.asarray

    def _rec_inputs():
        import jax
        import jax.numpy as jnp
        _rk = jax.random.key(seed)
        x = -0.000125 + 0.9999 * jax.random.normal(jax.random.fold_in(_rk, 1), (8, 256, 256), jnp.float32)
        _lenS = 256 - jax.random.randint(jax.random.fold_in(_rk, 7), (8,), 0, max(1, 256 // 4) + 1, jnp.int32)
        _lenS2 = 256 - jax.random.randint(jax.random.fold_in(_rk, 8), (8,), 0, max(1, 256 // 4) + 1, jnp.int32)
        _ctx_1024P = jax.random.normal(jax.random.fold_in(_rk, 11), (8, 16, 256), jnp.float32)
        _ctx_1024c = jax.random.dirichlet(jax.random.fold_in(_rk, 511), 0.3 * jnp.ones((16,), jnp.float32), (8, 256))
        _ctx_1024t = jnp.einsum('bsk,bkd->bsd', _ctx_1024c, _ctx_1024P)
        _ctx_1024t = _ctx_1024t * jax.lax.rsqrt(jnp.mean(jnp.square(_ctx_1024t)) + 1e-12) * 0.953939
        ctx_1024 = -1.52775e-05 + 0.999936 * (_ctx_1024t + 0.3 * jax.random.normal(jax.random.fold_in(_rk, 611), (8, 256, 256), jnp.float32))
        _validS = jnp.arange(256)[None, :] < _lenS[:, None]
        _validS2 = jnp.arange(256)[None, :] < _lenS2[:, None]
        _causal = jnp.tril(jnp.ones((256, 256), dtype=bool))
        mask_Bx1x1xS2_if1 = jnp.where(jnp.ones((8, 1, 1, 256), dtype=bool), 1, 0).astype(jnp.int32)
        return (x, ctx_1024, _lenS2, mask_Bx1x1xS2_if1)
    x, ctx_1024, _lenS2, mask_Bx1x1xS2_if1 = _rec_inputs()

    def _L0_attn_setup():
        import jax, jax.numpy as jnp
        import numpy as np
        DIM_IN, DIM_K, DIM_V, N_QUERY = (256, 128, 128, 8)

        def _kaiming_uniform(key, shape):
            fan_in = shape[-2] if len(shape) > 1 else shape[-1]
            gain = 1.0 / np.sqrt(3.0)
            bound = gain * np.sqrt(3.0 / fan_in)
            return jax.random.uniform(key, shape, jnp.float32, -bound, bound)
        key = jax.random.key(seed)
        kx, kq, kk, kv, ko = jax.random.split(key, 5)
        x = jax.random.normal(kx, (4, 512, DIM_IN), dtype=jnp.float32)
        proj_q = _kaiming_uniform(kq, (N_QUERY, DIM_IN, DIM_K))
        proj_k = _kaiming_uniform(kk, (DIM_IN, DIM_K))
        proj_v = _kaiming_uniform(kv, (DIM_IN, DIM_V))
        proj_o = _kaiming_uniform(ko, (N_QUERY, DIM_IN, DIM_V))
        return {'x': x, 'proj_q': proj_q, 'proj_k': proj_k, 'proj_v': proj_v, 'proj_o': proj_o}
    _L0_attn_all = _L0_attn_setup()
    _L0_attn_in = {k: v for k, v in _L0_attn_all.items() if k in ('proj_q', 'proj_k', 'proj_v', 'proj_o')}
    del _L0_attn_all

    def _L0_xattn_setup():
        import jax, jax.numpy as jnp
        import numpy as np
        B, S, D, E = (16, 512, 256, 256)
        NEG = -10000000000000.0
        key = jax.random.key(seed)
        k1, k2, k3, k4, k5, k6 = jax.random.split(key, 6)
        return {'Q': jax.random.normal(k1, (B, S, D), dtype=jnp.float32), 'K': jax.random.normal(k2, (B, S, D), dtype=jnp.float32), 'V': jax.random.normal(k3, (B, S, D), dtype=jnp.float32), 'pad_idxs': jax.random.randint(k4, (B,), 0, S, dtype=jnp.int64), 'W': jax.random.normal(k5, (D, E), dtype=jnp.float32) * (1.0 / np.sqrt(D)), 'b': jax.random.normal(k6, (E,), dtype=jnp.float32) * 0.01}
    _L0_xattn_all = _L0_xattn_setup()
    _L0_xattn_in = {k: v for k, v in _L0_xattn_all.items() if k in ('W', 'b')}
    del _L0_xattn_all

    def _L0_ffn_setup():
        import jax, jax.numpy as jnp
        import numpy as np
        EPS = 1e-05
        TOP_K = 2

        def _rmsnorm(x, w):
            xf = x.astype(jnp.float32)
            rms = jax.lax.rsqrt(jnp.mean(xf * xf, axis=-1, keepdims=True) + EPS)
            return (xf * rms).astype(x.dtype) * w

        def _attention(x, wq, wk, wv, wo, num_heads=16):
            B, S, H = x.shape
            D = H // num_heads
            q = (x @ wq.T).reshape(B, S, num_heads, D)
            k = (x @ wk.T).reshape(B, S, num_heads, D)
            v = (x @ wv.T).reshape(B, S, num_heads, D)
            scale = 1.0 / jnp.sqrt(jnp.float32(D)).astype(x.dtype)
            scores = jnp.einsum('bqhd,bkhd->bhqk', q, k) * scale
            probs = jax.nn.softmax(scores, axis=-1)
            out = jnp.einsum('bhqk,bkhd->bqhd', probs, v).reshape(B, S, H)
            return out @ wo.T

        def _moe(x, gate_w, w1, w2, w3):
            B, S, H = x.shape
            xf = x.reshape(-1, H)
            logits = xf @ gate_w.T
            rw, sel = jax.lax.top_k(logits, TOP_K)
            rw = jax.nn.softmax(rw.astype(jnp.float32), axis=-1).astype(x.dtype)
            E = gate_w.shape[0]
            out = jnp.zeros_like(xf)
            for e in range(E):
                we = jnp.sum(jnp.where(sel == e, rw, 0.0), axis=-1)
                h = jax.nn.silu(xf @ w1[e].T) * (xf @ w3[e].T)
                out = out + h @ w2[e].T * we[:, None]
            return out.reshape(B, S, H)
        key = jax.random.key(seed)
        ks = jax.random.split(key, 10)
        H, I, E, NH = (256, 512, 8, 16)
        B, S = (2, 512)
        s = 0.02
        return {'x': jax.random.normal(ks[0], (B, S, H), jnp.float32), 'ln1_w': jnp.ones((H,), jnp.float32), 'ln2_w': jnp.ones((H,), jnp.float32), 'wq': jax.random.normal(ks[1], (H, H), jnp.float32) * s, 'wk': jax.random.normal(ks[2], (H, H), jnp.float32) * s, 'wv': jax.random.normal(ks[3], (H, H), jnp.float32) * s, 'wo': jax.random.normal(ks[4], (H, H), jnp.float32) * s, 'gate_w': jax.random.normal(ks[5], (E, H), jnp.float32) * s, 'w1': jax.random.normal(ks[6], (E, I, H), jnp.float32) * s, 'w2': jax.random.normal(ks[7], (E, H, I), jnp.float32) * s, 'w3': jax.random.normal(ks[8], (E, I, H), jnp.float32) * s}
    _L0_ffn_all = _L0_ffn_setup()
    _L0_ffn_in = {k: v for k, v in _L0_ffn_all.items() if k in ('ln1_w', 'ln2_w', 'wq', 'wk', 'wv', 'wo', 'gate_w', 'w1', 'w2', 'w3')}
    del _L0_ffn_all

    def _L1_attn_setup():
        import jax, jax.numpy as jnp
        import numpy as np
        B, T, D = (8, 1024, 256)

        def _ssm_scan(a_bc, bx):

            def combine(e1, e2):
                a1, u1 = e1
                a2, u2 = e2
                return (a1 * a2, a2 * u1 + u2)
            _, y = jax.lax.associative_scan(combine, (a_bc, bx), axis=1)
            return y
        key = jax.random.key(seed)
        k_x, k_a, k_b, k_w, k_bo = jax.random.split(key, 5)
        x = jax.random.normal(k_x, (B, T, D), dtype=jnp.float32)
        a = jax.random.normal(k_a, (D,), dtype=jnp.float32) * 0.5
        b = jax.random.normal(k_b, (D,), dtype=jnp.float32)
        w_out = jax.random.normal(k_w, (D, D), dtype=jnp.float32) * (1.0 / np.sqrt(D))
        b_out = jax.random.normal(k_bo, (D,), dtype=jnp.float32) * 0.01
        return {'x': x, 'a': a, 'b': b, 'w_out': w_out, 'b_out': b_out}
    _L1_attn_all = _L1_attn_setup()
    _L1_attn_in = {k: v for k, v in _L1_attn_all.items() if k in ('a', 'b', 'w_out', 'b_out')}
    del _L1_attn_all

    def _L1_xattn_setup():
        import jax, jax.numpy as jnp
        import numpy as np
        EMBED = 256
        HEADS = 16
        HEAD_DIM = EMBED // HEADS
        key = jax.random.key(seed)
        ks = jax.random.split(key, 12)
        N, L, E = (4, 512, EMBED)
        s = 1.0 / np.sqrt(E)
        return {'values': jax.random.normal(ks[0], (N, L, E), jnp.float32), 'keys': jax.random.normal(ks[1], (N, L, E), jnp.float32), 'query': jax.random.normal(ks[2], (N, L, E), jnp.float32), 'mask': jnp.ones((N, 1, 1, L), jnp.int32), 'Wv': jax.random.normal(ks[3], (E, E), jnp.float32) * s, 'bv': jnp.zeros((E,), jnp.float32), 'Wk': jax.random.normal(ks[4], (E, E), jnp.float32) * s, 'bk': jnp.zeros((E,), jnp.float32), 'Wq': jax.random.normal(ks[5], (E, E), jnp.float32) * s, 'bq': jnp.zeros((E,), jnp.float32), 'Wo': jax.random.normal(ks[6], (E, E), jnp.float32) * s, 'bo': jnp.zeros((E,), jnp.float32)}
    _L1_xattn_all = _L1_xattn_setup()
    _L1_xattn_in = {k: v for k, v in _L1_xattn_all.items() if k in ('Wv', 'bv', 'Wk', 'bk', 'Wq', 'bq', 'Wo', 'bo')}
    del _L1_xattn_all

    def _L1_ffn_setup():
        import jax, jax.numpy as jnp
        import numpy as np
        D_MODEL = 256
        D_FF = 1024
        NUM_EXPERTS = 8
        B, N = (16, 256)
        key = jax.random.key(seed)
        ks = jax.random.split(key, 7)
        s_in = 1.0 / np.sqrt(D_MODEL)
        s_ff = 1.0 / np.sqrt(D_FF)
        return {'x': jax.random.normal(ks[0], (B, N, D_MODEL), dtype=jnp.float32), 'Wr': jax.random.uniform(ks[1], (D_MODEL, NUM_EXPERTS), jnp.float32, -s_in, s_in), 'br': jax.random.uniform(ks[2], (NUM_EXPERTS,), jnp.float32, -s_in, s_in), 'W1': jax.random.uniform(ks[3], (NUM_EXPERTS, D_MODEL, D_FF), jnp.float32, -s_in, s_in), 'b1': jax.random.uniform(ks[4], (NUM_EXPERTS, D_FF), jnp.float32, -s_in, s_in), 'W2': jax.random.uniform(ks[5], (NUM_EXPERTS, D_FF, D_MODEL), jnp.float32, -s_ff, s_ff), 'b2': jax.random.uniform(ks[6], (NUM_EXPERTS, D_MODEL), jnp.float32, -s_ff, s_ff)}
    _L1_ffn_all = _L1_ffn_setup()
    _L1_ffn_in = {k: v for k, v in _L1_ffn_all.items() if k in ('Wr', 'br', 'W1', 'b1', 'W2', 'b2')}
    del _L1_ffn_all
    return {'x': x, 'ctx_1024': ctx_1024, '_lenS2': _lenS2, 'mask_Bx1x1xS2_if1': mask_Bx1x1xS2_if1, 'L0_attn_proj_q': _L0_attn_in['proj_q'], 'L0_attn_proj_k': _L0_attn_in['proj_k'], 'L0_attn_proj_v': _L0_attn_in['proj_v'], 'L0_attn_proj_o': _L0_attn_in['proj_o'], 'L0_xattn_W': _L0_xattn_in['W'], 'L0_xattn_b': _L0_xattn_in['b'], 'L0_ffn_ln1_w': _L0_ffn_in['ln1_w'], 'L0_ffn_ln2_w': _L0_ffn_in['ln2_w'], 'L0_ffn_wq': _L0_ffn_in['wq'], 'L0_ffn_wk': _L0_ffn_in['wk'], 'L0_ffn_wv': _L0_ffn_in['wv'], 'L0_ffn_wo': _L0_ffn_in['wo'], 'L0_ffn_gate_w': _L0_ffn_in['gate_w'], 'L0_ffn_w1': _L0_ffn_in['w1'], 'L0_ffn_w2': _L0_ffn_in['w2'], 'L0_ffn_w3': _L0_ffn_in['w3'], 'L1_attn_a': _L1_attn_in['a'], 'L1_attn_b': _L1_attn_in['b'], 'L1_attn_w_out': _L1_attn_in['w_out'], 'L1_attn_b_out': _L1_attn_in['b_out'], 'L1_xattn_Wv': _L1_xattn_in['Wv'], 'L1_xattn_bv': _L1_xattn_in['bv'], 'L1_xattn_Wk': _L1_xattn_in['Wk'], 'L1_xattn_bk': _L1_xattn_in['bk'], 'L1_xattn_Wq': _L1_xattn_in['Wq'], 'L1_xattn_bq': _L1_xattn_in['bq'], 'L1_xattn_Wo': _L1_xattn_in['Wo'], 'L1_xattn_bo': _L1_xattn_in['bo'], 'L1_ffn_Wr': _L1_ffn_in['Wr'], 'L1_ffn_br': _L1_ffn_in['br'], 'L1_ffn_W1': _L1_ffn_in['W1'], 'L1_ffn_b1': _L1_ffn_in['b1'], 'L1_ffn_W2': _L1_ffn_in['W2'], 'L1_ffn_b2': _L1_ffn_in['b2']}

def reference(x, ctx_1024, _lenS2, mask_Bx1x1xS2_if1, L0_attn_proj_q, L0_attn_proj_k, L0_attn_proj_v, L0_attn_proj_o, L0_xattn_W, L0_xattn_b, L0_ffn_ln1_w, L0_ffn_ln2_w, L0_ffn_wq, L0_ffn_wk, L0_ffn_wv, L0_ffn_wo, L0_ffn_gate_w, L0_ffn_w1, L0_ffn_w2, L0_ffn_w3, L1_attn_a, L1_attn_b, L1_attn_w_out, L1_attn_b_out, L1_xattn_Wv, L1_xattn_bv, L1_xattn_Wk, L1_xattn_bk, L1_xattn_Wq, L1_xattn_bq, L1_xattn_Wo, L1_xattn_bo, L1_ffn_Wr, L1_ffn_br, L1_ffn_W1, L1_ffn_b1, L1_ffn_W2, L1_ffn_b2):
    import jax
    import jax.numpy as jnp

    def _L0_attn_ref(x, proj_q, proj_k, proj_v, proj_o):
        import jax, jax.numpy as jnp
        import numpy as np
        DIM_IN, DIM_K, DIM_V, N_QUERY = (256, 128, 128, 8)

        def _kaiming_uniform(key, shape):
            fan_in = shape[-2] if len(shape) > 1 else shape[-1]
            gain = 1.0 / np.sqrt(3.0)
            bound = gain * np.sqrt(3.0 / fan_in)
            return jax.random.uniform(key, shape, jnp.float32, -bound, bound)
        Q = jnp.einsum('bnd,hdk->bhnk', x, proj_q)
        K = jnp.einsum('bmd,dk->bmk', x, proj_k)
        V = jnp.einsum('bmd,dv->bmv', x, proj_v)
        logits = jnp.einsum('bhnk,bmk->bhnm', Q, K)
        weights = jax.nn.softmax(logits, axis=-1)
        O = jnp.einsum('bhnm,bmv->bhnv', weights, V)
        Y = jnp.einsum('bhnv,hdv->bnd', O, proj_o)
        return Y

    def _L0_xattn_ref(Q, K, V, pad_idxs, W, b):
        import jax, jax.numpy as jnp
        import numpy as np
        B, S, D, E = (16, 512, 256, 256)
        NEG = -10000000000000.0
        d = Q.shape[2]
        scores = jnp.einsum('bqd,bkd->bqk', Q, K) / jnp.sqrt(jnp.asarray(d, Q.dtype))
        idx = jnp.arange(scores.shape[1])
        p = pad_idxs[:, None, None]
        mask = (idx[None, :, None] >= p) & (idx[None, None, :] >= p)
        scores = jnp.where(mask, jnp.asarray(NEG, scores.dtype), scores)
        attn = jax.nn.softmax(scores, axis=2)
        out = jnp.einsum('bqk,bkd->bqd', attn, V)
        return out @ W + b

    def _L0_ffn_ref(x, ln1_w, ln2_w, wq, wk, wv, wo, gate_w, w1, w2, w3):
        import jax, jax.numpy as jnp
        import numpy as np
        EPS = 1e-05
        TOP_K = 2

        def _rmsnorm(x, w):
            xf = x.astype(jnp.float32)
            rms = jax.lax.rsqrt(jnp.mean(xf * xf, axis=-1, keepdims=True) + EPS)
            return (xf * rms).astype(x.dtype) * w

        def _attention(x, wq, wk, wv, wo, num_heads=16):
            B, S, H = x.shape
            D = H // num_heads
            q = (x @ wq.T).reshape(B, S, num_heads, D)
            k = (x @ wk.T).reshape(B, S, num_heads, D)
            v = (x @ wv.T).reshape(B, S, num_heads, D)
            scale = 1.0 / jnp.sqrt(jnp.float32(D)).astype(x.dtype)
            scores = jnp.einsum('bqhd,bkhd->bhqk', q, k) * scale
            probs = jax.nn.softmax(scores, axis=-1)
            out = jnp.einsum('bhqk,bkhd->bqhd', probs, v).reshape(B, S, H)
            return out @ wo.T

        def _moe(x, gate_w, w1, w2, w3):
            B, S, H = x.shape
            xf = x.reshape(-1, H)
            logits = xf @ gate_w.T
            rw, sel = jax.lax.top_k(logits, TOP_K)
            rw = jax.nn.softmax(rw.astype(jnp.float32), axis=-1).astype(x.dtype)
            E = gate_w.shape[0]
            out = jnp.zeros_like(xf)
            for e in range(E):
                we = jnp.sum(jnp.where(sel == e, rw, 0.0), axis=-1)
                h = jax.nn.silu(xf @ w1[e].T) * (xf @ w3[e].T)
                out = out + h @ w2[e].T * we[:, None]
            return out.reshape(B, S, H)
        h = x + _attention(_rmsnorm(x, ln1_w), wq, wk, wv, wo)
        h = h + _moe(_rmsnorm(h, ln2_w), gate_w, w1, w2, w3)
        return h

    def _L1_attn_ref(x, a, b, w_out, b_out):
        import jax, jax.numpy as jnp
        import numpy as np
        B, T, D = (8, 1024, 256)

        def _ssm_scan(a_bc, bx):

            def combine(e1, e2):
                a1, u1 = e1
                a2, u2 = e2
                return (a1 * a2, a2 * u1 + u2)
            _, y = jax.lax.associative_scan(combine, (a_bc, bx), axis=1)
            return y
        ah = jnp.tanh(a)
        bx = b * x
        a_bc = jnp.broadcast_to(ah, x.shape)
        y = _ssm_scan(a_bc, bx)
        return jnp.einsum('btd,ed->bte', y, w_out) + b_out

    def _L1_xattn_ref(values, keys, query, mask, Wv, bv, Wk, bk, Wq, bq, Wo, bo):
        import jax, jax.numpy as jnp
        import numpy as np
        EMBED = 256
        HEADS = 16
        HEAD_DIM = EMBED // HEADS
        N, L, E = values.shape
        H, D = (HEADS, HEAD_DIM)
        v = (values @ Wv + bv).reshape(N, L, H, D)
        k = (keys @ Wk + bk).reshape(N, L, H, D)
        q = (query @ Wq + bq).reshape(N, L, H, D)
        energy = jnp.einsum('nqhd,nkhd->nhqk', q, k)
        energy = jnp.where(mask == 0, jnp.float32(-1e+20), energy)
        attn = jax.nn.softmax(energy / np.sqrt(D), axis=3)
        out = jnp.einsum('nhqk,nkhd->nqhd', attn, v).reshape(N, L, E)
        return out @ Wo + bo

    def _L1_ffn_ref(x, Wr, br, W1, b1, W2, b2):
        import jax, jax.numpy as jnp
        import numpy as np
        D_MODEL = 256
        D_FF = 1024
        NUM_EXPERTS = 8
        B, N = (16, 256)
        scores = jnp.einsum('bh,he->be', x.mean(axis=1), Wr) + br
        top1 = jnp.argmax(scores, axis=-1)
        w1 = W1[top1]
        c1 = b1[top1]
        w2 = W2[top1]
        c2 = b2[top1]
        h = jax.nn.relu(jnp.einsum('bnh,bhf->bnf', x, w1) + c1[:, None, :])
        out = jnp.einsum('bnf,bfh->bnh', h, w2) + c2[:, None, :]
        return out
    x = _layernorm(x + _L0_attn_ref(x, L0_attn_proj_q, L0_attn_proj_k, L0_attn_proj_v, L0_attn_proj_o), axis=-1)
    x = _layernorm(x + _L0_xattn_ref(x, ctx_1024, ctx_1024, _lenS2, L0_xattn_W, L0_xattn_b), axis=-1)
    x = _layernorm(x + _L0_ffn_ref(x, L0_ffn_ln1_w, L0_ffn_ln2_w, L0_ffn_wq, L0_ffn_wk, L0_ffn_wv, L0_ffn_wo, L0_ffn_gate_w, L0_ffn_w1, L0_ffn_w2, L0_ffn_w3), axis=-1)
    x = _layernorm(x + _L1_attn_ref(x, L1_attn_a, L1_attn_b, L1_attn_w_out, L1_attn_b_out), axis=-1)
    x = _layernorm(x + _L1_xattn_ref(ctx_1024, ctx_1024, x, mask_Bx1x1xS2_if1, L1_xattn_Wv, L1_xattn_bv, L1_xattn_Wk, L1_xattn_bk, L1_xattn_Wq, L1_xattn_bq, L1_xattn_Wo, L1_xattn_bo), axis=-1)
    x = _layernorm(x + _L1_ffn_ref(x, L1_ffn_Wr, L1_ffn_br, L1_ffn_W1, L1_ffn_b1, L1_ffn_W2, L1_ffn_b2), axis=-1)
    return x

_drawn_inputs = setup_inputs


def setup_inputs(seed=0):
    import zlib

    import numpy as np

    out = dict(_drawn_inputs(seed))
    spreads = {'L0_ffn_ln1_w': (1.0, 0.6),
     'L0_ffn_ln2_w': (1.0, 0.6),
     'L1_xattn_bv': (0.0, 0.1),
     'L1_xattn_bk': (0.0, 0.8),
     'L1_xattn_bq': (0.0, 0.431),
     'L1_xattn_bo': (0.0, 0.1)}
    factors = {'L0_xattn_b': 6.672,
     'L0_ffn_wq': 8.0,
     'L0_ffn_wk': 8.0,
     'L0_ffn_gate_w': 8.0,
     'L0_ffn_w1': 7.023,
     'L0_ffn_w2': 6.951,
     'L0_ffn_w3': 6.952,
     'L1_attn_b_out': 8.0,
     'L1_ffn_b1': 4.013,
     'L1_ffn_b2': 3.16}
    for name, (base, spread) in spreads.items():
        noise = np.random.default_rng([zlib.crc32(name.encode()), seed]).standard_normal(out[name].shape)
        drawn = base * np.exp(spread * noise) if base else spread * noise
        out[name] = jnp.asarray(drawn.astype(out[name].dtype))
    for name, factor in factors.items():
        out[name] = (out[name] * factor).astype(out[name].dtype)
    return out
```

```python
from contextlib import ExitStack

import concourse.bass as bass
from concourse import mybir

F32 = mybir.dt.float32
I32 = mybir.dt.int32
U32 = mybir.dt.uint32
ALU = mybir.AluOpType
ACT = mybir.ActivationFunctionType
AX = mybir.AxisListType

P = 128
B = 8
S = 256
D = 256
T2 = S // P
D2 = D // P
H0 = 8
HM = 16
HD = D // HM
E = 8
F0 = 512
FT0 = F0 // P
F1 = 1024
FT1 = F1 // P
TOK = B * S
REG = TOK + P
SLOTS = 2 * TOK // P + E
EPS = 1e-5
NEG0 = -1e13
NEG1 = -1e20
U_A = H0 + 1 + HM
U_C = HM
SQ0 = float(D) ** 0.5
SQM = float(HD) ** 0.5
BIG = 3e38


def build(nc, A, out):
    with ExitStack() as ctx:
        def sb(name, shape, dt=F32):
            return ctx.enter_context(nc.sbuf_tensor("s_" + name, shape, dt))

        def sem(name):
            return ctx.enter_context(nc.semaphore(name))

        rows_d = nc.dram_tensor("rows_by_expert", [E * REG, D], F32, kind="Internal").ap()
        y_d = nc.dram_tensor("expert_out", [SLOTS * P, D], F32, kind="Internal").ap()
        hx_d = nc.dram_tensor("residual", [B, P, T2 * D], F32, kind="Internal").ap()

        bank = [ctx.enter_context(nc.psum_tensor(f"bank{i}", [P, 2, 256], F32)) for i in range(8)]
        sc_ps = bank[0:2]
        pt_ps = bank[2:4]
        W_BANK = (bank[4], bank[7])
        F_BANK = (bank[5], bank[6])

        wq0 = sb("wq0", [P, D2, H0 * P])
        wk0 = sb("wk0", [P, D2, P])
        wv0 = sb("wv0", [P, D2, P])
        wo0 = sb("wo0", [P, H0, D])
        wx = sb("wx", [P, D2, D])
        wqm = sb("wqm", [P, D2, D])
        wkm = sb("wkm", [P, D2, D])
        wvm = sb("wvm", [P, D2, D])
        wom = sb("wom", [P, D2, D])
        wg = sb("wg", [P, D2, E])
        w1 = sb("w1", [P, E, D2, F0])
        w3 = sb("w3", [P, E, D2, F0])
        w2 = sb("w2", [P, E, FT0, D])
        cw = wq0[:].rearrange("p a (c n) -> p (a c) n", n=D)
        wv1, wk1, wq1, wo1 = (cw[:, 2 * i:2 * i + 2, :] for i in range(4))
        wout = wx
        wr = sb("wr", [P, D2, E])

        ident = sb("ident", [P, P])
        upper = sb("upper", [P, P])
        ones = sb("ones", [P, P])
        ki = sb("ki", [P, S])
        qi = sb("qi", [P, T2])
        ei = sb("ei", [P, E])
        ebase = sb("ebase", [P, E])
        thr = sb("thr", [P, TOK // P])
        si = sb("si", [P, SLOTS])
        half = sb("half", [P, T2])
        even = sb("even", [P, 1])
        odd = sb("odd", [P, 1])
        lens_i = sb("lens_i", [P, B], I32)
        lens = sb("lens", [P, B])
        ln1w = sb("ln1w", [P, D2])
        bx = sb("bx", [P, D])
        ln2w = sb("ln2w", [P, D])
        bout, bo1, bv1 = bx, ln2w, sb("bv1", [P, D])
        ah = sb("ah", [P, D2])
        av = sb("av", [P, D2])
        bvec = sb("bvec", [P, D2])
        bq1 = sb("bq1", [P, D2])
        bk1 = sb("bk1", [P, D2])
        bke = sb("bke", [P, D2])
        bko = sb("bko", [P, D2])
        br1 = sb("br1", [1, E])

        def act_tile(name):
            return sb(name, [P, 2, 256])

        x = act_tile("x")
        xT = act_tile("xT")
        cT = act_tile("cT")
        QT = sb("QT", [P, H0, S])
        OT = sb("OT", [P, H0, S])
        KT = sb("KT", [P, S])
        V = sb("V", [P, T2, P])
        probs = [act_tile(f"probs{i}") for i in range(3)]
        probsT = [act_tile(f"probsT{i}") for i in range(2)]
        cW = act_tile("cW")
        r = act_tile("r")
        x1 = act_tile("x1")
        xb = act_tile("xb")
        tT = act_tile("tT")
        mask0 = act_tile("mask0")
        x2 = act_tile("x2")
        nT = act_tile("nT")
        QTm = act_tile("QTm")
        KTe = act_tile("KTe")
        KTo = act_tile("KTo")
        Vm = act_tile("Vm")
        On = act_tile("On")
        h = act_tile("h")
        n2 = act_tile("n2")
        nmax = sb("nmax", [P, 4, T2])
        rs0 = sb("rs0", [P, 3, T2])
        rr0 = sb("rr0", [P, 3, T2])
        rsm = sb("rsm", [P, T2, HM])
        rrm = sb("rrm", [P, T2, HM])

        W1s = QT[:].rearrange("p h n -> p (h n)").rearrange("p (t f) -> p t f", t=D2)
        W2s = OT[:].rearrange("p h n -> p (h n)").rearrange("p (f d) -> p f d", d=D)
        b1s = sb("b1s", [P, FT1])
        b2s = sb("b2s", [P, D])
        hF = wo0[:].rearrange("p h n -> p (h n)").rearrange("p (f n) -> p f n", n=S)
        mask_i = sb("mask_i", [P, S], I32)
        mask1 = sb("mask1", [P, S])

        class Norm:
            def __init__(self, name):
                self.st = sb(name + "_st", [P, T2, 6])
                self.mv = sb(name + "_mv", [P, T2, 2])
                self.ve = sb(name + "_ve", [P, T2])
                self.rstd = sb(name + "_rstd", [P, T2])
                self.stats, self.mean, self.var, self.root = (
                    sem(name + s) for s in ("_stats", "_mean", "_var", "_root"))

        nA, nC, nF = Norm("na"), Norm("nc"), Norm("nf")

        lg = sb("lg", [P, T2, E])
        mx = sb("mx", [P, T2, 8])
        mi = sb("mi", [P, T2, 8], U32)
        mf = sb("mf", [P, T2, 2])
        sel = sb("sel", [P, T2, 2, E])
        cnt = sb("cnt", [P, T2, E])
        dl = sb("dl", [P, T2])
        el = sb("el", [P, T2])
        e1 = sb("e1", [P, T2])
        pk = sb("pk", [P, T2, 2])
        run = sb("run", [P, E])
        rank = sb("rank", [P, T2, E])
        rowsel = sb("rowsel", [P, T2, 2, E])
        rowat = sb("rowat", [P, T2, E])
        posf = sb("posf", [P, T2 * 2])
        posu = sb("posu", [P, T2 * 2], U32)
        sel_all = sb("sel_all", [P, B, T2 * 2 * E])
        rank_all = sb("rank_all", [P, B, T2 * E])
        pk_all = sb("pk_all", [P, B, T2 * 2])
        yu_all = sb("yu_all", [P, B, T2 * 2], U32)
        tiles = sb("tiles", [P, E])
        tcmp = sb("tcmp", [P, E, TOK // P])
        tend = sb("tend", [P, E])
        tbeg = sb("tbeg", [P, E])
        ybase = sb("ybase", [P, E])
        rbase = sb("rbase", [P, E])
        padf = sb("padf", [P, E])
        padu = sb("padu", [P, E], U32)
        pidx = sb("pidx", [P, 1])
        inA = sb("inA", [P, SLOTS, E])
        inB = sb("inB", [P, SLOTS, E])
        slf = sb("slf", [P, 3, SLOTS])
        slot_e = sb("slot_e", [P, SLOTS], I32)
        slot_r = sb("slot_r", [P, SLOTS], I32)
        zero = n2[:, 0, :]
        gidx = sb("gidx", [P, 4], U32)
        yk = [cW, mask0]
        yf = sb("yf", [P, B * T2 * 2])
        ymul = sb("ymul", [P, B * T2, 2, E])

        xg = [x[:, 0, :], x[:, 1, :]]
        xgT = [tT[:, 0, :].rearrange("p (t n) -> p t n", t=2), tT[:, 1, :].rearrange("p (t n) -> p t n", t=2)]
        gate = [QTm[:].rearrange("p a b -> p (a b)"), KTe[:].rearrange("p a b -> p (a b)")]
        hid = [KTo[:].rearrange("p a b -> p (a b)"), Vm[:].rearrange("p a b -> p (a b)")]
        hidT = [On[:].rearrange("p a b -> p (a b)").rearrange("p (f n) -> p f n", n=P),
                h[:].rearrange("p a b -> p (a b)").rearrange("p (f n) -> p f n", n=P)]
        yo = [nT[:, 0, :], nT[:, 1, :]]

        msum = sb("msum", [P, D2])
        lr = sb("lr", [1, E])
        lmx = sb("lmx", [1, 8])
        lmi = sb("lmi", [1, 8], U32)
        x3, x3T, yT, x4, x4T, x5, x5T = x1, tT, nT, x2, xT, h, n2
        qF, kFe, kFo, vF = QTm, KTe, KTo, Vm
        rF, xF = wqm, wkm

        const_in = sem("const_in")
        w0_in = sem("w0_in")
        wA_in = sem("wA_in")
        wM_in = sem("wM_in")
        wC_in = sem("wC_in")
        consts = sem("consts")
        cv = sem("cv")
        xT_in = sem("xT_in")
        x_in = sem("x_in")
        cT_in = sem("cT_in")
        w_filled = [sem("w_filled0"), sem("w_filled1")]
        w_copied = [sem("w_copied0"), sem("w_copied1")]
        f_filled = [sem("f_filled0"), sem("f_filled1")]
        f_copied = [sem("f_copied0"), sem("f_copied1")]
        scores = sem("scores")
        smax = sem("smax")
        expd = sem("expd")
        sums_inv = sem("sums_inv")
        normed = sem("normed")
        turned = sem("turned")
        turned_sb = sem("turned_sb")
        pv = sem("pv")
        x1_ok = sem("x1_ok")
        x2_ok = sem("x2_ok")
        route_pos = sem("route_pos")
        n1_ok = sem("n1_ok")
        xb_ok = sem("xb_ok")
        len_ok = sem("len_ok")
        mask_ok = sem("mask_ok")
        inv_m = sem("inv_m")
        hx_ok = sem("hx_ok")
        hx_out = sem("hx_out")
        n2_ok = sem("n2_ok")
        rt = sem("rt")
        cnt_ok = sem("cnt_ok")
        dl_ok = sem("dl_ok")
        el_ok = sem("el_ok")
        pos_ok = sem("pos_ok")
        scattered = sem("scattered")
        plan = sem("plan")
        padded = sem("padded")
        zeroed = sem("zeroed")
        xg_in = [sem("xg_in0"), sem("xg_in1")]
        b_x = sem("b_x")
        b_xs = sem("b_xs")
        b_h = sem("b_h")
        b_gate = sem("b_gate")
        b_hid = sem("b_hid")
        b_t = sem("b_t")
        b_ts = sem("b_ts")
        b_y = sem("b_y")
        b_ys = sem("b_ys")
        y_out = [sem("y_out0"), sem("y_out1")]
        gi = sem("gi")
        yk_in = sem("yk_in")
        hx_in = sem("hx_in")
        comb1 = sem("comb1")
        comb = sem("comb")
        c_r = sem("c_r")
        x3_ok = sem("x3_ok")
        scan_ok = sem("scan_ok")
        x4_ok = sem("x4_ok")
        x5_ok = sem("x5_ok")
        cb = sem("cb")
        mi_in = sem("mi_in")
        mask1_ok = sem("mask1_ok")
        rt1 = sem("rt1")
        pick_ok = sem("pick_ok")
        ex_in = sem("ex_in")
        f_r = sem("f_r")
        f_out = sem("f_out")
        out_done = sem("out_done")

        def need(eng, s, n):
            if isinstance(n, int) and n <= 0:
                return
            eng.wait_ge(s, n)

        def apart(eng):
            eng.nop(nofuse=True)

        class Work:
            def __init__(self, banks, filled, copied, per, base):
                self.banks, self.filled, self.copied, self.per, self.base = banks, filled, copied, per, base

            def ps(self, i):
                return self.banks[i % 2]

            def n(self, b, i):
                return b * self.per[i % 2] + (self.base[i % 2] + i // 2)

            def free(self, eng, b, i):
                need(eng, self.copied[i % 2], self.n(b, i))

            def full(self, eng, b, i):
                need(eng, self.filled[i % 2], self.n(b, i) + 1)

            def out(self, eng, b, i):
                need(eng, self.copied[i % 2], self.n(b, i) + 1)

            def fill(self, ins, i):
                ins.then_inc(self.filled[i % 2], 1)

            def copy(self, ins, i):
                ins.then_inc(self.copied[i % 2], 1)

        (CTXW, ATTN0, X1T, XATT, N1T, QM, KM, VM, OM, OMT, PROJ, N2T, LOGIT, RANK) = range(8, 22)
        WA = Work(W_BANK, w_filled, w_copied, (11, 11), (0, 0))
        FA = Work(F_BANK, f_filled, f_copied, (3, 2), (0, 0))
        (K1, V1, X3T, SSM, X4T, Q1, O1, O1T, PROJ1, X5T, ROUTE) = range(11)
        WC = Work(W_BANK, w_filled, w_copied, (6, 5), (11 * B, 11 * B))
        FC = Work(F_BANK, f_filled, f_copied, (3, 2), (3 * B, 2 * B))
        U0 = U_A * B

        block = ctx.enter_context(nc.Block())

        @block.sync
        def _(sp):
            for t, name in ((wq0, "wq0"), (wk0, "wk0"), (wv0, "wv0")):
                sp.dma_start(t[:], A[name]).then_inc(w0_in, 16)
            sp.dma_start(xT[:], A["xT"][0]).then_inc(xT_in, 16)
            sp.dma_start(cT[:], A["cT"][0]).then_inc(cT_in, 16)
            sp.dma_start(x[:], A["x"][0]).then_inc(x_in, 16)
            sp.dma_start(lens_i[:], A["lens"].partition_broadcast(P)).then_inc(const_in, 16)
            sp.dma_start(bx[:], A["bx"].partition_broadcast(P)).then_inc(const_in, 16)
            sp.dma_start(ln2w[:], A["ln2w"].partition_broadcast(P)).then_inc(const_in, 16)
            sp.dma_start(bv1[:], A["bv1"].partition_broadcast(P)).then_inc(const_in, 16)
            for t, name in ((ln1w, "ln1w"), (av, "a"), (bvec, "b"), (bq1, "bq1"), (bk1, "bk1"), (br1, "br1"),
                            (wr, "wr")):
                sp.dma_start(t[:], A[name]).then_inc(const_in, 16)
            for t, name in ((wo0, "wo0"), (wx, "wx"), (wqm, "wqm"), (wkm, "wkm"), (wvm, "wvm"), (wom, "wom"),
                            (wg, "wg")):
                sp.dma_start(t[:], A[name]).then_inc(wA_in, 16)

            def loads(b, last):
                for t, name in ((w1, "w1"), (w3, "w3"), (w2, "w2")):
                    sp.dma_start(t[:, bass.ds(b, 1)].rearrange("p e a n -> p (e a n)"),
                                 A[name][bass.ds(b, 1)].rearrange("e p a n -> p (e a n)")).then_inc(wM_in, 16)
                if not last:
                    FA.full(sp, b, 4)
                    sp.dma_start(xT[:], A["xT"][bass.ds(b + 1, 1)].rearrange("e p a n -> p (e a) n")).then_inc(xT_in, 16)
                    WA.out(sp, b, ATTN0)
                    sp.dma_start(x[:], A["x"][bass.ds(b + 1, 1)].rearrange("e p a n -> p (e a) n")).then_inc(x_in, 16)
                    sp.wait_ge(scores, U_A * b + H0 + 1)
                    sp.dma_start(cT[:], A["cT"][bass.ds(b + 1, 1)].rearrange("e p a n -> p (e a) n")).then_inc(cT_in, 16)
                sp.wait_ge(hx_ok, b + 1)
                sp.dma_start(hx_d[bass.ds(b, 1)].rearrange("e p n -> p (e n)"),
                             xb[:].rearrange("p a b -> p (a b)")).then_inc(hx_out, 16)

            loads(0, False)
            with sp.Fori(1, B - 1) as b:
                loads(b, False)
            loads(B - 1, True)

            WA.full(sp, B - 1, RANK)
            for t, name in ((wq1, "wq1"), (wk1, "wk1"), (wv1, "wv1"), (wo1, "wo1")):
                sp.dma_start(t, A[name]).then_inc(wC_in, 16)
            sp.dma_start(wout[:], A["wout"]).then_inc(wC_in, 16)
            sp.wait_ge(n2_ok, B)
            sp.dma_start(bout[:], A["bout"].partition_broadcast(P)).then_inc(wC_in, 16)
            sp.dma_start(bo1[:], A["bo1"].partition_broadcast(P)).then_inc(wC_in, 16)

            sp.wait_ge(plan, 14)
            sp.wait_ge(padded, 16 * E)
            sp.wait_ge(scattered, 64 * B)

            def slot_load(t, p, first):
                s = 2 * t + p
                if not first:
                    sp.wait_ge(b_x, s - 1)
                apart(sp)
                row = sp.value_load(slot_r[0:1, bass.ds(s, 1)], min_val=0, max_val=E * REG - P)
                sp.dma_start(xg[p], rows_d[bass.ds(row, P)]).then_inc(xg_in[p], 16)

            def slot_store(t, p):
                s = 2 * t + p
                sp.wait_ge(b_ys, s + 1)
                sp.dma_start(y_d[bass.ds(s * P, P)], yo[p]).then_inc(y_out[p], 16)

            for p in range(2):
                slot_load(0, p, True)
            with sp.Fori(0, SLOTS // 2 - 1) as t:
                for p in range(2):
                    slot_load(t + 1, p, False)
                    slot_store(t, p)
            for p in range(2):
                slot_store(SLOTS // 2 - 1, p)
            for p in range(2):
                sp.wait_ge(y_out[p], 16 * (SLOTS // 2))

            sp.wait_ge(hx_out, 16 * B)

            def loads_c(b, first):
                if not first:
                    sp.wait_ge(comb, b)
                    WC.full(sp, b - 1, V1)
                sp.dma_start(x[:], hx_d[bass.ds(b, 1)].rearrange("e p n -> p (e n)")).then_inc(hx_in, 16)
                sp.dma_start(cT[:], A["cT"][bass.ds(b, 1)].rearrange("e p a n -> p (e a) n")).then_inc(cT_in, 16)
                if not first:
                    sp.wait_ge(mask1_ok, b)
                sp.dma_start(mask_i[:], A["mask"][bass.ds(b, 1)].rearrange("b n -> (b n)").partition_broadcast(P)).then_inc(mi_in, 16)

            def expert_load(b):
                sp.wait_ge(pick_ok, b + 1)
                if not isinstance(b, int) or b > 0:
                    FC.full(sp, b - 1, 4)
                    FC.out(sp, b - 1, 3)
                    sp.wait_ge(f_r, b)
                apart(sp)
                e = sp.value_load(lmi[0:1, 0:1], min_val=0, max_val=E - 1)
                sp.dma_start(W1s, A["W1"][bass.ds(e, 1)].rearrange("e p a n -> p (e a) n")).then_inc(ex_in, 16)
                sp.dma_start(W2s, A["W2"][bass.ds(e, 1)].rearrange("e p a n -> p (e a) n")).then_inc(ex_in, 16)
                sp.dma_start(b1s[:], A["b1"][bass.ds(e, 1)].rearrange("e p n -> p (e n)")).then_inc(ex_in, 16)
                sp.dma_start(b2s[:], A["b2"][bass.ds(e, 1)].rearrange("b n -> (b n)").partition_broadcast(P)).then_inc(ex_in, 16)

            def store_c(b):
                sp.wait_ge(f_out, b + 1)
                sp.dma_start(out[bass.ds(b, 1)].rearrange("e (a p) n -> p (e a) n", p=P), xF[:]).then_inc(out_done, 16)

            loads_c(0, True)
            loads_c(1, False)
            expert_load(0)
            with sp.Fori(1, B - 1) as b:
                loads_c(b + 1, False)
                store_c(b - 1)
                expert_load(b)
            store_c(B - 2)
            expert_load(B - 1)
            store_c(B - 1)
            sp.wait_ge(out_done, 16 * B)

        @block.gpsimd
        def _(g):
            g.memset(ident[:], 0.0).then_inc(cv, 1)
            g.memset(upper[:], 1.0).then_inc(cv, 1)
            g.memset(ones[:], 1.0).then_inc(consts, 1)
            g.memset(half[:], -0.5).then_inc(consts, 1)
            g.memset(run[:], 0.0).then_inc(consts, 1)
            g.wait_ge(cv, 2)
            g.affine_select(out=ident[:], in_=ident[:], compare_op=ALU.not_equal, fill=1.0, base=0,
                            pattern=[[-1, P]], channel_multiplier=1).then_inc(consts, 1)
            g.affine_select(out=upper[:], in_=upper[:], compare_op=ALU.is_gt, fill=0.0, base=0,
                            pattern=[[1, P]], channel_multiplier=-1).then_inc(consts, 1)
            big = dict(allow_small_or_imprecise_dtypes=True)
            g.iota(ki[:], [[1, S]], base=0, channel_multiplier=0, **big).then_inc(consts, 1)
            g.iota(qi[:], [[P, T2]], base=0, channel_multiplier=1, **big).then_inc(consts, 1)
            g.iota(ei[:], [[1, E]], base=0, channel_multiplier=0, **big).then_inc(consts, 1)
            g.iota(ebase[:], [[REG, E]], base=0, channel_multiplier=0, **big).then_inc(consts, 1)
            g.iota(thr[:], [[P, TOK // P]], base=0, channel_multiplier=0, **big).then_inc(consts, 1)
            g.iota(si[:], [[1, SLOTS]], base=0, channel_multiplier=0, **big).then_inc(consts, 1)
            g.iota(pidx[:], [[1, 1]], base=0, channel_multiplier=1, **big).then_inc(consts, 1)
            g.wait_ge(const_in, 16 * 11)
            g.tensor_copy(lens[:], lens_i[:]).then_inc(len_ok, 1)
            g.wait_ge(len_ok, 1)

            def root(n, k):
                g.wait_ge(n.var, k)
                g.tensor_tensor(n.rstd[:], n.ve[:], half[:], ALU.pow).then_inc(n.root, 1)

            pc = sb("pc", [P, 1])
            qn = sb("qn", [P, T2])

            def layer0(b):
                g.tensor_copy(pc[:], lens[:, bass.ds(b, 1)]).then_inc(len_ok, 1)
                g.wait_ge(len_ok, 2 * b + 2)
                apart(g)
                g.tensor_scalar(qn[:], qi[:], pc[:, 0:1], NEG0 * SQ0, ALU.is_ge, ALU.mult).then_inc(len_ok, 1)
                g.wait_ge(len_ok, 2 * b + 3)
                apart(g)
                for t in range(T2):
                    ins = g.tensor_scalar(mask0[:, t, :], ki[:], pc[:, 0:1], qn[:, t:t + 1], ALU.is_ge, ALU.mult)
                ins.then_inc(mask_ok, 1)
                root(nA, 4 * b + 1)
                g.wait_ge(x1_ok, b + 1)
                need(g, hx_out, 16 * b)
                for t in range(T2):
                    ins = g.tensor_tensor(xb[:, t, :], x1[:, t, :], bx[:], ALU.add)
                ins.then_inc(xb_ok, 1)
                root(nA, 4 * b + 2)
                root(nA, 4 * b + 3)
                WA.out(g, b, PROJ)
                g.wait_ge(x2_ok, b + 1)
                g.tensor_tensor(xb[:], h[:], x2[:], ALU.add).then_inc(hx_ok, 1)
                root(nA, 4 * b + 4)
                g.wait_ge(pos_ok, b + 1)
                apart(g)
                for t in range(T2):
                    for k in range(2):
                        j = 2 * t + k
                        g.indirect_dma_start(rows_d, bass.IndirectOffsetOnAxis(ap=posu[:, j:j + 1], axis=0),
                                             n2[:, t, :], None).then_inc(scattered, 16)

            layer0(0)
            with g.Fori(1, B) as b:
                layer0(b)
            g.wait_ge(scattered, 64 * B)
            g.memset(zero, 0.0).then_inc(zeroed, 1)
            g.wait_ge(zeroed, 1)
            g.wait_ge(plan, 14)
            for e in range(E):
                g.indirect_dma_start(rows_d, bass.IndirectOffsetOnAxis(ap=padu[:, e:e + 1], axis=0),
                                     zero, None).then_inc(padded, 16)

            def gather(b):
                need(g, comb, b)
                need(g, yk_in, 64 * b)
                g.tensor_copy(gidx[:], yu_all[:, bass.ds(b, 1), :].rearrange("p b n -> p (b n)")).then_inc(gi, 1)
                g.wait_ge(gi, b + 1)
                apart(g)
                for t in range(T2):
                    for k in range(2):
                        j = 2 * t + k
                        g.indirect_dma_start(yk[k][:, t, :], None, y_d,
                                             bass.IndirectOffsetOnAxis(ap=gidx[:, j:j + 1], axis=0)).then_inc(yk_in, 16)

            def layer1(b, first, last):
                root(nC, 3 * b + 1)
                if not last:
                    gather(b + 1)
                g.wait_ge(x3_ok, b + 1)
                for t in range(T2):
                    ins = g.tensor_tensor(xb[:, t, :], x3[:, t, :], bout[:], ALU.add)
                ins.then_inc(cb, 1)
                root(nC, 3 * b + 2)
                g.wait_ge(x4_ok, b + 1)
                for t in range(T2):
                    ins = g.tensor_tensor(xb[:, t, :], x4[:, t, :], bo1[:], ALU.add)
                ins.then_inc(cb, 1)
                if not first:
                    ffn_part(b - 1)
                root(nC, 3 * b + 3)

            def ffn_part(b):
                g.wait_ge(ex_in, 64 * (b + 1))
                g.wait_ge(x5_ok, b + 1)
                need(g, f_out, b)
                for t in range(T2):
                    ins = g.tensor_tensor(rF[:, t, :], x5[:, t, :], b2s[:], ALU.add)
                ins.then_inc(f_r, 1)
                root(nF, b + 1)

            for p in range(2):
                g.wait_ge(y_out[p], 16 * (SLOTS // 2))
            g.wait_ge(plan, 17)
            g.wait_ge(wC_in, 16 * 7)
            gather(0)
            layer1(0, True, False)
            with g.Fori(1, B - 1) as b:
                layer1(b, False, False)
            layer1(B - 1, False, True)
            ffn_part(B - 1)

        @block.scalar
        def _(a):
            def exps(src, dst, bias, scale, acc, nm):
                a.wait_ge(smax, nm)
                for t in range(T2):
                    ins = a.activation(dst[:, t, :], src[:, t, :], ACT.Exp, bias=bias[:, t:t + 1], scale=scale,
                                       accum_out=acc(t))
                ins.then_inc(expd, 1)

            def copy_f(b, i):
                FA.full(a, b, i)
                ps = FA.ps(i)
                if i > 0:
                    ins = a.activation(QT[:, 2 * i - 2:2 * i, :], ps[:], ACT.Copy)
                else:
                    a.activation(KT[:], ps[:, 0, :], ACT.Copy)
                    ins = a.activation(V[:], ps[:, 1, :].rearrange("p (t n) -> p t n", t=2), ACT.Copy)
                FA.copy(ins, i)

            def copy_w(W, b, i, dst):
                W.full(a, b, i)
                W.copy(a.activation(dst, W.ps(i)[:], ACT.Copy), i)

            for i in range(5):
                copy_f(0, i)

            def layer0(b, last):
                for i in range(H0 + 3):
                    if i < H0:
                        u = U_A * b + i
                        if i >= 3:
                            a.wait_ge(turned, u - 2)
                        exps(sc_ps[i % 2], probs[i % 3], nmax[:, i % 4], 1.0,
                             lambda t: rs0[:, i % 3, t:t + 1], u + 1)
                    if i >= 3:
                        j = i - 3
                        WA.full(a, b, j)
                        WA.copy(a.activation(OT[:, j, :], WA.ps(j)[:, 0, :], ACT.Copy), j)
                copy_w(WA, b, CTXW, cW[:])
                if not last:
                    copy_f(b + 1, 0)
                    copy_f(b + 1, 1)
                copy_w(WA, b, X1T, tT[:])
                exps(probs[2], probs[2], nmax[:, 0], -1.0, lambda t: rs0[:, 0, t:t + 1], U_A * b + H0 + 1)
                if not last:
                    copy_f(b + 1, 2)
                    copy_f(b + 1, 3)
                if not last:
                    copy_f(b + 1, 4)
                WA.full(a, b, N1T)
                for t in range(D2):
                    ins = a.activation(nT[:, t, :], WA.ps(N1T)[:, t, :], ACT.Copy, scale=ln1w[:, t:t + 1])
                WA.copy(ins, N1T)
                WA.full(a, b, QM)
                WA.copy(a.activation(QTm[:], WA.ps(QM)[:], ACT.Copy, scale=1.0 / SQM), QM)
                WA.full(a, b, KM)
                a.activation(KTe[:], WA.ps(KM)[:], ACT.Copy, scale=even[:, 0:1])
                WA.copy(a.activation(KTo[:], WA.ps(KM)[:], ACT.Copy, scale=odd[:, 0:1]), KM)
                for k in range(HM):
                    u = U_A * b + H0 + 1 + k
                    if k >= 3:
                        a.wait_ge(turned, u - 2)
                    exps(sc_ps[k % 2], probs[k % 3], nmax[:, k % 4], 1.0,
                         lambda t: rsm[:, t, k:k + 1], u + 1)
                copy_w(WA, b, OMT, tT[:])
                copy_w(WA, b, N2T, nT[:])
                a.wait_ge(dl_ok, b + 1)
                a.activation(el[:], dl[:], ACT.Exp).then_inc(el_ok, 1)

            a.wait_ge(consts, 14)
            layer0(0, False)
            with a.Fori(1, B - 1) as b:
                layer0(b, False)
            layer0(B - 1, True)
            a.activation(ah[:], av[:], ACT.Tanh).then_inc(consts, 1)

            def slot(s, p, first):
                a.wait_ge(b_x, s + 1)
                if not first:
                    a.wait_ge(b_h, s - 1)
                a.activation(xgT[p], bank[p][:, 0, :].rearrange("p (t n) -> p t n", t=2), ACT.Copy).then_inc(b_xs, 1)
                a.wait_ge(b_h, s + 1)
                if not first:
                    a.wait_ge(b_hid, s - 1)
                a.activation(gate[p], bank[2 + 2 * p][:].rearrange("p a b -> p (a b)"), ACT.Silu).then_inc(b_gate, 1)

            def slot_out(s, p, first):
                a.wait_ge(b_t, s + 1)
                if not first:
                    need(a, b_y, s - 1)
                a.activation(hidT[p], bank[6][:].rearrange("p a (c n) -> p (a c) n", n=P), ACT.Copy).then_inc(b_ts, 1)

            slot(0, 0, True)
            slot_out(0, 0, True)
            slot(1, 1, True)

            def slots(t):
                slot_out(2 * t - 1, 1, False)
                slot(2 * t, 0, False)
                slot_out(2 * t, 0, False)
                slot(2 * t + 1, 1, False)

            slots(1)
            with a.Fori(2, SLOTS // 2) as t:
                slots(t)
            slot_out(SLOTS - 1, 1, False)

            def ffn_up(b, i):
                FC.full(a, b, i)
                if i == 0:
                    a.wait_ge(ex_in, 64 * (b + 1))
                for j in range(2):
                    f = 2 * i + j
                    ins = a.activation(hF[:, f, :], FC.ps(i)[:, j, :], ACT.Relu, bias=b1s[:, f:f + 1])
                FC.copy(ins, i)

            def layer1(b, first):
                WC.full(a, b, K1)
                for t in range(D2):
                    a.activation(kFe[:, t, :], WC.ps(K1)[:, t, :], ACT.Identity, bias=bke[:, t:t + 1],
                                 scale=even[:, 0:1])
                    ins = a.activation(kFo[:, t, :], WC.ps(K1)[:, t, :], ACT.Identity, bias=bko[:, t:t + 1],
                                       scale=odd[:, 0:1])
                WC.copy(ins, K1)
                WC.full(a, b, X3T)
                for t in range(D2):
                    ins = a.activation(x3T[:, t, :], WC.ps(X3T)[:, t, :], ACT.Copy, scale=bvec[:, t:t + 1])
                WC.copy(ins, X3T)
                copy_w(WC, b, X4T, x4T[:])
                WC.full(a, b, Q1)
                for t in range(D2):
                    ins = a.activation(qF[:, t, :], WC.ps(Q1)[:, t, :], ACT.Identity, bias=bq1[:, t:t + 1])
                WC.copy(ins, Q1)
                for k in range(HM):
                    u = U_C * b + (U0 + k)
                    exps(probs[k % 3], probs[k % 3], nmax[:, k % 4], -1.0, lambda t: rsm[:, t, k:k + 1], u + 1)
                    if not first and k in (5, 7, 9, 11):
                        ffn_up(b - 1, (k - 5) // 2)
                copy_w(WC, b, O1T, x3T[:])
                WC.full(a, b, X5T)
                for t in range(D2):
                    ins = a.activation(x5T[:, t, :], WC.ps(X5T)[:, t, :], ACT.Copy, accum_out=msum[:, t:t + 1])
                WC.copy(ins, X5T)

            a.wait_ge(consts, 16)
            layer1(0, True)
            with a.Fori(1, B) as b:
                layer1(b, False)
            for i in range(4):
                ffn_up(B - 1, i)

        @block.tensor
        def _(pe):
            def mm(o, l, rh, k, n):
                return pe.matmul(o, l, rh, start=(k == 0), stop=(k == n - 1))

            def proj(b, i):
                FA.free(pe, b, i)
                ps = FA.ps(i)
                if i > 0:
                    for j in range(2):
                        hh = 2 * i - 2 + j
                        for t in range(D2):
                            ins = mm(ps[:, j, :], wq0[:, t, hh * P:(hh + 1) * P], xT[:, t, :], t, D2)
                else:
                    for t in range(D2):
                        mm(ps[:, 0, :], wk0[:, t, :], xT[:, t, :], t, D2)
                    for m in range(T2):
                        for t in range(D2):
                            ins = mm(ps[:, 1, m * P:(m + 1) * P], xT[:, t, m * P:(m + 1) * P], wv0[:, t, :], t, D2)
                FA.fill(ins, i)

            def turn(W, b, i, src):
                W.free(pe, b, i)
                for t in range(T2):
                    for d in range(D2):
                        ins = pe.transpose(W.ps(i)[:, d, t * P:(t + 1) * P], src[:, t, d * P:(d + 1) * P], ident[:])
                W.fill(ins, i)

            def lin(W, b, i, lT, rh, n=D):
                W.free(pe, b, i)
                for t in range(T2):
                    for d in range(D2):
                        ins = mm(W.ps(i)[:, t, 0:n], lT[:, d, t * P:(t + 1) * P], rh[:, d, :], d, D2)
                W.fill(ins, i)

            def linT(W, b, i, w, xt):
                W.free(pe, b, i)
                for o in range(D2):
                    for d in range(D2):
                        ins = mm(W.ps(i)[:, o, :], w[:, d, o * P:(o + 1) * P], xt[:, d, :], d, D2)
                W.fill(ins, i)

            def turn_probs(src, k, u, ringed):
                if ringed:
                    pe.wait_ge(turned_sb, u - 1)
                for t in range(T2):
                    for m in range(T2):
                        ins = pe.transpose(pt_ps[k % 2][:, m, t * P:(t + 1) * P], src[:, t, m * P:(m + 1) * P], ident[:])
                ins.then_inc(turned, 1)

            def heads(W, b, u_of, q, ke, ko, v, oi, between):
                for i in range(HM + 3):
                    if i < HM:
                        if i >= 2:
                            pe.wait_ge(expd if W is WA else smax, u_of(i) - 1)
                        j, p0 = i // 8, 32 * ((i % 8) // 2)
                        kk = (ke, ko)[i % 2]
                        for t in range(T2):
                            ins = mm(sc_ps[i % 2][:, t, :], q[p0:p0 + 32, j, t * P:(t + 1) * P], kk[p0:p0 + 32, j, :], 0, 1)
                        ins.then_inc(scores, 1)
                    if 2 <= i < HM + 2:
                        k = i - 2
                        pe.wait_ge(expd, u_of(k) + 1)
                        turn_probs(probs[k % 3], k, u_of(k), k >= 2)
                    if i >= 3:
                        k = i - 3
                        pe.wait_ge(turned_sb, u_of(k) + 1)
                        if k == 0:
                            W.free(pe, b, oi)
                        for t in range(T2):
                            for m in range(T2):
                                ins = mm(W.ps(oi)[:, t, k * HD:(k + 1) * HD], probsT[k % 2][:, m, t * P:(t + 1) * P],
                                         v[:, m, k * HD:(k + 1) * HD], m, T2)
                        if k < HM - 1:
                            ins.then_inc(pv, 1)
                        else:
                            W.fill(ins, oi)
                    between(i)

            pe.wait_ge(consts, 12)
            pe.wait_ge(w0_in, 16 * 3)
            pe.wait_ge(xT_in, 16)
            for i in range(5):
                proj(0, i)
            pe.wait_ge(wA_in, 16 * 7)

            def layer0(b, last):
                def u(k):
                    return U_A * b + k
                FA.out(pe, b, 0)
                for i in range(H0 + 3):
                    if i < H0:
                        if i % 2 == 0:
                            FA.out(pe, b, 1 + i // 2)
                        if i >= 2:
                            pe.wait_ge(expd, u(i) - 1)
                        for t in range(T2):
                            ins = mm(sc_ps[i % 2][:, t, :], QT[:, i, t * P:(t + 1) * P], KT[:], 0, 1)
                        ins.then_inc(scores, 1)
                    if 2 <= i < H0 + 2:
                        k = i - 2
                        pe.wait_ge(normed, H0 * b + k + 1)
                        turn_probs(probs[k % 3], k, u(k), k >= 2)
                    if i >= 3:
                        k = i - 3
                        pe.wait_ge(turned_sb, u(k) + 1)
                        WA.free(pe, b, k)
                        for m in range(T2):
                            ins = mm(WA.ps(k)[:, 0, :], V[:, m, :], probsT[k % 2][:, m, :], m, T2)
                        WA.fill(ins, k)
                pe.wait_ge(cT_in, 16 * (b + 1))
                lin(WA, b, CTXW, cT, wx)
                WA.out(pe, b, H0 - 2)
                WA.out(pe, b, H0 - 1)
                for t in range(T2):
                    for k in range(H0):
                        ins = mm(WA.ps(ATTN0)[:, t, :], OT[:, k, t * P:(t + 1) * P], wo0[:, k, :], k, H0)
                WA.fill(ins, ATTN0)
                if not last:
                    pe.wait_ge(xT_in, 16 * (b + 2))
                    proj(b + 1, 0)
                    proj(b + 1, 1)
                pe.wait_ge(x1_ok, b + 1)
                turn(WA, b, X1T, x1)
                WA.out(pe, b, X1T)
                for t in range(T2):
                    for d in range(D2):
                        ins = mm(sc_ps[0][:, t, :], tT[:, d, t * P:(t + 1) * P], cT[:, d, :], d, D2)
                ins.then_inc(scores, 1)
                if not last:
                    proj(b + 1, 2)
                    proj(b + 1, 3)
                pe.wait_ge(expd, u(H0) + 1)
                turn_probs(probs[2], 0, 0, False)
                pe.wait_ge(turned_sb, u(H0) + 1)
                lin(WA, b, XATT, probsT[0], cW)
                if not last:
                    proj(b + 1, 4)
                pe.wait_ge(n1_ok, b + 1)
                turn(WA, b, N1T, r)
                WA.out(pe, b, N1T)
                linT(WA, b, QM, wqm, nT)
                linT(WA, b, KM, wkm, nT)
                lin(WA, b, VM, nT, wvm)
                WA.out(pe, b, QM)
                WA.out(pe, b, KM)
                WA.out(pe, b, VM)
                heads(WA, b, lambda k: U_A * b + (H0 + 1 + k), QTm, KTe, KTo, Vm, OM, lambda i: None)
                WA.out(pe, b, OM)
                turn(WA, b, OMT, On)
                WA.out(pe, b, OMT)
                lin(WA, b, PROJ, tT, wom)
                pe.wait_ge(n2_ok, b + 1)
                turn(WA, b, N2T, n2)
                WA.out(pe, b, N2T)
                lin(WA, b, LOGIT, nT, wg, E)
                pe.wait_ge(cnt_ok, b + 1)
                WA.free(pe, b, RANK)
                rk = WA.ps(RANK)[:, 0, :]
                mm(rk[:, 0:E], upper[:], cnt[:, 0, :], 0, 1)
                mm(rk[:, E:2 * E], upper[:], cnt[:, 1, :], 0, 2)
                mm(rk[:, E:2 * E], ones[:], cnt[:, 0, :], 1, 2)
                mm(rk[:, 2 * E:3 * E], ones[:], cnt[:, 0, :], 0, 2)
                WA.fill(mm(rk[:, 2 * E:3 * E], ones[:], cnt[:, 1, :], 1, 2), RANK)

            layer0(0, False)
            with pe.Fori(1, B - 1) as b:
                layer0(b, False)
            layer0(B - 1, True)

            def slot_x(t, p):
                pe.wait_ge(xg_in[p], 16 * (t + 1))
                for d in range(D2):
                    ins = pe.transpose(bank[p][:, 0, d * P:(d + 1) * P], xg[p][:, d * P:(d + 1) * P], ident[:])
                ins.then_inc(b_x, 1)

            def slot_up(s, p, first):
                e = pe.value_load(slot_e[0:1, bass.ds(s, 1)], min_val=0, max_val=E - 1)
                pe.wait_ge(b_xs, s + 1)
                if not first:
                    pe.wait_ge(b_hid, s - 1)
                for w, o in ((w1, 2), (w3, 3)):
                    for d in range(D2):
                        ins = mm(bank[o + 2 * p][:].rearrange("p a b -> p (a b)"), xgT[p][:, d, :],
                                 w[:, bass.ds(e, 1), d, :].rearrange("p e n -> p (e n)"), d, D2)
                ins.then_inc(b_h, 1)
                return e

            def slot_t(s, p, first):
                pe.wait_ge(b_hid, s + 1)
                if not first:
                    pe.wait_ge(b_ts, s)
                for f in range(FT0):
                    ins = pe.transpose(bank[6][:].rearrange("p a b -> p (a b)")[:, f * P:(f + 1) * P],
                                       hid[p][:, f * P:(f + 1) * P], ident[:])
                ins.then_inc(b_t, 1)

            def slot_down(s, p, first):
                e = pe.value_load(slot_e[0:1, bass.ds(s, 1)], min_val=0, max_val=E - 1)
                pe.wait_ge(b_ts, s + 1)
                if not first:
                    pe.wait_ge(b_ys, s)
                for f in range(FT0):
                    ins = mm(bank[7][:, 0, :], hidT[p][:, f, :], w2[:, bass.ds(e, 1), f, :].rearrange("p e n -> p (e n)"),
                             f, FT0)
                ins.then_inc(b_y, 1)

            pe.wait_ge(plan, 14)
            pe.wait_ge(wM_in, 48 * B)
            slot_x(0, 0)
            slot_up(0, 0, True)
            slot_x(0, 1)
            slot_t(0, 0, True)
            slot_up(1, 1, True)
            slot_down(0, 0, True)
            with pe.Fori(1, SLOTS // 2) as t:
                slot_x(t, 0)
                slot_t(2 * t - 1, 1, False)
                slot_up(2 * t, 0, False)
                slot_down(2 * t - 1, 1, False)
                slot_x(t, 1)
                slot_t(2 * t, 0, False)
                slot_up(2 * t + 1, 1, False)
                slot_down(2 * t, 0, False)
            slot_t(SLOTS - 1, 1, False)
            slot_down(SLOTS - 1, 1, False)

            def ffn_up(b, i):
                FC.free(pe, b, i)
                for j in range(2):
                    f = 2 * i + j
                    for d in range(D2):
                        ins = mm(FC.ps(i)[:, j, :], W1s[:, d, f * P:(f + 1) * P], x5T[:, d, :], d, D2)
                FC.fill(ins, i)

            def ffn_down(b):
                FC.out(pe, b, 2)
                FC.out(pe, b, 3)
                for t in range(T2):
                    for f in range(FT1):
                        ins = mm(FC.ps(4)[:, t, :], hF[:, f, t * P:(t + 1) * P], W2s[:, f, :], f, FT1)
                FC.fill(ins, 4)

            def layer1(b, first):
                pe.wait_ge(cT_in, 16 * B + 16 * (b + 1))
                linT(WC, b, K1, wk1, cT)
                lin(WC, b, V1, cT, wv1)
                pe.wait_ge(x3_ok, b + 1)
                turn(WC, b, X3T, x3)
                pe.wait_ge(scan_ok, b + 1)
                lin(WC, b, SSM, yT, wout)
                pe.wait_ge(x4_ok, b + 1)
                turn(WC, b, X4T, x4)
                WC.out(pe, b, X4T)
                linT(WC, b, Q1, wq1, x4T)
                WC.out(pe, b, K1)
                WC.out(pe, b, V1)
                WC.out(pe, b, Q1)

                def between(i):
                    if first:
                        return
                    if i in (3, 5, 7, 9):
                        if i == 3:
                            pe.wait_ge(ex_in, 64 * b)
                        ffn_up(b - 1, (i - 3) // 2)
                    if i == 12:
                        ffn_down(b - 1)
                heads(WC, b, lambda k: U_C * b + (U0 + k), qF, kFe, kFo, vF, O1, between)
                WC.out(pe, b, O1)
                turn(WC, b, O1T, On)
                WC.out(pe, b, O1T)
                lin(WC, b, PROJ1, x3T, wo1)
                pe.wait_ge(x5_ok, b + 1)
                turn(WC, b, X5T, x5)
                WC.out(pe, b, X5T)
                WC.free(pe, b, ROUTE)
                for d in range(D2):
                    ins = mm(WC.ps(ROUTE)[0:1, 0, 0:E], msum[:, d:d + 1], wr[:, d, :], d, D2)
                WC.fill(ins, ROUTE)

            pe.wait_ge(wC_in, 16 * 7)
            layer1(0, True)
            with pe.Fori(1, B) as b:
                layer1(b, False)
            pe.wait_ge(ex_in, 64 * B)
            for i in range(4):
                ffn_up(B - 1, i)
            ffn_down(B - 1)

        @block.vector
        def _(v):
            v.wait_ge(consts, 12)
            idv = ident[:].rearrange("p (g two n) -> p g two n", two=2, n=HD)
            v.tensor_reduce(even[:], idv[:, :, 0, :], AX.XY, ALU.add).then_inc(consts, 1)
            v.tensor_reduce(odd[:], idv[:, :, 1, :], AX.XY, ALU.add).then_inc(consts, 1)
            v.wait_ge(consts, 14)
            v.wait_ge(const_in, 16 * 11)
            v.tensor_scalar(bke[:], bk1[:], even[:, 0:1], None, ALU.mult)
            v.tensor_scalar(bko[:], bk1[:], odd[:, 0:1], None, ALU.mult).then_inc(consts, 1)

            def finish_norm(n, k, src, dst, done, mean=True):
                v.wait_ge(n.root, k + 1)
                for t in range(T2):
                    if mean:
                        ins = v.tensor_scalar(dst[:, t, :], src[:, t, :], n.mv[:, t, 0:1], n.rstd[:, t:t + 1],
                                              ALU.subtract, ALU.mult)
                    else:
                        ins = v.tensor_scalar(dst[:, t, :], src[:, t, :], n.rstd[:, t:t + 1], None, ALU.mult)
                ins.then_inc(done, 1)

            def stats(n, k, ks, src):
                for t in range(T2):
                    ins = v.bn_stats(n.st[:, t, :], src[:, t, :])
                ins.then_inc(n.stats, 1)
                v.wait_ge(n.stats, k + 1)
                apart(v)
                for t in range(T2):
                    ins = v.bn_aggr(n.mv[:, t, :], n.st[:, t, :])
                ins.then_inc(n.mean, 1)
                v.wait_ge(n.mean, ks + 1)
                v.tensor_scalar(n.ve[:], n.mv[:, :, 1], EPS, None, ALU.add).then_inc(n.var, 1)

            def squares(n, k, src, junk):
                for t in range(T2):
                    ins = v.tensor_tensor_reduce(junk[:, t, :], src[:, t, :], src[:, t, :], 1.0, 0.0, ALU.mult, ALU.add,
                                                 n.st[:, t, 0:1])
                ins.then_inc(n.stats, 1)
                v.wait_ge(n.stats, k + 1)
                v.tensor_scalar(n.ve[:], n.st[:, :, 0], 1.0 / D, EPS, ALU.mult, ALU.add).then_inc(n.var, 1)

            def max_of(u, k):
                v.wait_ge(scores, u + 1)
                v.tensor_reduce(nmax[:, k % 4, :], sc_ps[k % 2][:], AX.X, ALU.max, negate=True).then_inc(smax, 1)

            def masked_max(u, k, mask, scale, src, dst):
                v.wait_ge(scores, u + 1)
                apart(v)
                for t in range(T2):
                    ins = v.tensor_tensor_reduce(dst[:, t, :], src[:, t, :], mask(t), -scale, BIG, ALU.add, ALU.min,
                                                 nmax[:, k % 4, t:t + 1])
                ins.then_inc(smax, 1)

            def copy_turned(u, k, used=None):
                v.wait_ge(turned, u + 1)
                if used:
                    used()
                v.tensor_copy(probsT[k % 2][:], pt_ps[k % 2][:]).then_inc(turned_sb, 1)

            def head_out(W, b, oi, n):
                v.reciprocal(rrm[:], rsm[:]).then_inc(inv_m, 1)
                v.wait_ge(inv_m, n + 1)
                W.full(v, b, oi)
                for t in range(T2):
                    ins = v.tensor_tensor(On[:, t, :].rearrange("p (h n) -> p h n", n=HD),
                                          W.ps(oi)[:, t, :].rearrange("p (h n) -> p h n", n=HD),
                                          rrm[:, t, :].unsqueeze(2).broadcast_to([P, HM, HD]), ALU.mult)
                W.copy(ins, oi)

            RT = 8

            def layer0(b):
                def u(k):
                    return U_A * b + k
                for i in range(H0 + 2):
                    if i < H0:
                        max_of(u(i), i)
                    if 1 <= i <= H0:
                        k = i - 1
                        v.wait_ge(expd, u(k) + 1)
                        v.reciprocal(rr0[:, k % 3, :], rs0[:, k % 3, :]).then_inc(sums_inv, 1)
                        v.wait_ge(sums_inv, (H0 + 1) * b + k + 1)
                        for t in range(T2):
                            ins = v.tensor_scalar(probs[k % 3][:, t, :], probs[k % 3][:, t, :],
                                                  rr0[:, k % 3, t:t + 1], None, ALU.mult)
                        ins.then_inc(normed, 1)
                    if i >= 2:
                        k = i - 2
                        copy_turned(u(k), k, (lambda: WA.full(v, b, k - 2)) if k >= 2 else None)
                v.wait_ge(x_in, 16 * (b + 1))
                WA.full(v, b, ATTN0)
                ins = v.tensor_tensor(r[:], WA.ps(ATTN0)[:], x[:], ALU.add)
                WA.copy(ins, ATTN0)
                WA.out(v, b, ATTN0)
                stats(nA, 4 * b, 2 * b, r)
                finish_norm(nA, 4 * b, r, x1, x1_ok)
                v.wait_ge(mask_ok, b + 1)
                masked_max(u(H0), 0, lambda t: mask0[:, t, :], 1.0 / SQ0, sc_ps[0], probs[2])
                copy_turned(u(H0), 0)
                v.wait_ge(expd, u(H0) + 1)
                v.reciprocal(rr0[:, 0, :], rs0[:, 0, :]).then_inc(sums_inv, 1)
                v.wait_ge(sums_inv, (H0 + 1) * b + H0 + 1)
                v.wait_ge(xb_ok, b + 1)
                WA.full(v, b, XATT)
                for t in range(T2):
                    ins = v.scalar_tensor_tensor(r[:, t, :], WA.ps(XATT)[:, t, :], rr0[:, 0, t:t + 1], xb[:, t, :],
                                                 ALU.mult, ALU.add)
                WA.copy(ins, XATT)
                WA.out(v, b, XATT)
                stats(nA, 4 * b + 1, 2 * b + 1, r)
                finish_norm(nA, 4 * b + 1, r, x2, x2_ok)
                v.wait_ge(x2_ok, b + 1)
                squares(nA, 4 * b + 2, x2, r)
                finish_norm(nA, 4 * b + 2, x2, r, n1_ok, mean=False)
                WA.full(v, b, VM)
                WA.copy(v.tensor_copy(Vm[:], WA.ps(VM)[:]), VM)
                for i in range(HM + 2):
                    if i < HM:
                        max_of(u(H0 + 1 + i), i)
                    if i >= 2:
                        k = i - 2
                        copy_turned(u(H0 + 1 + k), k, (lambda: v.wait_ge(pv, (HM - 1) * b + (k - 1))) if k >= 2 else None)
                v.wait_ge(expd, u(U_A))
                head_out(WA, b, OM, b)
                WA.full(v, b, PROJ)
                ins = v.tensor_tensor(h[:], WA.ps(PROJ)[:], x2[:], ALU.add)
                WA.copy(ins, PROJ)
                WA.out(v, b, PROJ)
                need(v, scattered, 64 * b)
                squares(nA, 4 * b + 3, h, n2)
                v.wait_ge(nA.root, 4 * b + 4)
                for t in range(T2):
                    ins = v.scalar_tensor_tensor(n2[:, t, :], h[:, t, :], nA.rstd[:, t:t + 1], ln2w[:], ALU.mult, ALU.mult)
                ins.then_inc(n2_ok, 1)
                WA.full(v, b, LOGIT)
                WA.copy(v.tensor_copy(lg[:], WA.ps(LOGIT)[:, :, 0:E]), LOGIT)
                WA.out(v, b, LOGIT)
                apart(v)
                for t in range(T2):
                    ins = v.max(mx[:, t, :], lg[:, t, :])
                ins.then_inc(rt, 1)
                v.wait_ge(rt, RT * b + 1)
                apart(v)
                for t in range(T2):
                    ins = v.max_index(mi[:, t, :], mx[:, t, :], lg[:, t, :])
                ins.then_inc(rt, 1)
                v.tensor_tensor(dl[:], mx[:, :, 1], mx[:, :, 0], ALU.subtract).then_inc(dl_ok, 1)
                v.wait_ge(rt, RT * b + 2)
                v.tensor_copy(mf[:], mi[:, :, 0:2]).then_inc(rt, 1)
                v.wait_ge(rt, RT * b + 3)
                for t in range(T2):
                    for k in range(2):
                        ins = v.tensor_scalar(sel[:, t, k, :], ei[:], mf[:, t, k:k + 1], None, ALU.is_equal)
                ins.then_inc(rt, 1)
                v.wait_ge(rt, RT * b + 4)
                v.tensor_tensor(cnt[:], sel[:, :, 0, :], sel[:, :, 1, :], ALU.add).then_inc(cnt_ok, 1)
                v.tensor_copy(sel_all[:, bass.ds(b, 1), :].rearrange("p b n -> p (b n)"),
                              sel[:].rearrange("p t k e -> p (t k e)"))
                v.wait_ge(el_ok, b + 1)
                v.tensor_scalar(e1[:], el[:], 1.0, None, ALU.add).then_inc(rt, 1)
                v.wait_ge(rt, RT * b + 5)
                v.reciprocal(pk[:, :, 0], e1[:]).then_inc(rt, 1)
                v.wait_ge(rt, RT * b + 6)
                v.tensor_tensor(pk[:, :, 1], pk[:, :, 0], el[:], ALU.mult).then_inc(rt, 1)
                WA.full(v, b, RANK)
                v.tensor_tensor(rank[:], WA.ps(RANK)[:, 0, 0:2 * E].rearrange("p (t e) -> p t e", t=2),
                                run[:].unsqueeze(1).broadcast_to([P, T2, E]), ALU.add).then_inc(route_pos, 1)
                v.wait_ge(route_pos, 3 * b + 1)
                WA.copy(v.tensor_tensor(run[:], WA.ps(RANK)[:, 0, 2 * E:3 * E], run[:], ALU.add), RANK)
                WA.out(v, b, RANK)
                v.wait_ge(rt, RT * b + 7)
                v.tensor_copy(pk_all[:, bass.ds(b, 1), :].rearrange("p b n -> p (b n)"), pk[:].rearrange("p t k -> p (t k)"))
                v.tensor_copy(rank_all[:, bass.ds(b, 1), :].rearrange("p b n -> p (b n)"), rank[:].rearrange("p t e -> p (t e)"))
                v.tensor_tensor(rowat[:], rank[:], ebase[:].unsqueeze(1).broadcast_to([P, T2, E]), ALU.add).then_inc(rt, 1)
                v.wait_ge(rt, RT * b + 8)
                for k in range(2):
                    ins = v.tensor_tensor(rowsel[:, :, k, :], sel[:, :, k, :], rowat[:], ALU.mult)
                ins.then_inc(route_pos, 1)
                v.wait_ge(route_pos, 3 * b + 2)
                v.tensor_reduce(posf[:], rowsel[:].rearrange("p t k e -> p (t k) e"), AX.X, ALU.add).then_inc(route_pos, 1)
                v.wait_ge(route_pos, 3 * b + 3)
                v.tensor_copy(posu[:], posf[:]).then_inc(pos_ok, 1)

            layer0(0)
            with v.Fori(1, B) as b:
                layer0(b)

            step = [0]

            def link(ins):
                step[0] += 1
                ins.then_inc(plan, 1)
                v.wait_ge(plan, step[0])

            link(v.tensor_tensor(tcmp[:], run[:].unsqueeze(2).broadcast_to([P, E, TOK // P]),
                                 thr[:].unsqueeze(1).broadcast_to([P, E, TOK // P]), ALU.is_gt))
            link(v.tensor_reduce(tiles[:], tcmp[:], AX.X, ALU.add))
            link(v.tensor_tensor_scan(tend[:], ones[:, 0:E], tiles[:], 0.0, ALU.mult, ALU.add))
            link(v.tensor_tensor(tbeg[:], tend[:], tiles[:], ALU.subtract))
            link(v.tensor_tensor(padf[:], run[:], ebase[:], ALU.add))
            link(v.tensor_scalar(padf[:], padf[:], pidx[:, 0:1], None, ALU.add))
            link(v.tensor_copy(padu[:], padf[:]))
            sl = si[:].unsqueeze(2).broadcast_to([P, SLOTS, E])
            v.tensor_tensor(inA[:], tbeg[:].unsqueeze(1).broadcast_to([P, SLOTS, E]), sl, ALU.is_le)
            link(v.tensor_tensor(inB[:], tend[:].unsqueeze(1).broadcast_to([P, SLOTS, E]), sl, ALU.is_gt))
            link(v.tensor_tensor(inA[:], inA[:], inB[:], ALU.mult))
            v.scalar_tensor_tensor(rbase[:], tbeg[:], -float(P), ebase[:], ALU.mult, ALU.add)
            link(v.tensor_tensor(inB[:], inA[:], ei[:].unsqueeze(1).broadcast_to([P, SLOTS, E]), ALU.mult))
            link(v.tensor_reduce(slf[:, 0, :], inB[:], AX.X, ALU.add))
            link(v.scalar_tensor_tensor(inB[:], sl, float(P), rbase[:].unsqueeze(1).broadcast_to([P, SLOTS, E]), ALU.mult, ALU.add))
            link(v.tensor_tensor(inB[:], inB[:], inA[:], ALU.mult))
            v.tensor_copy(slot_e[:], slf[:, 0, :])
            v.tensor_reduce(slf[:, 1, :], inB[:], AX.X, ALU.add).then_inc(route_pos, 1)
            v.wait_ge(route_pos, 3 * B + 1)
            link(v.tensor_copy(slot_r[:], slf[:, 1, :]))
            assert step[0] == 14
            v.tensor_scalar(ybase[:], tbeg[:], float(P), None, ALU.mult).then_inc(route_pos, 1)
            v.wait_ge(route_pos, 3 * B + 2)
            ra = rank_all[:].rearrange("p b (t e) -> p (b t) e", e=E)
            link(v.tensor_tensor(ra, ra, ybase[:].unsqueeze(1).broadcast_to([P, B * T2, E]), ALU.add))
            sa = sel_all[:].rearrange("p b (t k e) -> p (b t) k e", k=2, e=E)
            for k in range(2):
                ins = v.tensor_tensor(ymul[:, :, k, :], sa[:, :, k, :], ra, ALU.mult)
            link(ins)
            v.tensor_reduce(yf[:], ymul[:].rearrange("p t k e -> p (t k) e"), AX.X, ALU.add).then_inc(route_pos, 1)
            v.wait_ge(route_pos, 3 * B + 3)
            link(v.tensor_copy(yu_all[:].rearrange("p b n -> p (b n)"), yf[:]))

            def slot(s, p, first):
                v.wait_ge(b_gate, s + 1)
                if not first:
                    v.wait_ge(b_t, s - 1)
                v.tensor_tensor(hid[p], bank[3 + 2 * p][:].rearrange("p a b -> p (a b)"), gate[p], ALU.mult).then_inc(b_hid, 1)

            def slot_y(t, p, first):
                s = 2 * t + p
                v.wait_ge(b_y, s + 1)
                if not first:
                    need(v, y_out[p], 16 * t)
                v.tensor_copy(yo[p], bank[7][:, 0, :]).then_inc(b_ys, 1)

            slot(0, 0, True)
            slot(1, 1, True)
            slot_y(0, 0, True)

            def slots(t):
                slot(2 * t, 0, False)
                slot_y(t - 1, 1, False)
                slot(2 * t + 1, 1, False)
                slot_y(t, 0, False)

            slots(1)
            with v.Fori(2, SLOTS // 2) as t:
                slots(t)
            slot_y(SLOTS // 2 - 1, 1, False)

            def ffn_end(b):
                FC.full(v, b, 4)
                v.wait_ge(f_r, b + 1)
                FC.copy(v.tensor_tensor(rF[:], FC.ps(4)[:], rF[:], ALU.add), 4)
                FC.out(v, b, 4)
                stats(nF, b, b, rF)
                need(v, out_done, 16 * b)
                finish_norm(nF, b, rF, xF, f_out)

            def layer1(b, first):
                v.wait_ge(mi_in, 16 * (b + 1))
                v.tensor_scalar(mask1[:], mask_i[:], 0.0, NEG1, ALU.is_equal, ALU.mult).then_inc(mask1_ok, 1)
                WC.full(v, b, V1)
                WC.copy(v.tensor_tensor(vF[:], WC.ps(V1)[:], bv1[:].unsqueeze(1).broadcast_to([P, 2, D]), ALU.add), V1)
                v.wait_ge(yk_in, 64 * (b + 1))
                v.wait_ge(hx_in, 16 * (b + 1))
                v.tensor_copy(pk[:].rearrange("p t k -> p (t k)"), pk_all[:, bass.ds(b, 1), :].rearrange("p b n -> p (b n)")).then_inc(comb1, 1)
                v.wait_ge(comb1, 2 * b + 1)
                for t in range(T2):
                    ins = v.scalar_tensor_tensor(r[:, t, :], yk[0][:, t, :], pk[:, t, 0:1], x[:, t, :], ALU.mult, ALU.add)
                ins.then_inc(comb1, 1)
                v.wait_ge(comb1, 2 * b + 2)
                for t in range(T2):
                    ins = v.scalar_tensor_tensor(r[:, t, :], yk[1][:, t, :], pk[:, t, 1:2], r[:, t, :], ALU.mult, ALU.add)
                ins.then_inc(comb, 1)
                v.wait_ge(comb, b + 1)
                stats(nC, 3 * b, 3 * b, r)
                finish_norm(nC, 3 * b, r, x3, x3_ok)
                v.wait_ge(consts, 16)
                WC.out(v, b, X3T)
                for t in range(D2):
                    ins = v.tensor_tensor_scan(yT[:, t, :], ah[:, t:t + 1].broadcast_to([P, S]), x3T[:, t, :], 0.0,
                                               ALU.mult, ALU.add)
                ins.then_inc(scan_ok, 1)
                WC.full(v, b, SSM)
                v.wait_ge(cb, 2 * b + 1)
                WC.copy(v.tensor_tensor(r[:], WC.ps(SSM)[:], xb[:], ALU.add), SSM)
                WC.out(v, b, SSM)
                stats(nC, 3 * b + 1, 3 * b + 1, r)
                finish_norm(nC, 3 * b + 1, r, x4, x4_ok)
                for i in range(HM + 2):
                    if i < HM:
                        uu = U_C * b + (U0 + i)
                        if i >= 3:
                            v.wait_ge(turned, uu - 2)
                        masked_max(uu, i, lambda t: mask1[:], 1.0 / SQM, sc_ps[i % 2], probs[i % 3])
                    if i >= 2:
                        k = i - 2
                        copy_turned(U_C * b + (U0 + k), k,
                                    (lambda: v.wait_ge(pv, (HM - 1) * b + ((HM - 1) * B + k - 1))) if k >= 2 else None)
                    if i == HM - 1 and not first:
                        ffn_end(b - 1)
                v.wait_ge(expd, U_C * b + (U0 + HM))
                head_out(WC, b, O1, b + B)
                v.wait_ge(cb, 2 * b + 2)
                WC.full(v, b, PROJ1)
                WC.copy(v.tensor_tensor(r[:], WC.ps(PROJ1)[:], xb[:], ALU.add), PROJ1)
                WC.out(v, b, PROJ1)
                stats(nC, 3 * b + 2, 3 * b + 2, r)
                finish_norm(nC, 3 * b + 2, r, x5, x5_ok)
                WC.full(v, b, ROUTE)
                WC.copy(v.scalar_tensor_tensor(lr[:], WC.ps(ROUTE)[0:1, 0, 0:E], 1.0 / S, br1[:], ALU.mult, ALU.add), ROUTE)
                WC.out(v, b, ROUTE)
                apart(v)
                v.max(lmx[:], lr[:]).then_inc(rt1, 1)
                v.wait_ge(rt1, b + 1)
                apart(v)
                v.max_index(lmi[:], lmx[:], lr[:]).then_inc(pick_ok, 1)

            layer1(0, True)
            with v.Fori(1, B) as b:
                layer1(b, False)
            ffn_end(B - 1)


def lay(inputs):
    import numpy as np

    def tiled(w):
        return np.asarray(w).reshape(2, P, -1).transpose(1, 0, 2)

    def a(name):
        return np.asarray(inputs[name])

    def turned(x):
        return x.reshape(B, S, 2, P).transpose(0, 3, 2, 1)

    x, c = a("x"), a("ctx_1024")
    d = {
        "x": x.reshape(B, 2, P, D).transpose(0, 2, 1, 3),
        "xT": turned(x),
        "cT": turned(c),
        "lens": a("_lenS2"),
        "mask": a("mask_Bx1x1xS2_if1").reshape(B, S),
        "wq0": tiled(a("L0_attn_proj_q").transpose(1, 0, 2).reshape(D, H0 * P)),
        "wk0": tiled(a("L0_attn_proj_k")),
        "wv0": tiled(a("L0_attn_proj_v")),
        "wo0": a("L0_attn_proj_o").transpose(2, 0, 1),
        "wx": tiled(a("L0_xattn_W")),
        "bx": a("L0_xattn_b"),
        "ln1w": a("L0_ffn_ln1_w").reshape(2, P).T,
        "ln2w": a("L0_ffn_ln2_w"),
        "wqm": tiled(a("L0_ffn_wq").T),
        "wkm": tiled(a("L0_ffn_wk").T),
        "wvm": tiled(a("L0_ffn_wv").T),
        "wom": tiled(a("L0_ffn_wo").T),
        "wg": tiled(a("L0_ffn_gate_w").T),
        "w1": a("L0_ffn_w1").transpose(0, 2, 1).reshape(E, 2, P, F0).transpose(0, 2, 1, 3).reshape(E, P, 1, 2 * F0),
        "w3": a("L0_ffn_w3").transpose(0, 2, 1).reshape(E, 2, P, F0).transpose(0, 2, 1, 3).reshape(E, P, 1, 2 * F0),
        "w2": a("L0_ffn_w2").transpose(0, 2, 1).reshape(E, FT0, P, D).transpose(0, 2, 1, 3).reshape(E, P, 1, FT0 * D),
        "a": a("L1_attn_a").reshape(2, P).T,
        "b": a("L1_attn_b").reshape(2, P).T,
        "wout": tiled(a("L1_attn_w_out").T),
        "bout": a("L1_attn_b_out"),
        "wv1": tiled(a("L1_xattn_Wv")),
        "wk1": tiled(a("L1_xattn_Wk")),
        "wq1": tiled(a("L1_xattn_Wq")),
        "wo1": tiled(a("L1_xattn_Wo")),
        "bv1": a("L1_xattn_bv"),
        "bk1": a("L1_xattn_bk").reshape(2, P).T,
        "bq1": a("L1_xattn_bq").reshape(2, P).T,
        "bo1": a("L1_xattn_bo"),
        "wr": tiled(a("L1_ffn_Wr")),
        "br1": a("L1_ffn_br").reshape(1, E),
        "W1": a("L1_ffn_W1").reshape(E, 2, P, F1).transpose(0, 2, 1, 3),
        "b1": a("L1_ffn_b1").reshape(E, FT1, P).transpose(0, 2, 1),
        "W2": a("L1_ffn_W2").reshape(E, FT1, P, D).transpose(0, 2, 1, 3),
        "b2": a("L1_ffn_b2"),
    }
    return {k: np.ascontiguousarray(v) for k, v in d.items()}


def kernel(**inputs):
    import concourse.bacc as _bacc
    from concourse.bass_utils import run_bass_kernel_spmd as _run

    nc = _bacc.Bacc("TRN2", target_bir_lowering=False, num_devices=1)
    arrays, A = {}, {}
    for name, v in lay(inputs).items():
        arrays[f"in_{name}"] = v
        A[name] = nc.dram_tensor(f"in_{name}", v.shape, mybir.dt.from_np(v.dtype), kind="ExternalInput").ap()
    out = nc.dram_tensor("out_0", [B, S, D], F32, kind="ExternalOutput").ap()
    build(nc, A, out)
    r = _run(nc, [arrays], core_ids=[0])
    return r.results[0]["out_0"]
```

```python
from contextlib import ExitStack

import concourse.bass as bass
from concourse import mybir

F32 = mybir.dt.float32
I32 = mybir.dt.int32
U32 = mybir.dt.uint32
ALU = mybir.AluOpType
ACT = mybir.ActivationFunctionType
AX = mybir.AxisListType

P = 128
B = 8
S = 256
D = 256
T2 = S // P
D2 = D // P
H0 = 8
HM = 16
HD = D // HM
E = 8
F0 = 512
FT0 = F0 // P
F1 = 1024
FT1 = F1 // P
TOK = B * S
REG = TOK + P
SLOTS = 2 * TOK // P + E
EPS = 1e-5
NEG0 = -1e13
NEG1 = -1e20
U_A = H0 + 1 + HM
U_C = HM
SQ0 = float(D) ** 0.5
SQM = float(HD) ** 0.5
BIG = 3e38


def build(nc, A, out):
    with ExitStack() as ctx:
        def sb(name, shape, dt=F32):
            return ctx.enter_context(nc.sbuf_tensor("s_" + name, shape, dt))

        def sem(name):
            return ctx.enter_context(nc.semaphore(name))

        rows_d = nc.dram_tensor("rows_by_expert", [E * REG, D], F32, kind="Internal").ap()
        y_d = nc.dram_tensor("expert_out", [SLOTS * P, D], F32, kind="Internal").ap()
        hx_d = nc.dram_tensor("residual", [B, P, T2 * D], F32, kind="Internal").ap()

        bank = [ctx.enter_context(nc.psum_tensor(f"bank{i}", [P, 2, 256], F32)) for i in range(8)]
        sc_ps = bank[0:2]
        pt_ps = bank[2:4]
        W_BANK = (bank[4], bank[7])
        F_BANK = (bank[5], bank[6])

        wq0 = sb("wq0", [P, D2, H0 * P])
        wk0 = sb("wk0", [P, D2, P])
        wv0 = sb("wv0", [P, D2, P])
        wo0 = sb("wo0", [P, H0, D])
        wx = sb("wx", [P, D2, D])
        wqm = sb("wqm", [P, D2, D])
        wkm = sb("wkm", [P, D2, D])
        wvm = sb("wvm", [P, D2, D])
        wom = sb("wom", [P, D2, D])
        wg = sb("wg", [P, D2, E])
        w1 = sb("w1", [P, E, D2, F0])
        w3 = sb("w3", [P, E, D2, F0])
        w2 = sb("w2", [P, E, FT0, D])
        cw = wq0[:].rearrange("p a (c n) -> p (a c) n", n=D)
        wv1, wk1, wq1, wo1 = (cw[:, 2 * i:2 * i + 2, :] for i in range(4))
        wout = wx
        wr = sb("wr", [P, D2, E])

        ident = sb("ident", [P, P])
        upper = sb("upper", [P, P])
        ones = sb("ones", [P, P])
        ki = sb("ki", [P, S])
        qi = sb("qi", [P, T2])
        ei = sb("ei", [P, E])
        ebase = sb("ebase", [P, E])
        thr = sb("thr", [P, TOK // P])
        si = sb("si", [P, SLOTS])
        half = sb("half", [P, T2])
        even = sb("even", [P, 1])
        odd = sb("odd", [P, 1])
        lens_i = sb("lens_i", [P, B], I32)
        lens = sb("lens", [P, B])
        ln1w = sb("ln1w", [P, D2])
        bx = sb("bx", [P, D])
        ln2w = sb("ln2w", [P, D])
        bout, bo1, bv1 = bx, ln2w, sb("bv1", [P, D])
        ah = sb("ah", [P, D2])
        av = sb("av", [P, D2])
        bvec = sb("bvec", [P, D2])
        bq1 = sb("bq1", [P, D2])
        bk1 = sb("bk1", [P, D2])
        bke = sb("bke", [P, D2])
        bko = sb("bko", [P, D2])
        br1 = sb("br1", [1, E])

        def act_tile(name):
            return sb(name, [P, 2, 256])

        x = act_tile("x")
        xT = act_tile("xT")
        cT = act_tile("cT")
        QT = sb("QT", [P, H0, S])
        OT = sb("OT", [P, H0, S])
        KT = sb("KT", [P, S])
        V = sb("V", [P, T2, P])
        probs = [act_tile(f"probs{i}") for i in range(3)]
        probsT = [act_tile(f"probsT{i}") for i in range(2)]
        cW = act_tile("cW")
        r = act_tile("r")
        x1 = act_tile("x1")
        xb = act_tile("xb")
        tT = act_tile("tT")
        mask0 = act_tile("mask0")
        x2 = act_tile("x2")
        nT = act_tile("nT")
        QTm = act_tile("QTm")
        KTe = act_tile("KTe")
        KTo = act_tile("KTo")
        VmP = sb("VmP", [P, T2, D + HD])
        Vm = VmP[:, :, 0:D]
        On = act_tile("On")
        h = act_tile("h")
        n2 = act_tile("n2")
        nmax = sb("nmax", [P, 4, T2])
        rs0 = sb("rs0", [P, 3, T2])
        rr0 = sb("rr0", [P, 3, T2])
        rsm = sb("rsm", [P, T2, HM])
        rrm = sb("rrm", [P, T2, HM])

        W1s = QT[:].rearrange("p h n -> p (h n)").rearrange("p (t f) -> p t f", t=D2)
        ring0 = [probsT[i][:] for i in range(2)] + [OT[:, 2 * i:2 * i + 2, :] for i in range(4)]
        ring1 = [w1[:, i, :, 0:S] for i in range(6)]
        OTq = r
        W2s = OT[:].rearrange("p h n -> p (h n)").rearrange("p (f d) -> p f d", d=D)
        b1s = sb("b1s", [P, FT1])
        b2s = sb("b2s", [P, D])
        hF = wo0[:].rearrange("p h n -> p (h n)").rearrange("p (f n) -> p f n", n=S)
        mask_i = sb("mask_i", [P, S], I32)
        mask1 = sb("mask1", [P, S])

        class Norm:
            def __init__(self, name):
                self.st = sb(name + "_st", [P, T2, 6])
                self.mv = sb(name + "_mv", [P, T2, 2])
                self.ve = sb(name + "_ve", [P, T2])
                self.rstd = sb(name + "_rstd", [P, T2])
                self.stats, self.mean, self.var, self.root = (
                    sem(name + s) for s in ("_stats", "_mean", "_var", "_root"))

        nA, nC, nF = Norm("na"), Norm("nc"), Norm("nf")

        lg = sb("lg", [P, T2, E])
        mx = sb("mx", [P, T2, 8])
        mi = sb("mi", [P, T2, 8], U32)
        mf = sb("mf", [P, T2, 2])
        sel = sb("sel", [P, T2, 2, E])
        cnt = sb("cnt", [P, T2, E])
        dl = sb("dl", [P, T2])
        el = sb("el", [P, T2])
        e1 = sb("e1", [P, T2])
        pk = sb("pk", [P, T2, 2])
        run = sb("run", [P, E])
        rank = sb("rank", [P, T2, E])
        rowsel = sb("rowsel", [P, T2, 2, E])
        rowat = sb("rowat", [P, T2, E])
        posf = sb("posf", [P, T2 * 2])
        posu = sb("posu", [P, T2 * 2], U32)
        sel_all = sb("sel_all", [P, B, T2 * 2 * E])
        rank_all = sb("rank_all", [P, B, T2 * E])
        pk_all = sb("pk_all", [P, B, T2 * 2])
        yu_all = sb("yu_all", [P, B, T2 * 2], U32)
        tiles = sb("tiles", [P, E])
        tcmp = sb("tcmp", [P, E, TOK // P])
        tend = sb("tend", [P, E])
        tbeg = sb("tbeg", [P, E])
        ybase = sb("ybase", [P, E])
        rbase = sb("rbase", [P, E])
        padf = sb("padf", [P, E])
        padu = sb("padu", [P, E], U32)
        pidx = sb("pidx", [P, 1])
        inA = sb("inA", [P, SLOTS, E])
        inB = sb("inB", [P, SLOTS, E])
        slf = sb("slf", [P, 3, SLOTS])
        slot_e = sb("slot_e", [P, SLOTS], I32)
        slot_r = sb("slot_r", [P, SLOTS], I32)
        zero = n2[:, 0, :]
        gidx = sb("gidx", [P, 4], U32)
        yk = [cW, mask0]
        yf = sb("yf", [P, B * T2 * 2])
        ymul = sb("ymul", [P, B * T2, 2, E])

        xg = [x[:, 0, :], x[:, 1, :]]
        xgT = [tT[:, 0, :].rearrange("p (t n) -> p t n", t=2), tT[:, 1, :].rearrange("p (t n) -> p t n", t=2)]
        gate = [QTm[:].rearrange("p a b -> p (a b)"), KTe[:].rearrange("p a b -> p (a b)")]
        hid = [KTo[:].rearrange("p a b -> p (a b)"), VmP[:].rearrange("p a b -> p (a b)")[:, 0:F0]]
        hidT = [On[:].rearrange("p a b -> p (a b)").rearrange("p (f n) -> p f n", n=P),
                h[:].rearrange("p a b -> p (a b)").rearrange("p (f n) -> p f n", n=P)]
        yo = [nT[:, 0, :], nT[:, 1, :]]

        msum = sb("msum", [P, D2])
        lr = sb("lr", [1, E])
        lmx = sb("lmx", [1, 8])
        lmi = sb("lmi", [1, 8], U32)
        x3, x3T, yT, x4, x4T, x5, x5T = x1, tT, nT, x2, xT, h, n2
        qF, kFe, kFo, vF = QTm, KTe, KTo, Vm
        rF, xF = wqm, wkm

        const_in = sem("const_in")
        w0_in = sem("w0_in")
        wA_in = sem("wA_in")
        wM_in = sem("wM_in")
        wC_in = sem("wC_in")
        consts = sem("consts")
        cv = sem("cv")
        xT_in = sem("xT_in")
        x_in = sem("x_in")
        cT_in = sem("cT_in")
        w_filled = [sem("w_filled0"), sem("w_filled1")]
        w_copied = [sem("w_copied0"), sem("w_copied1")]
        f_filled = [sem("f_filled0"), sem("f_filled1")]
        f_copied = [sem("f_copied0"), sem("f_copied1")]
        scores = sem("scores")
        smax = sem("smax")
        expd = sem("expd")
        sums_inv = sem("sums_inv")
        normed = sem("normed")
        turned = sem("turned")
        turned_sb = sem("turned_sb")
        x1_ok = sem("x1_ok")
        x2_ok = sem("x2_ok")
        route_pos = sem("route_pos")
        n1_ok = sem("n1_ok")
        xb_ok = sem("xb_ok")
        len_ok = sem("len_ok")
        mask_ok = sem("mask_ok")
        inv_m = sem("inv_m")
        hx_ok = sem("hx_ok")
        hx_out = sem("hx_out")
        n2_ok = sem("n2_ok")
        rt = sem("rt")
        cnt_ok = sem("cnt_ok")
        dl_ok = sem("dl_ok")
        el_ok = sem("el_ok")
        pos_ok = sem("pos_ok")
        scattered = sem("scattered")
        plan = sem("plan")
        padded = sem("padded")
        zeroed = sem("zeroed")
        xg_in = [sem("xg_in0"), sem("xg_in1")]
        b_x = sem("b_x")
        b_xs = sem("b_xs")
        b_h = sem("b_h")
        b_gate = sem("b_gate")
        b_hid = sem("b_hid")
        b_t = sem("b_t")
        b_ts = sem("b_ts")
        b_y = sem("b_y")
        b_ys = sem("b_ys")
        y_out = [sem("y_out0"), sem("y_out1")]
        gi = sem("gi")
        yk_in = sem("yk_in")
        hx_in = sem("hx_in")
        comb1 = sem("comb1")
        comb = sem("comb")
        c_r = sem("c_r")
        x3_ok = sem("x3_ok")
        scan_ok = sem("scan_ok")
        x4_ok = sem("x4_ok")
        x5_ok = sem("x5_ok")
        cb = sem("cb")
        mi_in = sem("mi_in")
        mask1_ok = sem("mask1_ok")
        rt1 = sem("rt1")
        pick_ok = sem("pick_ok")
        ex_in = sem("ex_in")
        f_r = sem("f_r")
        f_out = sem("f_out")
        out_done = sem("out_done")

        def need(eng, s, n):
            if isinstance(n, int) and n <= 0:
                return
            eng.wait_ge(s, n)

        def apart(eng):
            eng.nop(nofuse=True)

        class Work:
            def __init__(self, banks, filled, copied, per, base):
                self.banks, self.filled, self.copied, self.per, self.base = banks, filled, copied, per, base

            def ps(self, i):
                return self.banks[i % 2]

            def n(self, b, i):
                return b * self.per[i % 2] + (self.base[i % 2] + i // 2)

            def free(self, eng, b, i):
                need(eng, self.copied[i % 2], self.n(b, i))

            def full(self, eng, b, i):
                need(eng, self.filled[i % 2], self.n(b, i) + 1)

            def out(self, eng, b, i):
                need(eng, self.copied[i % 2], self.n(b, i) + 1)

            def fill(self, ins, i):
                ins.then_inc(self.filled[i % 2], 1)

            def copy(self, ins, i):
                ins.then_inc(self.copied[i % 2], 1)

        (CTXW, ATTN0, X1T, XATT, N1T, QM, KM, VM) = range(8, 16)
        HEADS0 = 16
        WA = Work(W_BANK, w_filled, w_copied, (12, 12), (0, 0))
        (OMT, PROJ, N2T, LOGIT, RANK) = range(5, 10)
        F_FIRST = Work(F_BANK, f_filled, f_copied, (5, 5), (0, 0))
        F_NEXT = Work(F_BANK, f_filled, f_copied, (5, 5), (-2, -3))
        F_LAST = Work(F_BANK, f_filled, f_copied, (5, 5), (-5, -5))

        def FA(b):
            return F_NEXT if not isinstance(b, int) or 0 < b < B else F_FIRST if b == 0 else F_LAST

        (K1, V1, X3T, SSM, X4T, Q1) = range(6)
        HEADS1 = 6
        (O1T, PROJ1, X5T, ROUTE) = range(14, 18)
        WC = Work(W_BANK, w_filled, w_copied, (9, 9), (12 * B, 12 * B))
        FC = Work(F_BANK, f_filled, f_copied, (3, 2), (5 * B, 5 * B))
        U0 = U_A * B

        block = ctx.enter_context(nc.Block())

        @block.sync
        def _(sp):
            for t, name in ((wq0, "wq0"), (wk0, "wk0"), (wv0, "wv0")):
                sp.dma_start(t[:], A[name]).then_inc(w0_in, 16)
            sp.dma_start(xT[:], A["xT"][0]).then_inc(xT_in, 16)
            sp.dma_start(cT[:], A["cT"][0]).then_inc(cT_in, 16)
            sp.dma_start(x[:], A["x"][0]).then_inc(x_in, 16)
            sp.dma_start(lens_i[:], A["lens"].partition_broadcast(P)).then_inc(const_in, 16)
            sp.dma_start(bx[:], A["bx"].partition_broadcast(P)).then_inc(const_in, 16)
            sp.dma_start(ln2w[:], A["ln2w"].partition_broadcast(P)).then_inc(const_in, 16)
            sp.dma_start(bv1[:], A["bv1"].partition_broadcast(P)).then_inc(const_in, 16)
            for t, name in ((ln1w, "ln1w"), (av, "a"), (bvec, "b"), (bq1, "bq1"), (bk1, "bk1"), (br1, "br1"),
                            (wr, "wr")):
                sp.dma_start(t[:], A[name]).then_inc(const_in, 16)
            for t, name in ((wo0, "wo0"), (wx, "wx"), (wqm, "wqm"), (wkm, "wkm"), (wvm, "wvm"), (wom, "wom"),
                            (wg, "wg")):
                sp.dma_start(t[:], A[name]).then_inc(wA_in, 16)

            def residual_out(b):
                sp.wait_ge(hx_ok, b + 1)
                sp.dma_start(hx_d[bass.ds(b, 1)].rearrange("e p n -> p (e n)"),
                             xb[:].rearrange("p a b -> p (a b)")).then_inc(hx_out, 16)

            def loads(b, first, last):
                if not last:
                    FA(b).full(sp, b, 4)
                    sp.dma_start(xT[:], A["xT"][bass.ds(b + 1, 1)].rearrange("e p a n -> p (e a) n")).then_inc(xT_in, 16)
                if not first:
                    residual_out(b - 1)
                for t, name in ((w1, "w1"), (w3, "w3"), (w2, "w2")):
                    sp.dma_start(t[:, bass.ds(b, 1)].rearrange("p e a n -> p (e a n)"),
                                 A[name][bass.ds(b, 1)].rearrange("e p a n -> p (e a n)")).then_inc(wM_in, 16)
                if not last:
                    WA.out(sp, b, ATTN0)
                    sp.dma_start(x[:], A["x"][bass.ds(b + 1, 1)].rearrange("e p a n -> p (e a) n")).then_inc(x_in, 16)
                    sp.wait_ge(scores, U_A * b + H0 + 1)
                    sp.dma_start(cT[:], A["cT"][bass.ds(b + 1, 1)].rearrange("e p a n -> p (e a) n")).then_inc(cT_in, 16)

            loads(0, True, False)
            with sp.Fori(1, B - 1) as b:
                loads(b, False, False)
            loads(B - 1, False, True)
            residual_out(B - 1)

            F_LAST.full(sp, B, RANK)
            for t, name in ((wq1, "wq1"), (wk1, "wk1"), (wv1, "wv1"), (wo1, "wo1")):
                sp.dma_start(t, A[name]).then_inc(wC_in, 16)
            sp.dma_start(wout[:], A["wout"]).then_inc(wC_in, 16)
            sp.wait_ge(n2_ok, B)
            sp.dma_start(bout[:], A["bout"].partition_broadcast(P)).then_inc(wC_in, 16)
            sp.dma_start(bo1[:], A["bo1"].partition_broadcast(P)).then_inc(wC_in, 16)

            sp.wait_ge(plan, 14)
            sp.wait_ge(padded, 16 * E)
            sp.wait_ge(scattered, 64 * B)

            def slot_load(t, p, first):
                s = 2 * t + p
                if not first:
                    sp.wait_ge(b_x, s - 1)
                apart(sp)
                row = sp.value_load(slot_r[0:1, bass.ds(s, 1)], min_val=0, max_val=E * REG - P)
                sp.dma_start(xg[p], rows_d[bass.ds(row, P)]).then_inc(xg_in[p], 16)

            def slot_store(t, p):
                s = 2 * t + p
                sp.wait_ge(b_ys, s + 1)
                sp.dma_start(y_d[bass.ds(s * P, P)], yo[p]).then_inc(y_out[p], 16)

            for p in range(2):
                slot_load(0, p, True)
            with sp.Fori(0, SLOTS // 2 - 1) as t:
                for p in range(2):
                    slot_load(t + 1, p, False)
                    slot_store(t, p)
            for p in range(2):
                slot_store(SLOTS // 2 - 1, p)
            for p in range(2):
                sp.wait_ge(y_out[p], 16 * (SLOTS // 2))

            sp.wait_ge(hx_out, 16 * B)

            def loads_c(b, first):
                if not first:
                    sp.wait_ge(comb, b)
                    WC.full(sp, b - 1, V1)
                sp.dma_start(x[:], hx_d[bass.ds(b, 1)].rearrange("e p n -> p (e n)")).then_inc(hx_in, 16)
                sp.dma_start(cT[:], A["cT"][bass.ds(b, 1)].rearrange("e p a n -> p (e a) n")).then_inc(cT_in, 16)
                if not first:
                    sp.wait_ge(mask1_ok, b)
                sp.dma_start(mask_i[:], A["mask"][bass.ds(b, 1)].rearrange("b n -> (b n)").partition_broadcast(P)).then_inc(mi_in, 16)

            def expert_load(b):
                sp.wait_ge(pick_ok, b + 1)
                if not isinstance(b, int) or b > 0:
                    FC.full(sp, b - 1, 4)
                    FC.out(sp, b - 1, 3)
                    sp.wait_ge(f_r, b)
                apart(sp)
                e = sp.value_load(lmi[0:1, 0:1], min_val=0, max_val=E - 1)
                sp.dma_start(W1s, A["W1"][bass.ds(e, 1)].rearrange("e p a n -> p (e a) n")).then_inc(ex_in, 16)
                sp.dma_start(W2s, A["W2"][bass.ds(e, 1)].rearrange("e p a n -> p (e a) n")).then_inc(ex_in, 16)
                sp.dma_start(b1s[:], A["b1"][bass.ds(e, 1)].rearrange("e p n -> p (e n)")).then_inc(ex_in, 16)
                sp.dma_start(b2s[:], A["b2"][bass.ds(e, 1)].rearrange("b n -> (b n)").partition_broadcast(P)).then_inc(ex_in, 16)

            def store_c(b):
                sp.wait_ge(f_out, b + 1)
                sp.dma_start(out[bass.ds(b, 1)].rearrange("e (a p) n -> p (e a) n", p=P), xF[:]).then_inc(out_done, 16)

            loads_c(0, True)
            loads_c(1, False)
            expert_load(0)
            with sp.Fori(1, B - 1) as b:
                loads_c(b + 1, False)
                store_c(b - 1)
                expert_load(b)
            store_c(B - 2)
            expert_load(B - 1)
            store_c(B - 1)
            sp.wait_ge(out_done, 16 * B)

        @block.gpsimd
        def _(g):
            g.memset(ident[:], 0.0).then_inc(cv, 1)
            g.memset(upper[:], 1.0).then_inc(cv, 1)
            g.memset(ones[:], 1.0).then_inc(consts, 1)
            g.memset(half[:], -0.5).then_inc(consts, 1)
            g.memset(run[:], 0.0).then_inc(consts, 1)
            g.wait_ge(cv, 2)
            g.affine_select(out=ident[:], in_=ident[:], compare_op=ALU.not_equal, fill=1.0, base=0,
                            pattern=[[-1, P]], channel_multiplier=1).then_inc(consts, 1)
            g.affine_select(out=upper[:], in_=upper[:], compare_op=ALU.is_gt, fill=0.0, base=0,
                            pattern=[[1, P]], channel_multiplier=-1).then_inc(consts, 1)
            big = dict(allow_small_or_imprecise_dtypes=True)
            g.iota(ki[:], [[1, S]], base=0, channel_multiplier=0, **big).then_inc(consts, 1)
            g.iota(qi[:], [[P, T2]], base=0, channel_multiplier=1, **big).then_inc(consts, 1)
            g.iota(ei[:], [[1, E]], base=0, channel_multiplier=0, **big).then_inc(consts, 1)
            g.iota(ebase[:], [[REG, E]], base=0, channel_multiplier=0, **big).then_inc(consts, 1)
            g.iota(thr[:], [[P, TOK // P]], base=0, channel_multiplier=0, **big).then_inc(consts, 1)
            g.iota(si[:], [[1, SLOTS]], base=0, channel_multiplier=0, **big).then_inc(consts, 1)
            g.iota(pidx[:], [[1, 1]], base=0, channel_multiplier=1, **big).then_inc(consts, 1)
            g.wait_ge(const_in, 16 * 11)
            g.tensor_copy(lens[:], lens_i[:]).then_inc(len_ok, 1)
            g.wait_ge(len_ok, 1)

            def root(n, k):
                g.wait_ge(n.var, k)
                g.tensor_tensor(n.rstd[:], n.ve[:], half[:], ALU.pow).then_inc(n.root, 1)

            pc = sb("pc", [P, 1])
            qn = sb("qn", [P, T2])

            def end(b):
                FA(b).out(g, b, PROJ)
                g.wait_ge(x2_ok, b)
                g.tensor_tensor(xb[:], h[:], x2[:], ALU.add).then_inc(hx_ok, 1)
                root(nA, 4 * b)
                g.wait_ge(pos_ok, b)
                apart(g)
                for t in range(T2):
                    for k in range(2):
                        j = 2 * t + k
                        g.indirect_dma_start(rows_d, bass.IndirectOffsetOnAxis(ap=posu[:, j:j + 1], axis=0),
                                             n2[:, t, :], None).then_inc(scattered, 16)

            def layer0(b, first):
                g.tensor_copy(pc[:], lens[:, bass.ds(b, 1)]).then_inc(len_ok, 1)
                g.wait_ge(len_ok, 2 * b + 2)
                apart(g)
                g.tensor_scalar(qn[:], qi[:], pc[:, 0:1], NEG0 * SQ0, ALU.is_ge, ALU.mult).then_inc(len_ok, 1)
                g.wait_ge(len_ok, 2 * b + 3)
                apart(g)
                for t in range(T2):
                    ins = g.tensor_scalar(mask0[:, t, :], ki[:], pc[:, 0:1], qn[:, t:t + 1], ALU.is_ge, ALU.mult)
                ins.then_inc(mask_ok, 1)
                if not first:
                    end(b)
                root(nA, 4 * b + 1)
                g.wait_ge(x1_ok, b + 1)
                need(g, hx_out, 16 * b)
                for t in range(T2):
                    ins = g.tensor_tensor(xb[:, t, :], x1[:, t, :], bx[:], ALU.add)
                ins.then_inc(xb_ok, 1)
                root(nA, 4 * b + 2)
                root(nA, 4 * b + 3)
            layer0(0, True)
            with g.Fori(1, B) as b:
                layer0(b, False)
            end(B)
            g.wait_ge(scattered, 64 * B)
            g.memset(zero, 0.0).then_inc(zeroed, 1)
            g.wait_ge(zeroed, 1)
            g.wait_ge(plan, 14)
            for e in range(E):
                g.indirect_dma_start(rows_d, bass.IndirectOffsetOnAxis(ap=padu[:, e:e + 1], axis=0),
                                     zero, None).then_inc(padded, 16)

            def gather(b):
                need(g, comb, b)
                need(g, yk_in, 64 * b)
                g.tensor_copy(gidx[:], yu_all[:, bass.ds(b, 1), :].rearrange("p b n -> p (b n)")).then_inc(gi, 1)
                g.wait_ge(gi, b + 1)
                apart(g)
                for t in range(T2):
                    for k in range(2):
                        j = 2 * t + k
                        g.indirect_dma_start(yk[k][:, t, :], None, y_d,
                                             bass.IndirectOffsetOnAxis(ap=gidx[:, j:j + 1], axis=0)).then_inc(yk_in, 16)

            def layer1(b, first, last):
                root(nC, 3 * b + 1)
                if not last:
                    gather(b + 1)
                g.wait_ge(x3_ok, b + 1)
                for t in range(T2):
                    ins = g.tensor_tensor(xb[:, t, :], x3[:, t, :], bout[:], ALU.add)
                ins.then_inc(cb, 1)
                root(nC, 3 * b + 2)
                g.wait_ge(x4_ok, b + 1)
                for t in range(T2):
                    ins = g.tensor_tensor(xb[:, t, :], x4[:, t, :], bo1[:], ALU.add)
                ins.then_inc(cb, 1)
                if not first:
                    ffn_part(b - 1)
                root(nC, 3 * b + 3)

            def ffn_part(b):
                g.wait_ge(ex_in, 64 * (b + 1))
                g.wait_ge(x5_ok, b + 1)
                need(g, f_out, b)
                for t in range(T2):
                    ins = g.tensor_tensor(rF[:, t, :], x5[:, t, :], b2s[:], ALU.add)
                ins.then_inc(f_r, 1)
                root(nF, b + 1)

            for p in range(2):
                g.wait_ge(y_out[p], 16 * (SLOTS // 2))
            g.wait_ge(plan, 17)
            g.wait_ge(wC_in, 16 * 7)
            gather(0)
            layer1(0, True, False)
            with g.Fori(1, B - 1) as b:
                layer1(b, False, False)
            layer1(B - 1, False, True)
            ffn_part(B - 1)

        @block.scalar
        def _(a):
            def exps(src, dst, bias, scale, acc, nm):
                a.wait_ge(smax, nm)
                for t in range(T2):
                    ins = a.activation(dst[:, t, :], src[:, t, :], ACT.Exp, bias=bias[:, t:t + 1], scale=scale,
                                       accum_out=acc(t))
                ins.then_inc(expd, 1)

            def copy_f(b, i):
                FA(b).full(a, b, i)
                ps = FA(b).ps(i)
                if i > 0:
                    ins = a.activation(QT[:, 2 * i - 2:2 * i, :], ps[:], ACT.Copy)
                else:
                    a.activation(KT[:], ps[:, 0, :], ACT.Copy)
                    ins = a.activation(V[:], ps[:, 1, :].rearrange("p (t n) -> p t n", t=2), ACT.Copy)
                FA(b).copy(ins, i)

            def four_heads(W, b, i0, k):
                for g in range(HM // 4):
                    if k == min(4 * g + 6, HM - 1):
                        if g >= 2:
                            W.full(a, b, i0 + 2 * g - 3)
                        copy_half(W, b, i0 + 2 * g, OTq[:, g % 2, :])

            def copy_half(W, b, i, dst):
                W.full(a, b, i)
                W.copy(a.activation(dst, W.ps(i)[:, 0, :], ACT.Copy), i)

            def copy_w(W, b, i, dst):
                W.full(a, b, i)
                W.copy(a.activation(dst, W.ps(i)[:], ACT.Copy), i)

            for i in range(5):
                copy_f(0, i)

            def end(b, i):
                if i == 0:
                    copy_w(FA(b), b, OMT, tT[:])
                if i == 6:
                    copy_w(FA(b), b, N2T, nT[:])

            def end_exp(b):
                a.wait_ge(dl_ok, b)
                a.activation(el[:], dl[:], ACT.Exp).then_inc(el_ok, 1)

            def layer0(b, first, last):
                for i in range(H0 + 3):
                    if i < H0:
                        u = U_A * b + i
                        if i >= 3:
                            a.wait_ge(turned, u - 2)
                        exps(sc_ps[i % 2], probs[i % 3], nmax[:, i % 4], 1.0,
                             lambda t: rs0[:, i % 3, t:t + 1], u + 1)
                    if i >= 3:
                        j = i - 3
                        WA.full(a, b, j)
                        WA.copy(a.activation(OT[:, j, :], WA.ps(j)[:, 0, :], ACT.Copy), j)
                    if not first:
                        end(b, i)
                copy_w(WA, b, CTXW, cW[:])
                if not first:
                    end_exp(b)
                if not last:
                    copy_f(b + 1, 0)
                    copy_f(b + 1, 1)
                copy_w(WA, b, X1T, tT[:])
                exps(probs[2], probs[2], nmax[:, 0], -1.0, lambda t: rs0[:, 0, t:t + 1], U_A * b + H0 + 1)
                if not last:
                    copy_f(b + 1, 2)
                WA.full(a, b, N1T)
                for t in range(D2):
                    ins = a.activation(nT[:, t, :], WA.ps(N1T)[:, t, :], ACT.Copy, scale=ln1w[:, t:t + 1])
                WA.copy(ins, N1T)
                WA.full(a, b, QM)
                WA.copy(a.activation(QTm[:], WA.ps(QM)[:], ACT.Copy, scale=1.0 / SQM), QM)
                WA.full(a, b, KM)
                a.activation(KTe[:], WA.ps(KM)[:], ACT.Copy, scale=even[:, 0:1])
                WA.copy(a.activation(KTo[:], WA.ps(KM)[:], ACT.Copy, scale=odd[:, 0:1]), KM)
                for k in range(HM):
                    u = U_A * b + H0 + 1 + k
                    if k >= 3:
                        a.wait_ge(turned, u - 2)
                    exps(sc_ps[k % 2], probs[k % 3], nmax[:, k % 4], 1.0,
                         lambda t: rsm[:, t, k:k + 1], u + 1)
                    four_heads(WA, b, HEADS0, k)
                    if not last and k < 2:
                        copy_f(b + 1, 3 + k)

            a.wait_ge(consts, 14)
            layer0(0, True, False)
            with a.Fori(1, B - 1) as b:
                layer0(b, False, False)
            layer0(B - 1, False, True)
            for i in (0, 6):
                end(B, i)
            end_exp(B)
            a.activation(ah[:], av[:], ACT.Tanh).then_inc(consts, 1)

            def slot(s, p, first):
                a.wait_ge(b_x, s + 1)
                if not first:
                    a.wait_ge(b_h, s - 1)
                a.activation(xgT[p], bank[p][:, 0, :].rearrange("p (t n) -> p t n", t=2), ACT.Copy).then_inc(b_xs, 1)
                a.wait_ge(b_h, s + 1)
                if not first:
                    a.wait_ge(b_hid, s - 1)
                a.activation(gate[p], bank[2 + 2 * p][:].rearrange("p a b -> p (a b)"), ACT.Silu).then_inc(b_gate, 1)

            def slot_out(s, p, first):
                a.wait_ge(b_t, s + 1)
                if not first:
                    need(a, b_y, s - 1)
                a.activation(hidT[p], bank[6][:].rearrange("p a (c n) -> p (a c) n", n=P), ACT.Copy).then_inc(b_ts, 1)

            slot(0, 0, True)
            slot_out(0, 0, True)
            slot(1, 1, True)

            def slots(t):
                slot_out(2 * t - 1, 1, False)
                slot(2 * t, 0, False)
                slot_out(2 * t, 0, False)
                slot(2 * t + 1, 1, False)

            slots(1)
            with a.Fori(2, SLOTS // 2) as t:
                slots(t)
            slot_out(SLOTS - 1, 1, False)

            def ffn_up(b, i):
                FC.full(a, b, i)
                if i == 0:
                    a.wait_ge(ex_in, 64 * (b + 1))
                for j in range(2):
                    f = 2 * i + j
                    ins = a.activation(hF[:, f, :], FC.ps(i)[:, j, :], ACT.Relu, bias=b1s[:, f:f + 1])
                FC.copy(ins, i)

            def layer1(b, first):
                WC.full(a, b, K1)
                for t in range(D2):
                    a.activation(kFe[:, t, :], WC.ps(K1)[:, t, :], ACT.Identity, bias=bke[:, t:t + 1],
                                 scale=even[:, 0:1])
                    ins = a.activation(kFo[:, t, :], WC.ps(K1)[:, t, :], ACT.Identity, bias=bko[:, t:t + 1],
                                       scale=odd[:, 0:1])
                WC.copy(ins, K1)
                WC.full(a, b, X3T)
                for t in range(D2):
                    ins = a.activation(x3T[:, t, :], WC.ps(X3T)[:, t, :], ACT.Copy, scale=bvec[:, t:t + 1])
                WC.copy(ins, X3T)
                copy_w(WC, b, X4T, x4T[:])
                WC.full(a, b, Q1)
                for t in range(D2):
                    ins = a.activation(qF[:, t, :], WC.ps(Q1)[:, t, :], ACT.Identity, bias=bq1[:, t:t + 1])
                WC.copy(ins, Q1)
                for k in range(HM):
                    u = U_C * b + (U0 + k)
                    exps(probs[k % 3], probs[k % 3], nmax[:, k % 4], -1.0, lambda t: rsm[:, t, k:k + 1], u + 1)
                    four_heads(WC, b, HEADS1, k)
                    if not first and k < 4:
                        ffn_up(b - 1, k)
                copy_w(WC, b, O1T, x3T[:])
                WC.full(a, b, X5T)
                for t in range(D2):
                    ins = a.activation(x5T[:, t, :], WC.ps(X5T)[:, t, :], ACT.Copy, accum_out=msum[:, t:t + 1])
                WC.copy(ins, X5T)

            a.wait_ge(consts, 16)
            layer1(0, True)
            with a.Fori(1, B) as b:
                layer1(b, False)
            for i in range(4):
                ffn_up(B - 1, i)

        @block.tensor
        def _(pe):
            def mm(o, l, rh, k, n):
                return pe.matmul(o, l, rh, start=(k == 0), stop=(k == n - 1))

            def proj(b, i):
                FA(b).free(pe, b, i)
                ps = FA(b).ps(i)
                if i > 0:
                    for j in range(2):
                        hh = 2 * i - 2 + j
                        for t in range(D2):
                            ins = mm(ps[:, j, :], wq0[:, t, hh * P:(hh + 1) * P], xT[:, t, :], t, D2)
                else:
                    for t in range(D2):
                        mm(ps[:, 0, :], wk0[:, t, :], xT[:, t, :], t, D2)
                    for m in range(T2):
                        for t in range(D2):
                            ins = mm(ps[:, 1, m * P:(m + 1) * P], xT[:, t, m * P:(m + 1) * P], wv0[:, t, :], t, D2)
                FA(b).fill(ins, i)

            def turn(W, b, i, src):
                W.free(pe, b, i)
                for t in range(T2):
                    for d in range(D2):
                        ins = pe.transpose(W.ps(i)[:, d, t * P:(t + 1) * P], src[:, t, d * P:(d + 1) * P], ident[:])
                W.fill(ins, i)

            def lin(W, b, i, lT, rh, n=D):
                W.free(pe, b, i)
                for t in range(T2):
                    for d in range(D2):
                        ins = mm(W.ps(i)[:, t, 0:n], lT[:, d, t * P:(t + 1) * P], rh[:, d, :], d, D2)
                W.fill(ins, i)

            def linT(W, b, i, w, xt):
                W.free(pe, b, i)
                for o in range(D2):
                    for d in range(D2):
                        ins = mm(W.ps(i)[:, o, :], w[:, d, o * P:(o + 1) * P], xt[:, d, :], d, D2)
                W.fill(ins, i)

            def turn_probs(src, k, u, ringed):
                if ringed:
                    pe.wait_ge(turned_sb, u - 1)
                for t in range(T2):
                    for m in range(T2):
                        ins = pe.transpose(pt_ps[k % 2][:, m, t * P:(t + 1) * P], src[:, t, m * P:(m + 1) * P], ident[:])
                ins.then_inc(turned, 1)

            def heads(W, b, u_of, q, ke, ko, ring, i0, between):
                for i in range(HM + 5):
                    if i < HM:
                        if i >= 2:
                            pe.wait_ge(expd if W is WA else smax, u_of(i) - 1)
                        j, p0 = i // 8, 32 * ((i % 8) // 2)
                        kk = (ke, ko)[i % 2]
                        for t in range(T2):
                            ins = mm(sc_ps[i % 2][:, t, :], q[p0:p0 + 32, j, t * P:(t + 1) * P], kk[p0:p0 + 32, j, :], 0, 1)
                        ins.then_inc(scores, 1)
                    if 2 <= i < HM + 2:
                        k = i - 2
                        pe.wait_ge(expd, u_of(k) + 1)
                        turn_probs(probs[k % 3], k, u_of(k), k >= 2)
                    if i >= 6 and i % 4 == 2:
                        g = (i - 6) // 4
                        pe.wait_ge(turned_sb, u_of(4 * g + 3) + 1)
                        W.free(pe, b, i0 + 2 * g)
                        for m in range(T2):
                            for j in range(4):
                                k = 4 * g + j
                                ins = mm(W.ps(i0 + 2 * g)[32 * j:32 * j + 32, 0, :],
                                         VmP[:, m, k * HD:k * HD + 32], ring[k % len(ring)][:, m, :], m, T2)
                        W.fill(ins, i0 + 2 * g)
                    if i >= 8 and i % 4 == 0:
                        g = (i - 8) // 4
                        W.out(pe, b, i0 + 2 * g)
                        W.free(pe, b, i0 + 2 * g + 1)
                        for t in range(T2):
                            ins = pe.transpose(W.ps(i0 + 2 * g + 1)[:, t, 0:P], OTq[:, g % 2, t * P:(t + 1) * P], ident[:])
                        W.fill(ins, i0 + 2 * g + 1)
                    between(i)

            pe.wait_ge(consts, 12)
            pe.wait_ge(w0_in, 16 * 3)
            pe.wait_ge(xT_in, 16)
            for i in range(5):
                proj(0, i)
            pe.wait_ge(wA_in, 16 * 7)

            def end(b, i):
                W = FA(b)
                if i == 0:
                    WA.out(pe, b - 1, HEADS0 + 7)
                    turn(W, b, OMT, On)
                if i == 2:
                    W.out(pe, b, OMT)
                    lin(W, b, PROJ, tT, wom)
                if i == 6:
                    pe.wait_ge(n2_ok, b)
                    turn(W, b, N2T, n2)
                if i == 8:
                    W.out(pe, b, N2T)
                    lin(W, b, LOGIT, nT, wg, E)

            def end_ranks(b):
                W = FA(b)
                pe.wait_ge(cnt_ok, b)
                W.free(pe, b, RANK)
                rk = W.ps(RANK)[:, 0, :]
                mm(rk[:, 0:E], upper[:], cnt[:, 0, :], 0, 1)
                mm(rk[:, E:2 * E], upper[:], cnt[:, 1, :], 0, 2)
                mm(rk[:, E:2 * E], ones[:], cnt[:, 0, :], 1, 2)
                mm(rk[:, 2 * E:3 * E], ones[:], cnt[:, 0, :], 0, 2)
                W.fill(mm(rk[:, 2 * E:3 * E], ones[:], cnt[:, 1, :], 1, 2), RANK)

            def layer0(b, first, last):
                def u(k):
                    return U_A * b + k
                FA(b).out(pe, b, 0)
                for i in range(H0 + 3):
                    if i < H0:
                        if i % 2 == 0:
                            FA(b).out(pe, b, 1 + i // 2)
                        if i >= 2:
                            pe.wait_ge(expd, u(i) - 1)
                        for t in range(T2):
                            ins = mm(sc_ps[i % 2][:, t, :], QT[:, i, t * P:(t + 1) * P], KT[:], 0, 1)
                        ins.then_inc(scores, 1)
                    if 2 <= i < H0 + 2:
                        k = i - 2
                        pe.wait_ge(normed, H0 * b + k + 1)
                        turn_probs(probs[k % 3], k, u(k), k >= 2)
                    if i >= 3:
                        k = i - 3
                        pe.wait_ge(turned_sb, u(k) + 1)
                        WA.free(pe, b, k)
                        for m in range(T2):
                            ins = mm(WA.ps(k)[:, 0, :], V[:, m, :], probsT[k % 2][:, m, :], m, T2)
                        WA.fill(ins, k)
                    if not first:
                        end(b, i)
                pe.wait_ge(cT_in, 16 * (b + 1))
                lin(WA, b, CTXW, cT, wx)
                if not first:
                    end_ranks(b)
                WA.out(pe, b, H0 - 2)
                WA.out(pe, b, H0 - 1)
                for t in range(T2):
                    for k in range(H0):
                        ins = mm(WA.ps(ATTN0)[:, t, :], OT[:, k, t * P:(t + 1) * P], wo0[:, k, :], k, H0)
                WA.fill(ins, ATTN0)
                if not last:
                    pe.wait_ge(xT_in, 16 * (b + 2))
                    proj(b + 1, 0)
                    proj(b + 1, 1)
                pe.wait_ge(x1_ok, b + 1)
                turn(WA, b, X1T, x1)
                WA.out(pe, b, X1T)
                for t in range(T2):
                    for d in range(D2):
                        ins = mm(sc_ps[0][:, t, :], tT[:, d, t * P:(t + 1) * P], cT[:, d, :], d, D2)
                ins.then_inc(scores, 1)
                if not last:
                    proj(b + 1, 2)
                pe.wait_ge(expd, u(H0) + 1)
                turn_probs(probs[2], 0, 0, False)
                pe.wait_ge(turned_sb, u(H0) + 1)
                lin(WA, b, XATT, probsT[0], cW)
                pe.wait_ge(n1_ok, b + 1)
                turn(WA, b, N1T, r)
                WA.out(pe, b, N1T)
                linT(WA, b, QM, wqm, nT)
                linT(WA, b, KM, wkm, nT)
                lin(WA, b, VM, nT, wvm)
                WA.out(pe, b, KM)
                WA.out(pe, b, VM)

                def between(i):
                    if not last and i < 2:
                        proj(b + 1, 3 + i)

                heads(WA, b, lambda k: U_A * b + (H0 + 1 + k), QTm, KTe, KTo, ring0, HEADS0, between)
            layer0(0, True, False)
            with pe.Fori(1, B - 1) as b:
                layer0(b, False, False)
            layer0(B - 1, False, True)
            for i in (0, 2, 6, 8):
                end(B, i)
            end_ranks(B)

            def slot_x(t, p):
                pe.wait_ge(xg_in[p], 16 * (t + 1))
                for d in range(D2):
                    ins = pe.transpose(bank[p][:, 0, d * P:(d + 1) * P], xg[p][:, d * P:(d + 1) * P], ident[:])
                ins.then_inc(b_x, 1)

            def slot_up(s, p, first):
                e = pe.value_load(slot_e[0:1, bass.ds(s, 1)], min_val=0, max_val=E - 1)
                pe.wait_ge(b_xs, s + 1)
                if not first:
                    pe.wait_ge(b_hid, s - 1)
                for w, o in ((w1, 2), (w3, 3)):
                    for d in range(D2):
                        ins = mm(bank[o + 2 * p][:].rearrange("p a b -> p (a b)"), xgT[p][:, d, :],
                                 w[:, bass.ds(e, 1), d, :].rearrange("p e n -> p (e n)"), d, D2)
                ins.then_inc(b_h, 1)
                return e

            def slot_t(s, p, first):
                pe.wait_ge(b_hid, s + 1)
                if not first:
                    pe.wait_ge(b_ts, s)
                for f in range(FT0):
                    ins = pe.transpose(bank[6][:].rearrange("p a b -> p (a b)")[:, f * P:(f + 1) * P],
                                       hid[p][:, f * P:(f + 1) * P], ident[:])
                ins.then_inc(b_t, 1)

            def slot_down(s, p, first):
                e = pe.value_load(slot_e[0:1, bass.ds(s, 1)], min_val=0, max_val=E - 1)
                pe.wait_ge(b_ts, s + 1)
                if not first:
                    pe.wait_ge(b_ys, s)
                for f in range(FT0):
                    ins = mm(bank[7][:, 0, :], hidT[p][:, f, :], w2[:, bass.ds(e, 1), f, :].rearrange("p e n -> p (e n)"),
                             f, FT0)
                ins.then_inc(b_y, 1)

            pe.wait_ge(plan, 14)
            pe.wait_ge(wM_in, 48 * B)
            slot_x(0, 0)
            slot_up(0, 0, True)
            slot_x(0, 1)
            slot_t(0, 0, True)
            slot_up(1, 1, True)
            slot_down(0, 0, True)
            with pe.Fori(1, SLOTS // 2) as t:
                slot_x(t, 0)
                slot_t(2 * t - 1, 1, False)
                slot_up(2 * t, 0, False)
                slot_down(2 * t - 1, 1, False)
                slot_x(t, 1)
                slot_t(2 * t, 0, False)
                slot_up(2 * t + 1, 1, False)
                slot_down(2 * t, 0, False)
            slot_t(SLOTS - 1, 1, False)
            slot_down(SLOTS - 1, 1, False)

            def ffn_up(b, i):
                FC.free(pe, b, i)
                for j in range(2):
                    f = 2 * i + j
                    for d in range(D2):
                        ins = mm(FC.ps(i)[:, j, :], W1s[:, d, f * P:(f + 1) * P], x5T[:, d, :], d, D2)
                FC.fill(ins, i)

            def ffn_down(b):
                FC.out(pe, b, 2)
                FC.out(pe, b, 3)
                for t in range(T2):
                    for f in range(FT1):
                        ins = mm(FC.ps(4)[:, t, :], hF[:, f, t * P:(t + 1) * P], W2s[:, f, :], f, FT1)
                FC.fill(ins, 4)

            def layer1(b, first):
                pe.wait_ge(cT_in, 16 * B + 16 * (b + 1))
                linT(WC, b, K1, wk1, cT)
                lin(WC, b, V1, cT, wv1)
                pe.wait_ge(x3_ok, b + 1)
                turn(WC, b, X3T, x3)
                pe.wait_ge(scan_ok, b + 1)
                lin(WC, b, SSM, yT, wout)
                pe.wait_ge(x4_ok, b + 1)
                turn(WC, b, X4T, x4)
                WC.out(pe, b, X4T)
                linT(WC, b, Q1, wq1, x4T)
                WC.out(pe, b, Q1)

                def between(i):
                    if first:
                        return
                    if i < 4:
                        if i == 0:
                            pe.wait_ge(ex_in, 64 * b)
                        ffn_up(b - 1, i)
                    if i == HM:
                        ffn_down(b - 1)
                heads(WC, b, lambda k: U_C * b + (U0 + k), qF, kFe, kFo, ring1, HEADS1, between)
                WC.out(pe, b, O1T - 1)
                turn(WC, b, O1T, On)
                WC.out(pe, b, O1T)
                lin(WC, b, PROJ1, x3T, wo1)
                pe.wait_ge(x5_ok, b + 1)
                turn(WC, b, X5T, x5)
                WC.out(pe, b, X5T)
                WC.free(pe, b, ROUTE)
                for d in range(D2):
                    ins = mm(WC.ps(ROUTE)[0:1, 0, 0:E], msum[:, d:d + 1], wr[:, d, :], d, D2)
                WC.fill(ins, ROUTE)

            pe.wait_ge(wC_in, 16 * 7)
            layer1(0, True)
            with pe.Fori(1, B) as b:
                layer1(b, False)
            pe.wait_ge(ex_in, 64 * B)
            for i in range(4):
                ffn_up(B - 1, i)
            ffn_down(B - 1)

        @block.vector
        def _(v):
            v.memset(VmP[:, :, D:D + HD], 0.0)
            v.wait_ge(consts, 12)
            idv = ident[:].rearrange("p (g two n) -> p g two n", two=2, n=HD)
            v.tensor_reduce(even[:], idv[:, :, 0, :], AX.XY, ALU.add).then_inc(consts, 1)
            v.tensor_reduce(odd[:], idv[:, :, 1, :], AX.XY, ALU.add).then_inc(consts, 1)
            v.wait_ge(consts, 14)
            v.wait_ge(const_in, 16 * 11)
            v.tensor_scalar(bke[:], bk1[:], even[:, 0:1], None, ALU.mult)
            v.tensor_scalar(bko[:], bk1[:], odd[:, 0:1], None, ALU.mult).then_inc(consts, 1)

            def finish_norm(n, k, src, dst, done, mean=True):
                v.wait_ge(n.root, k + 1)
                for t in range(T2):
                    if mean:
                        ins = v.tensor_scalar(dst[:, t, :], src[:, t, :], n.mv[:, t, 0:1], n.rstd[:, t:t + 1],
                                              ALU.subtract, ALU.mult)
                    else:
                        ins = v.tensor_scalar(dst[:, t, :], src[:, t, :], n.rstd[:, t:t + 1], None, ALU.mult)
                ins.then_inc(done, 1)

            def stats(n, k, ks, src):
                for t in range(T2):
                    ins = v.bn_stats(n.st[:, t, :], src[:, t, :])
                ins.then_inc(n.stats, 1)
                v.wait_ge(n.stats, k + 1)
                apart(v)
                for t in range(T2):
                    ins = v.bn_aggr(n.mv[:, t, :], n.st[:, t, :])
                ins.then_inc(n.mean, 1)
                v.wait_ge(n.mean, ks + 1)
                v.tensor_scalar(n.ve[:], n.mv[:, :, 1], EPS, None, ALU.add).then_inc(n.var, 1)

            def squares(n, k, src, junk):
                for t in range(T2):
                    ins = v.tensor_tensor_reduce(junk[:, t, :], src[:, t, :], src[:, t, :], 1.0, 0.0, ALU.mult, ALU.add,
                                                 n.st[:, t, 0:1])
                ins.then_inc(n.stats, 1)
                v.wait_ge(n.stats, k + 1)
                v.tensor_scalar(n.ve[:], n.st[:, :, 0], 1.0 / D, EPS, ALU.mult, ALU.add).then_inc(n.var, 1)

            def max_of(u, k):
                v.wait_ge(scores, u + 1)
                v.tensor_reduce(nmax[:, k % 4, :], sc_ps[k % 2][:], AX.X, ALU.max, negate=True).then_inc(smax, 1)

            def masked_max(u, k, mask, scale, src, dst):
                v.wait_ge(scores, u + 1)
                apart(v)
                for t in range(T2):
                    ins = v.tensor_tensor_reduce(dst[:, t, :], src[:, t, :], mask(t), -scale, BIG, ALU.add, ALU.min,
                                                 nmax[:, k % 4, t:t + 1])
                ins.then_inc(smax, 1)

            def copy_turned(u, k, used=None, ring=None):
                v.wait_ge(turned, u + 1)
                if used:
                    used()
                dst = probsT[k % 2][:] if ring is None else ring[k % len(ring)]
                v.tensor_copy(dst, pt_ps[k % 2][:]).then_inc(turned_sb, 1)

            def copy_ring(W, b, i0, u, k, ring):
                n = len(ring)
                copy_turned(u, k, (lambda: W.full(v, b, i0 + 2 * ((k - n) // 4))) if k >= n else None, ring)

            def head_out(W, b, i0, g, n, ue):
                v.wait_ge(expd, ue)
                hs = slice(4 * g, 4 * g + 4)
                v.reciprocal(rrm[:, :, hs], rsm[:, :, hs]).then_inc(inv_m, 1)
                v.wait_ge(inv_m, 4 * n + (g + 1))
                i = i0 + 2 * g + 1
                W.full(v, b, i)
                for t in range(T2):
                    ins = v.tensor_tensor(On[:, t, 64 * g:64 * g + 64].rearrange("p (h n) -> p h n", n=HD),
                                          W.ps(i)[:, t, 0:P].rearrange("p (h n) -> p h n", n=32)[:, :, 0:HD],
                                          rrm[:, t, hs].unsqueeze(2).broadcast_to([P, 4, HD]), ALU.mult)
                W.copy(ins, i)

            RT = 8

            def end_sum(b):
                W, c = FA(b), b - 1
                W.full(v, b, PROJ)
                ins = v.tensor_tensor(h[:], W.ps(PROJ)[:], x2[:], ALU.add)
                W.copy(ins, PROJ)
                W.out(v, b, PROJ)
                need(v, scattered, 64 * c)
                squares(nA, 4 * c + 3, h, n2)

            def end_norm(b):
                c = b - 1
                v.wait_ge(nA.root, 4 * c + 4)
                for t in range(T2):
                    ins = v.scalar_tensor_tensor(n2[:, t, :], h[:, t, :], nA.rstd[:, t:t + 1], ln2w[:], ALU.mult, ALU.mult)
                ins.then_inc(n2_ok, 1)

            def end_choice(b):
                W, c = FA(b), b - 1
                W.full(v, b, LOGIT)
                W.copy(v.tensor_copy(lg[:], W.ps(LOGIT)[:, :, 0:E]), LOGIT)
                W.out(v, b, LOGIT)
                apart(v)
                for t in range(T2):
                    ins = v.max(mx[:, t, :], lg[:, t, :])
                ins.then_inc(rt, 1)
                v.wait_ge(rt, RT * c + 1)
                apart(v)
                for t in range(T2):
                    ins = v.max_index(mi[:, t, :], mx[:, t, :], lg[:, t, :])
                ins.then_inc(rt, 1)
                v.tensor_tensor(dl[:], mx[:, :, 1], mx[:, :, 0], ALU.subtract).then_inc(dl_ok, 1)
                v.wait_ge(rt, RT * c + 2)
                v.tensor_copy(mf[:], mi[:, :, 0:2]).then_inc(rt, 1)
                v.wait_ge(rt, RT * c + 3)
                for t in range(T2):
                    for k in range(2):
                        ins = v.tensor_scalar(sel[:, t, k, :], ei[:], mf[:, t, k:k + 1], None, ALU.is_equal)
                ins.then_inc(rt, 1)
                v.wait_ge(rt, RT * c + 4)
                v.tensor_tensor(cnt[:], sel[:, :, 0, :], sel[:, :, 1, :], ALU.add).then_inc(cnt_ok, 1)
                v.tensor_copy(sel_all[:, bass.ds(c, 1), :].rearrange("p b n -> p (b n)"),
                              sel[:].rearrange("p t k e -> p (t k e)"))

            def end_rows(b):
                W, c = FA(b), b - 1
                v.wait_ge(el_ok, c + 1)
                v.tensor_scalar(e1[:], el[:], 1.0, None, ALU.add).then_inc(rt, 1)
                v.wait_ge(rt, RT * c + 5)
                v.reciprocal(pk[:, :, 0], e1[:]).then_inc(rt, 1)
                v.wait_ge(rt, RT * c + 6)
                v.tensor_tensor(pk[:, :, 1], pk[:, :, 0], el[:], ALU.mult).then_inc(rt, 1)
                W.full(v, b, RANK)
                v.tensor_tensor(rank[:], W.ps(RANK)[:, 0, 0:2 * E].rearrange("p (t e) -> p t e", t=2),
                                run[:].unsqueeze(1).broadcast_to([P, T2, E]), ALU.add).then_inc(route_pos, 1)
                v.wait_ge(route_pos, 3 * c + 1)
                W.copy(v.tensor_tensor(run[:], W.ps(RANK)[:, 0, 2 * E:3 * E], run[:], ALU.add), RANK)
                W.out(v, b, RANK)
                v.wait_ge(rt, RT * c + 7)
                v.tensor_copy(pk_all[:, bass.ds(c, 1), :].rearrange("p b n -> p (b n)"), pk[:].rearrange("p t k -> p (t k)"))
                v.tensor_copy(rank_all[:, bass.ds(c, 1), :].rearrange("p b n -> p (b n)"), rank[:].rearrange("p t e -> p (t e)"))
                v.tensor_tensor(rowat[:], rank[:], ebase[:].unsqueeze(1).broadcast_to([P, T2, E]), ALU.add).then_inc(rt, 1)
                v.wait_ge(rt, RT * c + 8)
                for k in range(2):
                    ins = v.tensor_tensor(rowsel[:, :, k, :], sel[:, :, k, :], rowat[:], ALU.mult)
                ins.then_inc(route_pos, 1)
                v.wait_ge(route_pos, 3 * c + 2)
                v.tensor_reduce(posf[:], rowsel[:].rearrange("p t k e -> p (t k) e"), AX.X, ALU.add).then_inc(route_pos, 1)
                v.wait_ge(route_pos, 3 * c + 3)
                v.tensor_copy(posu[:], posf[:]).then_inc(pos_ok, 1)

            def layer0(b, first):
                def u(k):
                    return U_A * b + k
                for i in range(H0 + 2):
                    if i < H0:
                        max_of(u(i), i)
                    if 1 <= i <= H0:
                        k = i - 1
                        v.wait_ge(expd, u(k) + 1)
                        v.reciprocal(rr0[:, k % 3, :], rs0[:, k % 3, :]).then_inc(sums_inv, 1)
                        v.wait_ge(sums_inv, (H0 + 1) * b + k + 1)
                        for t in range(T2):
                            ins = v.tensor_scalar(probs[k % 3][:, t, :], probs[k % 3][:, t, :],
                                                  rr0[:, k % 3, t:t + 1], None, ALU.mult)
                        ins.then_inc(normed, 1)
                    if i >= 2:
                        k = i - 2
                        copy_turned(u(k), k, (lambda: WA.full(v, b, k - 2)) if k >= 2 else None)
                    if not first and i == 3:
                        end_sum(b)
                    if not first and i == 4:
                        end_norm(b)
                if not first:
                    end_choice(b)
                    end_rows(b)
                v.wait_ge(x_in, 16 * (b + 1))
                WA.full(v, b, ATTN0)
                ins = v.tensor_tensor(r[:], WA.ps(ATTN0)[:], x[:], ALU.add)
                WA.copy(ins, ATTN0)
                WA.out(v, b, ATTN0)
                stats(nA, 4 * b, 2 * b, r)
                finish_norm(nA, 4 * b, r, x1, x1_ok)
                v.wait_ge(mask_ok, b + 1)
                masked_max(u(H0), 0, lambda t: mask0[:, t, :], 1.0 / SQ0, sc_ps[0], probs[2])
                copy_turned(u(H0), 0)
                v.wait_ge(expd, u(H0) + 1)
                v.reciprocal(rr0[:, 0, :], rs0[:, 0, :]).then_inc(sums_inv, 1)
                v.wait_ge(sums_inv, (H0 + 1) * b + H0 + 1)
                v.wait_ge(xb_ok, b + 1)
                WA.full(v, b, XATT)
                for t in range(T2):
                    ins = v.scalar_tensor_tensor(r[:, t, :], WA.ps(XATT)[:, t, :], rr0[:, 0, t:t + 1], xb[:, t, :],
                                                 ALU.mult, ALU.add)
                WA.copy(ins, XATT)
                WA.out(v, b, XATT)
                stats(nA, 4 * b + 1, 2 * b + 1, r)
                finish_norm(nA, 4 * b + 1, r, x2, x2_ok)
                v.wait_ge(x2_ok, b + 1)
                squares(nA, 4 * b + 2, x2, r)
                finish_norm(nA, 4 * b + 2, x2, r, n1_ok, mean=False)
                WA.full(v, b, VM)
                WA.copy(v.tensor_copy(Vm, WA.ps(VM)[:]), VM)
                for i in range(HM + 2):
                    if i < HM:
                        max_of(u(H0 + 1 + i), i)
                    if i >= 2:
                        k = i - 2
                        copy_ring(WA, b, HEADS0, u(H0 + 1 + k), k, ring0)
                    if i >= 9 and i % 4 == 1:
                        g = (i - 9) // 4
                        head_out(WA, b, HEADS0, g, b, u(H0 + 1 + 4 * g + 3) + 1)
                head_out(WA, b, HEADS0, HM // 4 - 1, b, u(U_A))
            layer0(0, True)
            layer0(1, False)
            with v.Fori(2, B) as b:
                layer0(b, False)
            end_sum(B)
            end_norm(B)
            end_choice(B)
            end_rows(B)

            step = [0]

            def link(ins):
                step[0] += 1
                ins.then_inc(plan, 1)
                v.wait_ge(plan, step[0])

            link(v.tensor_tensor(tcmp[:], run[:].unsqueeze(2).broadcast_to([P, E, TOK // P]),
                                 thr[:].unsqueeze(1).broadcast_to([P, E, TOK // P]), ALU.is_gt))
            link(v.tensor_reduce(tiles[:], tcmp[:], AX.X, ALU.add))
            link(v.tensor_tensor_scan(tend[:], ones[:, 0:E], tiles[:], 0.0, ALU.mult, ALU.add))
            link(v.tensor_tensor(tbeg[:], tend[:], tiles[:], ALU.subtract))
            link(v.tensor_tensor(padf[:], run[:], ebase[:], ALU.add))
            link(v.tensor_scalar(padf[:], padf[:], pidx[:, 0:1], None, ALU.add))
            link(v.tensor_copy(padu[:], padf[:]))
            sl = si[:].unsqueeze(2).broadcast_to([P, SLOTS, E])
            v.tensor_tensor(inA[:], tbeg[:].unsqueeze(1).broadcast_to([P, SLOTS, E]), sl, ALU.is_le)
            link(v.tensor_tensor(inB[:], tend[:].unsqueeze(1).broadcast_to([P, SLOTS, E]), sl, ALU.is_gt))
            link(v.tensor_tensor(inA[:], inA[:], inB[:], ALU.mult))
            v.scalar_tensor_tensor(rbase[:], tbeg[:], -float(P), ebase[:], ALU.mult, ALU.add)
            link(v.tensor_tensor(inB[:], inA[:], ei[:].unsqueeze(1).broadcast_to([P, SLOTS, E]), ALU.mult))
            link(v.tensor_reduce(slf[:, 0, :], inB[:], AX.X, ALU.add))
            link(v.scalar_tensor_tensor(inB[:], sl, float(P), rbase[:].unsqueeze(1).broadcast_to([P, SLOTS, E]), ALU.mult, ALU.add))
            link(v.tensor_tensor(inB[:], inB[:], inA[:], ALU.mult))
            v.tensor_copy(slot_e[:], slf[:, 0, :])
            v.tensor_reduce(slf[:, 1, :], inB[:], AX.X, ALU.add).then_inc(route_pos, 1)
            v.wait_ge(route_pos, 3 * B + 1)
            link(v.tensor_copy(slot_r[:], slf[:, 1, :]))
            assert step[0] == 14
            v.tensor_scalar(ybase[:], tbeg[:], float(P), None, ALU.mult).then_inc(route_pos, 1)
            v.wait_ge(route_pos, 3 * B + 2)
            ra = rank_all[:].rearrange("p b (t e) -> p (b t) e", e=E)
            link(v.tensor_tensor(ra, ra, ybase[:].unsqueeze(1).broadcast_to([P, B * T2, E]), ALU.add))
            sa = sel_all[:].rearrange("p b (t k e) -> p (b t) k e", k=2, e=E)
            for k in range(2):
                ins = v.tensor_tensor(ymul[:, :, k, :], sa[:, :, k, :], ra, ALU.mult)
            link(ins)
            v.tensor_reduce(yf[:], ymul[:].rearrange("p t k e -> p (t k) e"), AX.X, ALU.add).then_inc(route_pos, 1)
            v.wait_ge(route_pos, 3 * B + 3)
            link(v.tensor_copy(yu_all[:].rearrange("p b n -> p (b n)"), yf[:]))

            def slot(s, p, first):
                v.wait_ge(b_gate, s + 1)
                if not first:
                    v.wait_ge(b_t, s - 1)
                v.tensor_tensor(hid[p], bank[3 + 2 * p][:].rearrange("p a b -> p (a b)"), gate[p], ALU.mult).then_inc(b_hid, 1)

            def slot_y(t, p, first):
                s = 2 * t + p
                v.wait_ge(b_y, s + 1)
                if not first:
                    need(v, y_out[p], 16 * t)
                v.tensor_copy(yo[p], bank[7][:, 0, :]).then_inc(b_ys, 1)

            slot(0, 0, True)
            slot(1, 1, True)
            slot_y(0, 0, True)

            def slots(t):
                slot(2 * t, 0, False)
                slot_y(t - 1, 1, False)
                slot(2 * t + 1, 1, False)
                slot_y(t, 0, False)

            slots(1)
            with v.Fori(2, SLOTS // 2) as t:
                slots(t)
            slot_y(SLOTS // 2 - 1, 1, False)

            def ffn_end(b):
                FC.full(v, b, 4)
                v.wait_ge(f_r, b + 1)
                FC.copy(v.tensor_tensor(rF[:], FC.ps(4)[:], rF[:], ALU.add), 4)
                FC.out(v, b, 4)
                stats(nF, b, b, rF)
                need(v, out_done, 16 * b)
                finish_norm(nF, b, rF, xF, f_out)

            def layer1(b, first):
                v.wait_ge(mi_in, 16 * (b + 1))
                v.tensor_scalar(mask1[:], mask_i[:], 0.0, NEG1, ALU.is_equal, ALU.mult).then_inc(mask1_ok, 1)
                WC.full(v, b, V1)
                WC.copy(v.tensor_tensor(vF, WC.ps(V1)[:], bv1[:].unsqueeze(1).broadcast_to([P, 2, D]), ALU.add), V1)
                v.wait_ge(yk_in, 64 * (b + 1))
                v.wait_ge(hx_in, 16 * (b + 1))
                v.tensor_copy(pk[:].rearrange("p t k -> p (t k)"), pk_all[:, bass.ds(b, 1), :].rearrange("p b n -> p (b n)")).then_inc(comb1, 1)
                v.wait_ge(comb1, 2 * b + 1)
                for t in range(T2):
                    ins = v.scalar_tensor_tensor(r[:, t, :], yk[0][:, t, :], pk[:, t, 0:1], x[:, t, :], ALU.mult, ALU.add)
                ins.then_inc(comb1, 1)
                v.wait_ge(comb1, 2 * b + 2)
                for t in range(T2):
                    ins = v.scalar_tensor_tensor(r[:, t, :], yk[1][:, t, :], pk[:, t, 1:2], r[:, t, :], ALU.mult, ALU.add)
                ins.then_inc(comb, 1)
                v.wait_ge(comb, b + 1)
                stats(nC, 3 * b, 3 * b, r)
                finish_norm(nC, 3 * b, r, x3, x3_ok)
                v.wait_ge(consts, 16)
                WC.out(v, b, X3T)
                for t in range(D2):
                    ins = v.tensor_tensor_scan(yT[:, t, :], ah[:, t:t + 1].broadcast_to([P, S]), x3T[:, t, :], 0.0,
                                               ALU.mult, ALU.add)
                ins.then_inc(scan_ok, 1)
                WC.full(v, b, SSM)
                v.wait_ge(cb, 2 * b + 1)
                WC.copy(v.tensor_tensor(r[:], WC.ps(SSM)[:], xb[:], ALU.add), SSM)
                WC.out(v, b, SSM)
                stats(nC, 3 * b + 1, 3 * b + 1, r)
                finish_norm(nC, 3 * b + 1, r, x4, x4_ok)
                for i in range(HM + 2):
                    if i < HM:
                        uu = U_C * b + (U0 + i)
                        if i >= 3:
                            v.wait_ge(turned, uu - 2)
                        masked_max(uu, i, lambda t: mask1[:], 1.0 / SQM, sc_ps[i % 2], probs[i % 3])
                    if i >= 2:
                        k = i - 2
                        copy_ring(WC, b, HEADS1, U_C * b + (U0 + k), k, ring1)
                    if i >= 9 and i % 4 == 1:
                        g = (i - 9) // 4
                        head_out(WC, b, HEADS1, g, b + B, U_C * b + (U0 + 4 * g + 4))
                head_out(WC, b, HEADS1, HM // 4 - 1, b + B, U_C * b + (U0 + HM))
                if not first:
                    ffn_end(b - 1)
                v.wait_ge(cb, 2 * b + 2)
                WC.full(v, b, PROJ1)
                WC.copy(v.tensor_tensor(r[:], WC.ps(PROJ1)[:], xb[:], ALU.add), PROJ1)
                WC.out(v, b, PROJ1)
                stats(nC, 3 * b + 2, 3 * b + 2, r)
                finish_norm(nC, 3 * b + 2, r, x5, x5_ok)
                WC.full(v, b, ROUTE)
                WC.copy(v.scalar_tensor_tensor(lr[:], WC.ps(ROUTE)[0:1, 0, 0:E], 1.0 / S, br1[:], ALU.mult, ALU.add), ROUTE)
                WC.out(v, b, ROUTE)
                apart(v)
                v.max(lmx[:], lr[:]).then_inc(rt1, 1)
                v.wait_ge(rt1, b + 1)
                apart(v)
                v.max_index(lmi[:], lmx[:], lr[:]).then_inc(pick_ok, 1)

            layer1(0, True)
            with v.Fori(1, B) as b:
                layer1(b, False)
            ffn_end(B - 1)


def lay(inputs):
    import numpy as np

    def tiled(w):
        return np.asarray(w).reshape(2, P, -1).transpose(1, 0, 2)

    def a(name):
        return np.asarray(inputs[name])

    def turned(x):
        return x.reshape(B, S, 2, P).transpose(0, 3, 2, 1)

    x, c = a("x"), a("ctx_1024")
    d = {
        "x": x.reshape(B, 2, P, D).transpose(0, 2, 1, 3),
        "xT": turned(x),
        "cT": turned(c),
        "lens": a("_lenS2"),
        "mask": a("mask_Bx1x1xS2_if1").reshape(B, S),
        "wq0": tiled(a("L0_attn_proj_q").transpose(1, 0, 2).reshape(D, H0 * P)),
        "wk0": tiled(a("L0_attn_proj_k")),
        "wv0": tiled(a("L0_attn_proj_v")),
        "wo0": a("L0_attn_proj_o").transpose(2, 0, 1),
        "wx": tiled(a("L0_xattn_W")),
        "bx": a("L0_xattn_b"),
        "ln1w": a("L0_ffn_ln1_w").reshape(2, P).T,
        "ln2w": a("L0_ffn_ln2_w"),
        "wqm": tiled(a("L0_ffn_wq").T),
        "wkm": tiled(a("L0_ffn_wk").T),
        "wvm": tiled(a("L0_ffn_wv").T),
        "wom": tiled(a("L0_ffn_wo").T),
        "wg": tiled(a("L0_ffn_gate_w").T),
        "w1": a("L0_ffn_w1").transpose(0, 2, 1).reshape(E, 2, P, F0).transpose(0, 2, 1, 3).reshape(E, P, 1, 2 * F0),
        "w3": a("L0_ffn_w3").transpose(0, 2, 1).reshape(E, 2, P, F0).transpose(0, 2, 1, 3).reshape(E, P, 1, 2 * F0),
        "w2": a("L0_ffn_w2").transpose(0, 2, 1).reshape(E, FT0, P, D).transpose(0, 2, 1, 3).reshape(E, P, 1, FT0 * D),
        "a": a("L1_attn_a").reshape(2, P).T,
        "b": a("L1_attn_b").reshape(2, P).T,
        "wout": tiled(a("L1_attn_w_out").T),
        "bout": a("L1_attn_b_out"),
        "wv1": tiled(a("L1_xattn_Wv")),
        "wk1": tiled(a("L1_xattn_Wk")),
        "wq1": tiled(a("L1_xattn_Wq")),
        "wo1": tiled(a("L1_xattn_Wo")),
        "bv1": a("L1_xattn_bv"),
        "bk1": a("L1_xattn_bk").reshape(2, P).T,
        "bq1": a("L1_xattn_bq").reshape(2, P).T,
        "bo1": a("L1_xattn_bo"),
        "wr": tiled(a("L1_ffn_Wr")),
        "br1": a("L1_ffn_br").reshape(1, E),
        "W1": a("L1_ffn_W1").reshape(E, 2, P, F1).transpose(0, 2, 1, 3),
        "b1": a("L1_ffn_b1").reshape(E, FT1, P).transpose(0, 2, 1),
        "W2": a("L1_ffn_W2").reshape(E, FT1, P, D).transpose(0, 2, 1, 3),
        "b2": a("L1_ffn_b2"),
    }
    return {k: np.ascontiguousarray(v) for k, v in d.items()}


def kernel(**inputs):
    import concourse.bacc as _bacc
    from concourse.bass_utils import run_bass_kernel_spmd as _run

    nc = _bacc.Bacc("TRN2", target_bir_lowering=False, num_devices=1)
    arrays, A = {}, {}
    for name, v in lay(inputs).items():
        arrays[f"in_{name}"] = v
        A[name] = nc.dram_tensor(f"in_{name}", v.shape, mybir.dt.from_np(v.dtype), kind="ExternalInput").ap()
    out = nc.dram_tensor("out_0", [B, S, D], F32, kind="ExternalOutput").ap()
    build(nc, A, out)
    r = _run(nc, [arrays], core_ids=[0])
    return r.results[0]["out_0"]
```

```python
from contextlib import ExitStack

import concourse.bass as bass
from concourse import mybir

F32 = mybir.dt.float32
I32 = mybir.dt.int32
U32 = mybir.dt.uint32
ALU = mybir.AluOpType
ACT = mybir.ActivationFunctionType
AX = mybir.AxisListType

P = 128
B = 8
S = 256
D = 256
T2 = S // P
D2 = D // P
H0 = 8
HM = 16
HD = D // HM
E = 8
F0 = 512
FT0 = F0 // P
F1 = 1024
FT1 = F1 // P
TOK = B * S
REG = TOK + P
SLOTS = 2 * TOK // P + E
EPS = 1e-5
NEG0 = -1e13
NEG1 = -1e20
U_A = H0 + 1 + HM
U_C = HM
SQ0 = float(D) ** 0.5
SQM = float(HD) ** 0.5
BIG = 3e38


def build(nc, A, out):
    with ExitStack() as ctx:
        def sb(name, shape, dt=F32):
            return ctx.enter_context(nc.sbuf_tensor("s_" + name, shape, dt))

        def sem(name):
            return ctx.enter_context(nc.semaphore(name))

        rows_d = nc.dram_tensor("rows_by_expert", [E * REG, D], F32, kind="Internal").ap()
        y_d = nc.dram_tensor("expert_out", [SLOTS * P, D], F32, kind="Internal").ap()
        hx_d = nc.dram_tensor("residual", [B, P, T2 * D], F32, kind="Internal").ap()

        bank = [ctx.enter_context(nc.psum_tensor(f"bank{i}", [P, 2, 256], F32)) for i in range(8)]
        sc_ps = bank[0:2]
        pt_ps = bank[2:4]
        W_BANK = (bank[4], bank[7])
        F_BANK = (bank[5], bank[6])

        wq0 = sb("wq0", [P, D2, H0 * P])
        wk0 = sb("wk0", [P, D2, P])
        wv0 = sb("wv0", [P, D2, P])
        wo0 = sb("wo0", [P, H0, D])
        wx = sb("wx", [P, D2, D])
        wqm = sb("wqm", [P, D2, D])
        wkm = sb("wkm", [P, D2, D])
        wvm = sb("wvm", [P, D2, D])
        wom = sb("wom", [P, D2, D])
        wg = sb("wg", [P, D2, E])
        w1 = sb("w1", [P, E, D2, F0])
        w3 = sb("w3", [P, E, D2, F0])
        w2 = sb("w2", [P, E, FT0, D])
        cw = wq0[:].rearrange("p a (c n) -> p (a c) n", n=D)
        wv1, wk1, wq1, wo1 = (cw[:, 2 * i:2 * i + 2, :] for i in range(4))
        wout = wx
        wr = sb("wr", [P, D2, E])

        ident = sb("ident", [P, P])
        upper = sb("upper", [P, P])
        ones = sb("ones", [P, P])
        ki = sb("ki", [P, S])
        qi = sb("qi", [P, T2])
        ei = sb("ei", [P, E])
        ebase = sb("ebase", [P, E])
        thr = sb("thr", [P, TOK // P])
        si = sb("si", [P, SLOTS])
        half = sb("half", [P, T2])
        even = sb("even", [P, 1])
        odd = sb("odd", [P, 1])
        lens_i = sb("lens_i", [P, B], I32)
        lens = sb("lens", [P, B])
        ln1w = sb("ln1w", [P, D2])
        bx = sb("bx", [P, D])
        ln2w = sb("ln2w", [P, D])
        bout, bo1, bv1 = bx, ln2w, sb("bv1", [P, D])
        ah = sb("ah", [P, D2])
        av = sb("av", [P, D2])
        bvec = sb("bvec", [P, D2])
        bq1 = sb("bq1", [P, D2])
        bk1 = sb("bk1", [P, D2])
        bke = sb("bke", [P, D2])
        bko = sb("bko", [P, D2])
        br1 = sb("br1", [1, E])

        def act_tile(name):
            return sb(name, [P, 2, 256])

        x = act_tile("x")
        xT = act_tile("xT")
        cT = act_tile("cT")
        QT = sb("QT", [P, H0, S])
        OT = sb("OT", [P, H0, S])
        KT = sb("KT", [P, S])
        V = sb("V", [P, T2, P])
        probs = [act_tile(f"probs{i}") for i in range(3)]
        probsT = [act_tile(f"probsT{i}") for i in range(2)]
        cW = act_tile("cW")
        r = act_tile("r")
        x1 = act_tile("x1")
        xb = act_tile("xb")
        tT = act_tile("tT")
        mask0 = act_tile("mask0")
        x2 = act_tile("x2")
        nT = act_tile("nT")
        QTm = act_tile("QTm")
        KTe = act_tile("KTe")
        KTo = act_tile("KTo")
        VmP = sb("VmP", [P, T2, D + HD])
        Vm = VmP[:, :, 0:D]
        On = act_tile("On")
        h = act_tile("h")
        n2 = act_tile("n2")
        nmax = sb("nmax", [P, 4, T2])
        rs0 = sb("rs0", [P, 3, T2])
        rr0 = sb("rr0", [P, 3, T2])
        rsm = sb("rsm", [P, T2, HM])
        rrm = sb("rrm", [P, T2, HM])

        W1s = QT[:].rearrange("p h n -> p (h n)").rearrange("p (t f) -> p t f", t=D2)
        ring0 = [probsT[i][:] for i in range(2)] + [OT[:, 2 * i:2 * i + 2, :] for i in range(4)]
        ring1 = [w1[:, i, :, 0:S] for i in range(6)]
        OTq0, OTq1 = r, w3[:, 0, :, 0:S]
        oT = w3[:, 1, :, 0:S]
        r5 = w3[:, 2, :, 0:S]
        x4b = w3[:, 3, :, 0:S]
        W2s = OT[:].rearrange("p h n -> p (h n)").rearrange("p (f d) -> p f d", d=D)
        b1s = sb("b1s", [P, FT1])
        b2s = sb("b2s", [P, D])
        hF = wo0[:].rearrange("p h n -> p (h n)").rearrange("p (f n) -> p f n", n=S)
        last_expert = (w2[:, 0:2].rearrange("p e f n -> p (e f n)").rearrange("p (t f) -> p t f", t=D2),
                       w2[:, 2:4].rearrange("p e f n -> p (e f) n"), w2[:, 5, 0, 0:FT1], w2[:, 4, 0, :])

        def expert_of(c):
            return last_expert if isinstance(c, int) and c == B - 1 else (W1s, W2s, b1s[:], b2s[:])

        mask_i = sb("mask_i", [P, S], I32)
        mask1 = sb("mask1", [P, S])

        class Norm:
            def __init__(self, name):
                self.st = sb(name + "_st", [P, T2, 6])
                self.mv = sb(name + "_mv", [P, T2, 2])
                self.ve = sb(name + "_ve", [P, T2])
                self.rstd = sb(name + "_rstd", [P, T2])
                self.stats, self.mean, self.var, self.root = (
                    sem(name + s) for s in ("_stats", "_mean", "_var", "_root"))

        nA, nC, nF = Norm("na"), Norm("nc"), Norm("nf")

        lg = sb("lg", [P, T2, E])
        mx = sb("mx", [P, T2, 8])
        mi = sb("mi", [P, T2, 8], U32)
        mf = sb("mf", [P, T2, 2])
        sel = sb("sel", [P, T2, 2, E])
        cnt = sb("cnt", [P, T2, E])
        dl = sb("dl", [P, T2])
        el = sb("el", [P, T2])
        e1 = sb("e1", [P, T2])
        pk = sb("pk", [P, T2, 2])
        run = sb("run", [P, E])
        rank = sb("rank", [P, T2, E])
        rowsel = sb("rowsel", [P, T2, 2, E])
        rowat = sb("rowat", [P, T2, E])
        posf = sb("posf", [P, T2 * 2])
        posu = sb("posu", [P, T2 * 2], U32)
        sel_all = sb("sel_all", [P, B, T2 * 2 * E])
        rank_all = sb("rank_all", [P, B, T2 * E])
        pk_all = sb("pk_all", [P, B, T2 * 2])
        yu_all = sb("yu_all", [P, B, T2 * 2], U32)
        tiles = sb("tiles", [P, E])
        tcmp = sb("tcmp", [P, E, TOK // P])
        tend = sb("tend", [P, E])
        tbeg = sb("tbeg", [P, E])
        ybase = sb("ybase", [P, E])
        rbase = sb("rbase", [P, E])
        padf = sb("padf", [P, E])
        padu = sb("padu", [P, E], U32)
        pidx = sb("pidx", [P, 1])
        inA = sb("inA", [P, SLOTS, E])
        inB = sb("inB", [P, SLOTS, E])
        slf = sb("slf", [P, 3, SLOTS])
        slot_e = sb("slot_e", [P, SLOTS], I32)
        slot_r = sb("slot_r", [P, SLOTS], I32)
        zero = cW[:, 0, :]
        gidx = sb("gidx", [P, 4], U32)
        yk = [cW, mask0]
        yf = sb("yf", [P, B * T2 * 2])
        ymul = sb("ymul", [P, B * T2, 2, E])

        xg = [x[:, 0, :], x[:, 1, :]]
        xgT = [tT[:, 0, :].rearrange("p (t n) -> p t n", t=2), tT[:, 1, :].rearrange("p (t n) -> p t n", t=2)]
        gate = [QTm[:].rearrange("p a b -> p (a b)"), KTe[:].rearrange("p a b -> p (a b)")]
        hid = [KTo[:].rearrange("p a b -> p (a b)"), VmP[:].rearrange("p a b -> p (a b)")[:, 0:F0]]
        hidT = [On[:].rearrange("p a b -> p (a b)").rearrange("p (f n) -> p f n", n=P),
                h[:].rearrange("p a b -> p (a b)").rearrange("p (f n) -> p f n", n=P)]
        yo = [nT[:, 0, :], nT[:, 1, :]]

        msum = sb("msum", [P, D2])
        lr = sb("lr", [1, E])
        lmx = sb("lmx", [1, 8])
        lmi = sb("lmi", [1, 8], U32)
        x3, x3T, yT, x4, x4T, x5, x5T = x1, tT, nT, x2, xT, h, n2
        qF, kFe, kFo, vF = QTm, KTe, KTo, Vm
        rF, xF = wqm, wkm

        const_in = sem("const_in")
        w0_in = sem("w0_in")
        wA_in = sem("wA_in")
        wM_in = sem("wM_in")
        wC_in = sem("wC_in")
        consts = sem("consts")
        cv = sem("cv")
        xT_in = sem("xT_in")
        x_in = sem("x_in")
        cT_in = sem("cT_in")
        w_filled = [sem("w_filled0"), sem("w_filled1")]
        w_copied = [sem("w_copied0"), sem("w_copied1")]
        f_filled = [sem("f_filled0"), sem("f_filled1")]
        f_copied = [sem("f_copied0"), sem("f_copied1")]
        scores = sem("scores")
        smax = sem("smax")
        expd = sem("expd")
        sums_inv = sem("sums_inv")
        normed = sem("normed")
        turned = sem("turned")
        turned_sb = sem("turned_sb")
        x1_ok = sem("x1_ok")
        x2_ok = sem("x2_ok")
        route_pos = sem("route_pos")
        n1_ok = sem("n1_ok")
        xb_ok = sem("xb_ok")
        len_ok = sem("len_ok")
        mask_ok = sem("mask_ok")
        inv_m = sem("inv_m")
        hx_ok = sem("hx_ok")
        hx_out = sem("hx_out")
        n2_ok = sem("n2_ok")
        rt = sem("rt")
        cnt_ok = sem("cnt_ok")
        dl_ok = sem("dl_ok")
        el_ok = sem("el_ok")
        pos_ok = sem("pos_ok")
        scattered = sem("scattered")
        plan = sem("plan")
        padded = sem("padded")
        zeroed = sem("zeroed")
        xg_in = [sem("xg_in0"), sem("xg_in1")]
        b_x = sem("b_x")
        b_xs = sem("b_xs")
        b_h = sem("b_h")
        b_gate = sem("b_gate")
        b_hid = sem("b_hid")
        b_t = sem("b_t")
        b_ts = sem("b_ts")
        b_y = sem("b_y")
        b_ys = sem("b_ys")
        y_out = [sem("y_out0"), sem("y_out1")]
        gi = sem("gi")
        yk_in = sem("yk_in")
        hx_in = sem("hx_in")
        comb1 = sem("comb1")
        comb = sem("comb")
        x3_ok = sem("x3_ok")
        scan_ok = sem("scan_ok")
        x4_ok = sem("x4_ok")
        x5_ok = sem("x5_ok")
        x3b_ok = sem("x3b_ok")
        x4b_ok = sem("x4b_ok")
        mi_in = sem("mi_in")
        mask1_ok = sem("mask1_ok")
        rt1 = sem("rt1")
        pick_ok = sem("pick_ok")
        ex_in = sem("ex_in")
        f_r = sem("f_r")
        f_out = sem("f_out")
        out_done = sem("out_done")

        def need(eng, s, n):
            if isinstance(n, int) and n <= 0:
                return
            eng.wait_ge(s, n)

        def apart(eng):
            eng.nop(nofuse=True)

        class Work:
            def __init__(self, banks, filled, copied, per, base):
                self.banks, self.filled, self.copied, self.per, self.base = banks, filled, copied, per, base

            def ps(self, i):
                return self.banks[i % 2]

            def n(self, b, i):
                return b * self.per[i % 2] + (self.base[i % 2] + i // 2)

            def free(self, eng, b, i):
                need(eng, self.copied[i % 2], self.n(b, i))

            def full(self, eng, b, i):
                need(eng, self.filled[i % 2], self.n(b, i) + 1)

            def out(self, eng, b, i):
                need(eng, self.copied[i % 2], self.n(b, i) + 1)

            def fill(self, ins, i):
                ins.then_inc(self.filled[i % 2], 1)

            def copy(self, ins, i):
                ins.then_inc(self.copied[i % 2], 1)

        (ATTN0, X1T, XATT, N1T, QM, KM, VM) = range(8, 15)
        HEADS0 = 15
        WA = Work(W_BANK, w_filled, w_copied, (12, 11), (0, 0))
        CTXW = 5
        (OMT, PROJ, N2T, LOGIT, RANK) = range(6, 11)
        F_FIRST = Work(F_BANK, f_filled, f_copied, (6, 5), (0, 0))
        F_NEXT = Work(F_BANK, f_filled, f_copied, (6, 5), (-3, -2))
        F_LAST = Work(F_BANK, f_filled, f_copied, (6, 5), (-6, -5))

        def FA(b):
            return F_NEXT if not isinstance(b, int) or 0 < b < B else F_FIRST if b == 0 else F_LAST

        (O1T, PROJ1, X3T, SSM, X5T, ROUTE, X4T, DOWN, K1, Q1, V1) = (1, 3, 5, 7, 8, 9, 10, 11, 12, 13, 14)
        UP = (0, 2, 4, 6)
        UP_AT = (0, 1, 3, 4)
        DOWN_AT = (11, 13)
        HEADS1 = 0
        WC = Work(W_BANK, w_filled, w_copied, (4, 4), (12 * B, 11 * B))
        BEGIN = (X3T, SSM, X4T, K1, Q1, V1)
        FIRST = (K1, V1, X3T, SSM, X4T, Q1)
        END = (O1T, PROJ1, X5T, ROUTE)
        EXPERT = (*UP, DOWN)

        class Bodies(Work):

            def n(self, b, i):
                if not isinstance(b, int):
                    return b * self.per[i % 2] + (self.n(2, i) - 2 * self.per[i % 2])
                done = [(-1, j) for j in FIRST]
                done += [(c, j) for c in range(B + 2) for j in range(15)
                        if (j in BEGIN and c + 1 < B) or (j in END and 0 <= c - 1 < B) or (j in EXPERT and c >= 2)]
                return self.base[i % 2] + sum(1 for u in done[:done.index((b, i))] if u[1] % 2 == i % 2)

        FC = Bodies(F_BANK, f_filled, f_copied, (8, 7), (6 * B, 5 * B))
        U0 = U_A * B

        block = ctx.enter_context(nc.Block())

        @block.sync
        def _(sp):
            for t, name in ((wq0, "wq0"), (wk0, "wk0"), (wv0, "wv0")):
                sp.dma_start(t[:], A[name]).then_inc(w0_in, 16)
            sp.dma_start(xT[:], A["xT"][0]).then_inc(xT_in, 16)
            sp.dma_start(cT[:], A["cT"][0]).then_inc(cT_in, 16)
            sp.dma_start(x[:], A["x"][0]).then_inc(x_in, 16)
            sp.dma_start(lens_i[:], A["lens"].partition_broadcast(P)).then_inc(const_in, 16)
            sp.dma_start(bx[:], A["bx"].partition_broadcast(P)).then_inc(const_in, 16)
            sp.dma_start(ln2w[:], A["ln2w"].partition_broadcast(P)).then_inc(const_in, 16)
            sp.dma_start(bv1[:], A["bv1"].partition_broadcast(P)).then_inc(const_in, 16)
            for t, name in ((ln1w, "ln1w"), (av, "a"), (bvec, "b"), (bq1, "bq1"), (bk1, "bk1"), (br1, "br1"),
                            (wr, "wr")):
                sp.dma_start(t[:], A[name]).then_inc(const_in, 16)
            for t, name in ((wo0, "wo0"), (wx, "wx"), (wqm, "wqm"), (wkm, "wkm"), (wvm, "wvm"), (wom, "wom"),
                            (wg, "wg")):
                sp.dma_start(t[:], A[name]).then_inc(wA_in, 16)

            def residual_out(b):
                sp.wait_ge(hx_ok, b + 1)
                sp.dma_start(hx_d[bass.ds(b, 1)].rearrange("e p n -> p (e n)"),
                             xb[:].rearrange("p a b -> p (a b)")).then_inc(hx_out, 16)

            def loads(b, first, last):
                if not last:
                    FA(b).full(sp, b, 4)
                    sp.dma_start(xT[:], A["xT"][bass.ds(b + 1, 1)].rearrange("e p a n -> p (e a) n")).then_inc(xT_in, 16)
                if not first:
                    residual_out(b - 1)
                for t, name in ((w1, "w1"), (w3, "w3"), (w2, "w2")):
                    sp.dma_start(t[:, bass.ds(b, 1)].rearrange("p e a n -> p (e a n)"),
                                 A[name][bass.ds(b, 1)].rearrange("e p a n -> p (e a n)")).then_inc(wM_in, 16)
                if not last:
                    WA.out(sp, b, ATTN0)
                    sp.dma_start(x[:], A["x"][bass.ds(b + 1, 1)].rearrange("e p a n -> p (e a) n")).then_inc(x_in, 16)
                    sp.wait_ge(scores, U_A * b + H0 + 1)
                    sp.dma_start(cT[:], A["cT"][bass.ds(b + 1, 1)].rearrange("e p a n -> p (e a) n")).then_inc(cT_in, 16)

            loads(0, True, False)
            with sp.Fori(1, B - 1) as b:
                loads(b, False, False)
            loads(B - 1, False, True)
            residual_out(B - 1)

            F_LAST.full(sp, B, RANK)
            for t, name in ((wq1, "wq1"), (wk1, "wk1"), (wv1, "wv1"), (wo1, "wo1")):
                sp.dma_start(t, A[name]).then_inc(wC_in, 16)
            sp.dma_start(wout[:], A["wout"]).then_inc(wC_in, 16)
            sp.wait_ge(n2_ok, B)
            sp.dma_start(bout[:], A["bout"].partition_broadcast(P)).then_inc(wC_in, 16)
            sp.dma_start(bo1[:], A["bo1"].partition_broadcast(P)).then_inc(wC_in, 16)

            def cT_load(b):
                sp.dma_start(cT[:], A["cT"][bass.ds(b, 1)].rearrange("e p a n -> p (e a) n")).then_inc(cT_in, 16)

            cT_load(0)

            sp.wait_ge(plan, 14)
            sp.wait_ge(padded, 16 * E)
            sp.wait_ge(scattered, 64 * B)

            def slot_load(t, p, first):
                s = 2 * t + p
                if not first:
                    sp.wait_ge(b_x, s - 1)
                apart(sp)
                row = sp.value_load(slot_r[0:1, bass.ds(s, 1)], min_val=0, max_val=E * REG - P)
                sp.dma_start(xg[p], rows_d[bass.ds(row, P)]).then_inc(xg_in[p], 16)

            def slot_store(t, p):
                s = 2 * t + p
                sp.wait_ge(b_ys, s + 1)
                sp.dma_start(y_d[bass.ds(s * P, P)], yo[p]).then_inc(y_out[p], 16)

            for p in range(2):
                slot_load(0, p, True)
            slot_load(1, 0, False)
            slot_load(1, 1, False)
            slot_store(0, 0)
            with sp.Fori(1, SLOTS // 2 - 1) as t:
                slot_load(t + 1, 0, False)
                slot_store(t - 1, 1)
                slot_load(t + 1, 1, False)
                slot_store(t, 0)
            slot_store(SLOTS // 2 - 2, 1)
            for p in range(2):
                slot_store(SLOTS // 2 - 1, p)
            for p in range(2):
                sp.wait_ge(y_out[p], 16 * (SLOTS // 2))

            sp.wait_ge(hx_out, 16 * B)

            def x_load(b):
                sp.dma_start(x[:], hx_d[bass.ds(b, 1)].rearrange("e p n -> p (e n)")).then_inc(hx_in, 16)

            def mask_load(b):
                sp.dma_start(mask_i[:], A["mask"][bass.ds(b, 1)].rearrange("b n -> (b n)").partition_broadcast(P)).then_inc(mi_in, 16)

            def expert_load(b):
                sp.wait_ge(pick_ok, b + 1)
                if not isinstance(b, int) or 0 < b < B - 1:
                    FC.full(sp, b + 1, DOWN)
                    FC.out(sp, b + 1, UP[3])
                    apart(sp)
                    sp.wait_ge(f_r, b)
                apart(sp)
                e = sp.value_load(lmi[0:1, 0:1], min_val=0, max_val=E - 1)
                v1, v2, c1, c2 = expert_of(b)
                sp.dma_start(v1, A["W1"][bass.ds(e, 1)].rearrange("e p a n -> p (e a) n")).then_inc(ex_in, 16)
                sp.dma_start(v2, A["W2"][bass.ds(e, 1)].rearrange("e p a n -> p (e a) n")).then_inc(ex_in, 16)
                sp.dma_start(c1, A["b1"][bass.ds(e, 1)].rearrange("e p n -> p (e n)")).then_inc(ex_in, 16)
                sp.dma_start(c2, A["b2"][bass.ds(e, 1)].rearrange("b n -> (b n)").partition_broadcast(P)).then_inc(ex_in, 16)

            def store_c(b):
                sp.wait_ge(f_out, b + 1)
                sp.dma_start(out[bass.ds(b, 1)].rearrange("e (a p) n -> p (e a) n", p=P), xF[:]).then_inc(out_done, 16)

            def body(b, load, expert, store):
                if load:
                    sp.wait_ge(comb, b + 2)
                    x_load(b + 2)
                if expert:
                    expert_load(b - 1)
                if store:
                    store_c(b - 2)
                if load:
                    sp.wait_ge(mask1_ok, b + 2)
                    mask_load(b + 2)
                    FC.full(sp, b, V1)
                    cT_load(b + 2)

            x_load(0)
            mask_load(0)
            body(-1, True, False, False)
            body(0, True, False, False)
            body(1, True, True, False)
            with sp.Fori(2, B - 2) as b:
                body(b, True, True, True)
            for b in range(B - 2, B + 1):
                body(b, False, True, True)
            store_c(B - 1)
            sp.wait_ge(out_done, 16 * B)

        @block.gpsimd
        def _(g):
            g.memset(ident[:], 0.0).then_inc(cv, 1)
            g.memset(upper[:], 1.0).then_inc(cv, 1)
            g.memset(ones[:], 1.0).then_inc(consts, 1)
            g.memset(half[:], -0.5).then_inc(consts, 1)
            g.memset(run[:], 0.0).then_inc(consts, 1)
            g.wait_ge(cv, 2)
            g.affine_select(out=ident[:], in_=ident[:], compare_op=ALU.not_equal, fill=1.0, base=0,
                            pattern=[[-1, P]], channel_multiplier=1).then_inc(consts, 1)
            g.affine_select(out=upper[:], in_=upper[:], compare_op=ALU.is_gt, fill=0.0, base=0,
                            pattern=[[1, P]], channel_multiplier=-1).then_inc(consts, 1)
            big = dict(allow_small_or_imprecise_dtypes=True)
            g.iota(ki[:], [[1, S]], base=0, channel_multiplier=0, **big).then_inc(consts, 1)
            g.iota(qi[:], [[P, T2]], base=0, channel_multiplier=1, **big).then_inc(consts, 1)
            g.iota(ei[:], [[1, E]], base=0, channel_multiplier=0, **big).then_inc(consts, 1)
            g.iota(ebase[:], [[REG, E]], base=0, channel_multiplier=0, **big).then_inc(consts, 1)
            g.iota(thr[:], [[P, TOK // P]], base=0, channel_multiplier=0, **big).then_inc(consts, 1)
            g.iota(si[:], [[1, SLOTS]], base=0, channel_multiplier=0, **big).then_inc(consts, 1)
            g.iota(pidx[:], [[1, 1]], base=0, channel_multiplier=1, **big).then_inc(consts, 1)
            g.wait_ge(const_in, 16 * 11)
            g.tensor_copy(lens[:], lens_i[:]).then_inc(len_ok, 1)
            g.wait_ge(len_ok, 1)

            def root(n, k):
                g.wait_ge(n.var, k)
                g.tensor_tensor(n.rstd[:], n.ve[:], half[:], ALU.pow).then_inc(n.root, 1)

            pc = sb("pc", [P, 1])
            qn = sb("qn", [P, T2])

            def end(b):
                FA(b).out(g, b, PROJ)
                g.wait_ge(x2_ok, b)
                g.tensor_tensor(xb[:], h[:], x2[:], ALU.add).then_inc(hx_ok, 1)
                root(nA, 4 * b)
                g.wait_ge(pos_ok, b)
                apart(g)
                for t in range(T2):
                    for k in range(2):
                        j = 2 * t + k
                        g.indirect_dma_start(rows_d, bass.IndirectOffsetOnAxis(ap=posu[:, j:j + 1], axis=0),
                                             n2[:, t, :], None).then_inc(scattered, 16)

            def layer0(b, first):
                g.tensor_copy(pc[:], lens[:, bass.ds(b, 1)]).then_inc(len_ok, 1)
                g.wait_ge(len_ok, 2 * b + 2)
                apart(g)
                g.tensor_scalar(qn[:], qi[:], pc[:, 0:1], NEG0 * SQ0, ALU.is_ge, ALU.mult).then_inc(len_ok, 1)
                g.wait_ge(len_ok, 2 * b + 3)
                apart(g)
                for t in range(T2):
                    ins = g.tensor_scalar(mask0[:, t, :], ki[:], pc[:, 0:1], qn[:, t:t + 1], ALU.is_ge, ALU.mult)
                ins.then_inc(mask_ok, 1)
                if not first:
                    end(b)
                root(nA, 4 * b + 1)
                g.wait_ge(x1_ok, b + 1)
                need(g, hx_out, 16 * b)
                for t in range(T2):
                    ins = g.tensor_tensor(xb[:, t, :], x1[:, t, :], bx[:], ALU.add)
                ins.then_inc(xb_ok, 1)
                root(nA, 4 * b + 2)
                root(nA, 4 * b + 3)
            layer0(0, True)
            with g.Fori(1, B) as b:
                layer0(b, False)
            end(B)
            g.memset(zero, 0.0).then_inc(zeroed, 1)
            g.wait_ge(zeroed, 1)
            g.wait_ge(plan, 14)
            for e in range(E):
                g.indirect_dma_start(rows_d, bass.IndirectOffsetOnAxis(ap=padu[:, e:e + 1], axis=0),
                                     zero, None).then_inc(padded, 16)

            def gather(b):
                need(g, comb, b)
                need(g, yk_in, 64 * b)
                g.tensor_copy(gidx[:], yu_all[:, bass.ds(b, 1), :].rearrange("p b n -> p (b n)")).then_inc(gi, 1)
                g.wait_ge(gi, b + 1)
                apart(g)
                for t in range(T2):
                    for k in range(2):
                        j = 2 * t + k
                        g.indirect_dma_start(yk[k][:, t, :], None, y_d,
                                             bass.IndirectOffsetOnAxis(ap=gidx[:, j:j + 1], axis=0)).then_inc(yk_in, 16)

            def body(b, begin, end, more, expert):
                if expert:
                    ffn_part(b - 2)
                if begin:
                    root(nC, 2 * (b + 1) + 1)
                    if more:
                        gather(b + 2)
                    g.wait_ge(x3_ok, b + 2)
                    for t in range(T2):
                        ins = g.tensor_tensor(xb[:, t, :], x3[:, t, :], bout[:], ALU.add)
                    ins.then_inc(x3b_ok, 1)
                if end:
                    root(nA, b + 4 * B)
                if not isinstance(b, int) or 0 <= b < B:
                    g.wait_ge(x4_ok, b + 1)
                    for t in range(T2):
                        ins = g.tensor_tensor(x4b[:, t, :], x4[:, t, :], bo1[:], ALU.add)
                    ins.then_inc(x4b_ok, 1)
                if begin:
                    root(nC, 2 * (b + 1) + 2)
                if expert:
                    root(nF, b - 1)

            def ffn_part(b):
                g.wait_ge(ex_in, 64 * (b + 1))
                g.wait_ge(x5_ok, b + 1)
                need(g, f_out, b)
                for t in range(T2):
                    ins = g.tensor_tensor(rF[:, t, :], x5[:, t, :], expert_of(b)[3], ALU.add)
                ins.then_inc(f_r, 1)

            for p in range(2):
                g.wait_ge(y_out[p], 16 * (SLOTS // 2))
            g.wait_ge(plan, 17)
            g.wait_ge(wC_in, 16 * 7)
            gather(0)
            body(-1, True, False, True, False)
            body(0, True, False, True, False)
            body(1, True, True, True, False)
            body(2, True, True, True, True)
            with g.Fori(3, B - 2) as b:
                body(b, True, True, True, True)
            body(B - 2, True, True, False, True)
            body(B - 1, False, True, False, True)
            body(B, False, True, False, True)
            body(B + 1, False, False, False, True)

        @block.scalar
        def _(a):
            def exps(src, dst, bias, scale, acc, nm):
                a.wait_ge(smax, nm)
                for t in range(T2):
                    ins = a.activation(dst[:, t, :], src[:, t, :], ACT.Exp, bias=bias[:, t:t + 1], scale=scale,
                                       accum_out=acc(t))
                ins.then_inc(expd, 1)

            def copy_f(b, i):
                FA(b).full(a, b, i)
                ps = FA(b).ps(i)
                if i > 0:
                    ins = a.activation(QT[:, 2 * i - 2:2 * i, :], ps[:], ACT.Copy)
                else:
                    a.activation(KT[:], ps[:, 0, :], ACT.Copy)
                    ins = a.activation(V[:], ps[:, 1, :].rearrange("p (t n) -> p t n", t=2), ACT.Copy)
                FA(b).copy(ins, i)

            def four_heads(W, b, i0, i, OTq):
                if i >= 6 and i % 4 == 2:
                    g = (i - 6) // 4
                    if g >= 2:
                        W.full(a, b, i0 + 2 * g - 3)
                    copy_half(W, b, i0 + 2 * g, OTq[:, g % 2, :])

            def copy_half(W, b, i, dst):
                W.full(a, b, i)
                W.copy(a.activation(dst, W.ps(i)[:, 0, :], ACT.Copy), i)

            def copy_w(W, b, i, dst):
                W.full(a, b, i)
                W.copy(a.activation(dst, W.ps(i)[:], ACT.Copy), i)

            for i in range(5):
                copy_f(0, i)
            copy_w(FA(0), 0, CTXW, cW[:])

            def end(b, i):
                if i == 0:
                    copy_w(FA(b), b, OMT, tT[:])
                if i == 6:
                    copy_w(FA(b), b, N2T, nT[:])

            def end_exp(b):
                a.wait_ge(dl_ok, b)
                a.activation(el[:], dl[:], ACT.Exp).then_inc(el_ok, 1)

            def layer0(b, first, last):
                for i in range(H0 + 3):
                    if i < H0:
                        u = U_A * b + i
                        if i >= 3:
                            a.wait_ge(turned, u - 2)
                        exps(sc_ps[i % 2], probs[i % 3], nmax[:, i % 4], 1.0,
                             lambda t: rs0[:, i % 3, t:t + 1], u + 1)
                    if 2 <= i < H0 + 2:
                        k = i - 2
                        a.wait_ge(turned, U_A * b + (k + 1))
                        a.activation(probsT[k % 2][:], pt_ps[k % 2][:], ACT.Copy).then_inc(turned_sb, 1)
                    if i >= 3:
                        j = i - 3
                        WA.full(a, b, j)
                        WA.copy(a.activation(OT[:, j, :], WA.ps(j)[:, 0, :], ACT.Copy), j)
                    if not first:
                        end(b, i)
                if not first:
                    end_exp(b)
                if not last:
                    copy_f(b + 1, 0)
                    copy_f(b + 1, 1)
                copy_w(WA, b, X1T, tT[:])
                exps(probs[2], probs[2], nmax[:, 0], -1.0, lambda t: rs0[:, 0, t:t + 1], U_A * b + H0 + 1)
                if not last:
                    copy_f(b + 1, 2)
                    copy_f(b + 1, 3)
                WA.full(a, b, N1T)
                for t in range(D2):
                    ins = a.activation(nT[:, t, :], WA.ps(N1T)[:, t, :], ACT.Copy, scale=ln1w[:, t:t + 1])
                WA.copy(ins, N1T)
                WA.full(a, b, QM)
                WA.copy(a.activation(QTm[:], WA.ps(QM)[:], ACT.Copy, scale=1.0 / SQM), QM)
                WA.full(a, b, KM)
                a.activation(KTe[:], WA.ps(KM)[:], ACT.Copy, scale=even[:, 0:1])
                WA.copy(a.activation(KTo[:], WA.ps(KM)[:], ACT.Copy, scale=odd[:, 0:1]), KM)
                for k in range(HM + 3):
                    if k < HM:
                        u = U_A * b + H0 + 1 + k
                        if k >= 3:
                            a.wait_ge(turned, u - 2)
                        exps(sc_ps[k % 2], probs[k % 3], nmax[:, k % 4], 1.0,
                             lambda t: rsm[:, t, k:k + 1], u + 1)
                    four_heads(WA, b, HEADS0, k, OTq0)
                    if not last and k == 0:
                        copy_f(b + 1, 4)
                    if not last and k == 1:
                        copy_w(FA(b + 1), b + 1, CTXW, cW[:])

            a.wait_ge(consts, 14)
            layer0(0, True, False)
            with a.Fori(1, B - 1) as b:
                layer0(b, False, False)
            layer0(B - 1, False, True)
            for i in (0, 6):
                end(B, i)
            end_exp(B)
            a.activation(ah[:], av[:], ACT.Tanh).then_inc(consts, 1)

            def slot_x(s, p, first):
                a.wait_ge(b_x, s + 1)
                if not first:
                    a.wait_ge(b_h, s - 1)
                a.activation(xgT[p], bank[p][:, 0, :].rearrange("p (t n) -> p t n", t=2), ACT.Copy).then_inc(b_xs, 1)

            def slot_gate(s, p, first):
                a.wait_ge(b_h, s + 1)
                if not first:
                    a.wait_ge(b_hid, s - 1)
                a.activation(gate[p], bank[2 + 2 * p][:].rearrange("p a b -> p (a b)"), ACT.Silu).then_inc(b_gate, 1)

            def slot_out(s, p, first):
                a.wait_ge(b_t, s + 1)
                if not first:
                    need(a, b_y, s - 1)
                a.activation(hidT[p], bank[6][:].rearrange("p a (c n) -> p (a c) n", n=P), ACT.Copy).then_inc(b_ts, 1)

            def slots(t, first=False, last=False):
                for p in range(2):
                    s = 2 * t + p
                    slot_gate(s, p, first)
                    if not (last and p == 1):
                        slot_x(s + 1, 1 - p, first and p == 0)
                    slot_out(s, p, first)

            slot_x(0, 0, True)
            slots(0, first=True)
            slots(1)
            with a.Fori(2, SLOTS // 2 - 1) as t:
                slots(t)
            slots(SLOTS // 2 - 1, last=True)

            def ffn_up(b, i):
                FC.full(a, b, UP[i])
                if i == 0:
                    a.wait_ge(ex_in, 64 * (b - 1))
                for j in range(2):
                    f = 2 * i + j
                    ins = a.activation(hF[:, f, :], FC.ps(UP[i])[:, j, :], ACT.Relu, bias=expert_of(b - 2)[2][:, f:f + 1])
                FC.copy(ins, UP[i])

            def keys(b):
                FC.full(a, b, K1)
                for t in range(D2):
                    a.activation(kFe[:, t, :], FC.ps(K1)[:, t, :], ACT.Identity, bias=bke[:, t:t + 1],
                                 scale=even[:, 0:1])
                    ins = a.activation(kFo[:, t, :], FC.ps(K1)[:, t, :], ACT.Identity, bias=bko[:, t:t + 1],
                                       scale=odd[:, 0:1])
                FC.copy(ins, K1)

            def between(b, i, begin, end, expert):
                if expert and i in UP_AT:
                    ffn_up(b, UP_AT.index(i))
                if end:
                    if i == 0:
                        copy_w(FC, b, O1T, oT)
                    if i == 6:
                        FC.full(a, b, X5T)
                        for t in range(D2):
                            ins = a.activation(x5T[:, t, :], FC.ps(X5T)[:, t, :], ACT.Copy, accum_out=msum[:, t:t + 1])
                        FC.copy(ins, X5T)
                if begin:
                    if i == 3:
                        FC.full(a, b, X3T)
                        for t in range(D2):
                            ins = a.activation(x3T[:, t, :], FC.ps(X3T)[:, t, :], ACT.Copy, scale=bvec[:, t:t + 1])
                        FC.copy(ins, X3T)
                    if i == 9:
                        copy_w(FC, b, X4T, x4T[:])
                    if i == 16:
                        keys(b)
                    if i == 17:
                        FC.full(a, b, Q1)
                        for t in range(D2):
                            ins = a.activation(qF[:, t, :], FC.ps(Q1)[:, t, :], ACT.Identity, bias=bq1[:, t:t + 1])
                        FC.copy(ins, Q1)

            def body(b, begin, heads, end, expert):
                for i in range(HM + 3):
                    if heads and i < HM:
                        u = U_C * b + (U0 + i)
                        exps(probs[i % 3], probs[i % 3], nmax[:, i % 4], -1.0, lambda t: rsm[:, t, i:i + 1], u + 1)
                    if heads:
                        four_heads(WC, b, HEADS1, i, OTq1)
                    between(b, i, begin, end, expert)

            a.wait_ge(consts, 16)
            keys(-1)
            for i in (3, 9, 17):
                between(-1, i, True, False, False)
            body(0, True, True, False, False)
            body(1, True, True, True, False)
            with a.Fori(2, B - 1) as b:
                body(b, True, True, True, True)
            body(B - 1, False, True, True, True)
            body(B, False, False, True, True)
            body(B + 1, False, False, False, True)

        @block.tensor
        def _(pe):
            def mm(o, l, rh, k, n):
                return pe.matmul(o, l, rh, start=(k == 0), stop=(k == n - 1))

            def proj(b, i):
                FA(b).free(pe, b, i)
                ps = FA(b).ps(i)
                if i > 0:
                    for j in range(2):
                        hh = 2 * i - 2 + j
                        for t in range(D2):
                            ins = mm(ps[:, j, :], wq0[:, t, hh * P:(hh + 1) * P], xT[:, t, :], t, D2)
                else:
                    for t in range(D2):
                        mm(ps[:, 0, :], wk0[:, t, :], xT[:, t, :], t, D2)
                    for m in range(T2):
                        for t in range(D2):
                            ins = mm(ps[:, 1, m * P:(m + 1) * P], xT[:, t, m * P:(m + 1) * P], wv0[:, t, :], t, D2)
                FA(b).fill(ins, i)

            def turn(W, b, i, src):
                W.free(pe, b, i)
                for t in range(T2):
                    for d in range(D2):
                        ins = pe.transpose(W.ps(i)[:, d, t * P:(t + 1) * P], src[:, t, d * P:(d + 1) * P], ident[:])
                W.fill(ins, i)

            def lin(W, b, i, lT, rh, n=D):
                W.free(pe, b, i)
                for t in range(T2):
                    for d in range(D2):
                        ins = mm(W.ps(i)[:, t, 0:n], lT[:, d, t * P:(t + 1) * P], rh[:, d, :], d, D2)
                W.fill(ins, i)

            def linT(W, b, i, w, xt):
                W.free(pe, b, i)
                for o in range(D2):
                    for d in range(D2):
                        ins = mm(W.ps(i)[:, o, :], w[:, d, o * P:(o + 1) * P], xt[:, d, :], d, D2)
                W.fill(ins, i)

            def turn_probs(src, k, u, ringed):
                if ringed:
                    pe.wait_ge(turned_sb, u - 1)
                for t in range(T2):
                    for m in range(T2):
                        ins = pe.transpose(pt_ps[k % 2][:, m, t * P:(t + 1) * P], src[:, t, m * P:(m + 1) * P], ident[:])
                ins.then_inc(turned, 1)

            def heads(W, b, u_of, q, ke, ko, ring, OTq, i0, between, values=None):
                for i in range(HM + 5):
                    if i < HM:
                        if i >= 2:
                            pe.wait_ge(expd if W is WA else smax, u_of(i) - 1)
                        j, p0 = i // 8, 32 * ((i % 8) // 2)
                        kk = (ke, ko)[i % 2]
                        for t in range(T2):
                            ins = mm(sc_ps[i % 2][:, t, :], q[p0:p0 + 32, j, t * P:(t + 1) * P], kk[p0:p0 + 32, j, :], 0, 1)
                        ins.then_inc(scores, 1)
                    if 2 <= i < HM + 2:
                        k = i - 2
                        pe.wait_ge(expd, u_of(k) + 1)
                        turn_probs(probs[k % 3], k, u_of(k), k >= 2)
                    if i >= 6 and i % 4 == 2:
                        g = (i - 6) // 4
                        if g == 0 and values:
                            values()
                        pe.wait_ge(turned_sb, u_of(4 * g + 3) + 1)
                        W.free(pe, b, i0 + 2 * g)
                        for m in range(T2):
                            for j in range(4):
                                k = 4 * g + j
                                ins = mm(W.ps(i0 + 2 * g)[32 * j:32 * j + 32, 0, :],
                                         VmP[:, m, k * HD:k * HD + 32], ring[k % len(ring)][:, m, :], m, T2)
                        W.fill(ins, i0 + 2 * g)
                    if i >= 8 and i % 4 == 0:
                        g = (i - 8) // 4
                        W.out(pe, b, i0 + 2 * g)
                        W.free(pe, b, i0 + 2 * g + 1)
                        for t in range(T2):
                            ins = pe.transpose(W.ps(i0 + 2 * g + 1)[:, t, 0:P], OTq[:, g % 2, t * P:(t + 1) * P], ident[:])
                        W.fill(ins, i0 + 2 * g + 1)
                    between(i)

            pe.wait_ge(consts, 12)
            pe.wait_ge(w0_in, 16 * 3)
            pe.wait_ge(xT_in, 16)
            for i in range(5):
                proj(0, i)
            pe.wait_ge(wA_in, 16 * 7)
            pe.wait_ge(cT_in, 16)
            lin(FA(0), 0, CTXW, cT, wx)

            def end(b, i):
                W = FA(b)
                if i == 0:
                    WA.out(pe, b - 1, HEADS0 + 7)
                    turn(W, b, OMT, On)
                if i == 2:
                    W.out(pe, b, OMT)
                    lin(W, b, PROJ, tT, wom)
                if i == 6:
                    pe.wait_ge(n2_ok, b)
                    turn(W, b, N2T, n2)
                if i == 8:
                    W.out(pe, b, N2T)
                    lin(W, b, LOGIT, nT, wg, E)

            def end_ranks(b):
                W = FA(b)
                pe.wait_ge(cnt_ok, b)
                W.free(pe, b, RANK)
                rk = W.ps(RANK)[:, 0, :]
                mm(rk[:, 0:E], upper[:], cnt[:, 0, :], 0, 1)
                mm(rk[:, E:2 * E], upper[:], cnt[:, 1, :], 0, 2)
                mm(rk[:, E:2 * E], ones[:], cnt[:, 0, :], 1, 2)
                mm(rk[:, 2 * E:3 * E], ones[:], cnt[:, 0, :], 0, 2)
                W.fill(mm(rk[:, 2 * E:3 * E], ones[:], cnt[:, 1, :], 1, 2), RANK)

            def layer0(b, first, last):
                def u(k):
                    return U_A * b + k
                FA(b).out(pe, b, 0)
                for i in range(H0 + 3):
                    if i < H0:
                        if i % 2 == 0:
                            FA(b).out(pe, b, 1 + i // 2)
                        if i >= 2:
                            pe.wait_ge(expd, u(i) - 1)
                        for t in range(T2):
                            ins = mm(sc_ps[i % 2][:, t, :], QT[:, i, t * P:(t + 1) * P], KT[:], 0, 1)
                        ins.then_inc(scores, 1)
                    if 2 <= i < H0 + 2:
                        k = i - 2
                        pe.wait_ge(normed, H0 * b + k + 1)
                        turn_probs(probs[k % 3], k, u(k), k >= 2)
                    if i >= 3:
                        k = i - 3
                        pe.wait_ge(turned_sb, u(k) + 1)
                        WA.free(pe, b, k)
                        for m in range(T2):
                            ins = mm(WA.ps(k)[:, 0, :], V[:, m, :], probsT[k % 2][:, m, :], m, T2)
                        WA.fill(ins, k)
                    if not first:
                        end(b, i)
                WA.out(pe, b, H0 - 2)
                WA.out(pe, b, H0 - 1)
                for t in range(T2):
                    for k in range(H0):
                        ins = mm(WA.ps(ATTN0)[:, t, :], OT[:, k, t * P:(t + 1) * P], wo0[:, k, :], k, H0)
                    if t == 0 and not first:
                        end_ranks(b)
                WA.fill(ins, ATTN0)
                if not last:
                    pe.wait_ge(xT_in, 16 * (b + 2))
                    proj(b + 1, 0)
                    proj(b + 1, 1)
                pe.wait_ge(x1_ok, b + 1)
                turn(WA, b, X1T, x1)
                WA.out(pe, b, X1T)
                for t in range(T2):
                    for d in range(D2):
                        ins = mm(sc_ps[0][:, t, :], tT[:, d, t * P:(t + 1) * P], cT[:, d, :], d, D2)
                ins.then_inc(scores, 1)
                if not last:
                    proj(b + 1, 2)
                pe.wait_ge(expd, u(H0) + 1)
                turn_probs(probs[2], 0, 0, False)
                pe.wait_ge(turned_sb, u(H0) + 1)
                lin(WA, b, XATT, probsT[0], cW)
                if not last:
                    proj(b + 1, 3)
                pe.wait_ge(n1_ok, b + 1)
                turn(WA, b, N1T, r)
                WA.out(pe, b, N1T)
                linT(WA, b, QM, wqm, nT)
                linT(WA, b, KM, wkm, nT)
                lin(WA, b, VM, nT, wvm)
                WA.out(pe, b, QM)
                WA.out(pe, b, KM)

                def between(i):
                    if not last and i == 0:
                        proj(b + 1, 4)
                    if not last and i == 1:
                        pe.wait_ge(cT_in, 16 * (b + 2))
                        lin(FA(b + 1), b + 1, CTXW, cT, wx)

                heads(WA, b, lambda k: U_A * b + (H0 + 1 + k), QTm, KTe, KTo, ring0, OTq0, HEADS0, between,
                      lambda: WA.out(pe, b, VM))
            layer0(0, True, False)
            with pe.Fori(1, B - 1) as b:
                layer0(b, False, False)
            layer0(B - 1, False, True)
            for i in (0, 2, 6, 8):
                end(B, i)
            end_ranks(B)

            def slot_x(t, p):
                pe.wait_ge(xg_in[p], 16 * (t + 1))
                for d in range(D2):
                    ins = pe.transpose(bank[p][:, 0, d * P:(d + 1) * P], xg[p][:, d * P:(d + 1) * P], ident[:])
                ins.then_inc(b_x, 1)

            def slot_up(s, p, first):
                e = pe.value_load(slot_e[0:1, bass.ds(s, 1)], min_val=0, max_val=E - 1)
                pe.wait_ge(b_xs, s + 1)
                if not first:
                    pe.wait_ge(b_hid, s - 1)
                for w, o in ((w1, 2), (w3, 3)):
                    for d in range(D2):
                        ins = mm(bank[o + 2 * p][:].rearrange("p a b -> p (a b)"), xgT[p][:, d, :],
                                 w[:, bass.ds(e, 1), d, :].rearrange("p e n -> p (e n)"), d, D2)
                ins.then_inc(b_h, 1)
                return e

            def slot_t(s, p, first):
                pe.wait_ge(b_hid, s + 1)
                if not first:
                    pe.wait_ge(b_ts, s)
                for f in range(FT0):
                    ins = pe.transpose(bank[6][:].rearrange("p a b -> p (a b)")[:, f * P:(f + 1) * P],
                                       hid[p][:, f * P:(f + 1) * P], ident[:])
                ins.then_inc(b_t, 1)

            def slot_down(s, p, first):
                e = pe.value_load(slot_e[0:1, bass.ds(s, 1)], min_val=0, max_val=E - 1)
                pe.wait_ge(b_ts, s + 1)
                if not first:
                    pe.wait_ge(b_ys, s)
                for f in range(FT0):
                    ins = mm(bank[7][:, 0, :], hidT[p][:, f, :], w2[:, bass.ds(e, 1), f, :].rearrange("p e n -> p (e n)"),
                             f, FT0)
                ins.then_inc(b_y, 1)

            pe.wait_ge(plan, 14)
            pe.wait_ge(wM_in, 48 * B)

            def slots(t, first=False, last=False):
                for p in range(2):
                    s = 2 * t + p
                    slot_up(s, p, first)
                    if not (last and p == 1):
                        slot_x(t + p, 1 - p)
                    if not (first and p == 0):
                        slot_down(s - 1, 1 - p, first)
                    slot_t(s, p, first and p == 0)

            slot_x(0, 0)
            slots(0, first=True)
            slots(1)
            with pe.Fori(2, SLOTS // 2 - 1) as t:
                slots(t)
            slots(SLOTS // 2 - 1, last=True)
            slot_down(SLOTS - 1, 1, False)

            def ffn_up(b, i):
                FC.free(pe, b, UP[i])
                for j in range(2):
                    f = 2 * i + j
                    for d in range(D2):
                        ins = mm(FC.ps(UP[i])[:, j, :], expert_of(b - 2)[0][:, d, f * P:(f + 1) * P], x5T[:, d, :], d, D2)
                FC.fill(ins, UP[i])

            def ffn_down(b, t):
                if t == 0:
                    FC.out(pe, b, UP[3])
                    FC.free(pe, b, DOWN)
                for f in range(FT1):
                    ins = mm(FC.ps(DOWN)[:, t, :], hF[:, f, t * P:(t + 1) * P], expert_of(b - 2)[1][:, f, :], f, FT1)
                if t == T2 - 1:
                    FC.fill(ins, DOWN)

            def keys(b):
                pe.wait_ge(cT_in, 16 * B + 16 * (b + 2))
                linT(FC, b, K1, wk1, cT)

            def body(b, begin, with_heads, end, expert, steps=range(HM + 5)):
                def between(i):
                    if expert and i in UP_AT:
                        if i == 0:
                            pe.wait_ge(ex_in, 64 * (b - 1))
                        ffn_up(b, UP_AT.index(i))
                    if expert and i in DOWN_AT:
                        ffn_down(b, DOWN_AT.index(i))
                    if end:
                        if i == 0:
                            WC.out(pe, b - 1, HEADS1 + 7)
                            turn(FC, b, O1T, On)
                        if i == 2:
                            FC.out(pe, b, O1T)
                            lin(FC, b, PROJ1, oT, wo1)
                        if i == 6:
                            pe.wait_ge(x5_ok, b)
                            turn(FC, b, X5T, x5)
                        if i == 8:
                            FC.out(pe, b, X5T)
                            FC.free(pe, b, ROUTE)
                            for d in range(D2):
                                ins = mm(FC.ps(ROUTE)[0:1, 0, 0:E], msum[:, d:d + 1], wr[:, d, :], d, D2)
                            FC.fill(ins, ROUTE)
                    if begin:
                        if i == 3:
                            pe.wait_ge(x3_ok, b + 2)
                            turn(FC, b, X3T, x3)
                        if i == 5:
                            pe.wait_ge(scan_ok, b + 2)
                            lin(FC, b, SSM, yT, wout)
                        if i == 9:
                            pe.wait_ge(x4_ok, b + 2)
                            turn(FC, b, X4T, x4)
                        if i == 16:
                            keys(b)
                        if i == 17:
                            FC.out(pe, b, X4T)
                            linT(FC, b, Q1, wq1, x4T)
                    if begin and i == 20:
                        lin(FC, b, V1, cT, wv1)

                if with_heads:
                    FC.out(pe, b - 1, K1)
                    FC.out(pe, b - 1, Q1)
                    heads(WC, b, lambda k: U_C * b + (U0 + k), qF, kFe, kFo, ring1, OTq1, HEADS1, between,
                          lambda: FC.out(pe, b - 1, V1))
                else:
                    for i in steps:
                        between(i)

            pe.wait_ge(wC_in, 16 * 7)
            keys(-1)
            lin(FC, -1, V1, cT, wv1)
            body(-1, True, False, False, False, (3, 5, 9, 17))
            body(0, True, True, False, False)
            body(1, True, True, True, False)
            with pe.Fori(2, B - 1) as b:
                body(b, True, True, True, True)
            body(B - 1, False, True, True, True)
            body(B, False, False, True, True)
            body(B + 1, False, False, False, True)

        @block.vector
        def _(v):
            v.memset(VmP[:, :, D:D + HD], 0.0)
            v.wait_ge(consts, 12)
            idv = ident[:].rearrange("p (g two n) -> p g two n", two=2, n=HD)
            v.tensor_reduce(even[:], idv[:, :, 0, :], AX.XY, ALU.add).then_inc(consts, 1)
            v.tensor_reduce(odd[:], idv[:, :, 1, :], AX.XY, ALU.add).then_inc(consts, 1)
            v.wait_ge(consts, 14)
            v.wait_ge(const_in, 16 * 11)
            v.tensor_scalar(bke[:], bk1[:], even[:, 0:1], None, ALU.mult)
            v.tensor_scalar(bko[:], bk1[:], odd[:, 0:1], None, ALU.mult).then_inc(consts, 1)

            def finish_norm(n, k, src, dst, done, mean=True):
                v.wait_ge(n.root, k + 1)
                for t in range(T2):
                    if mean:
                        ins = v.tensor_scalar(dst[:, t, :], src[:, t, :], n.mv[:, t, 0:1], n.rstd[:, t:t + 1],
                                              ALU.subtract, ALU.mult)
                    else:
                        ins = v.tensor_scalar(dst[:, t, :], src[:, t, :], n.rstd[:, t:t + 1], None, ALU.mult)
                ins.then_inc(done, 1)

            def stats(n, k, ks, src):
                for t in range(T2):
                    ins = v.bn_stats(n.st[:, t, :], src[:, t, :])
                ins.then_inc(n.stats, 1)
                v.wait_ge(n.stats, k + 1)
                apart(v)
                for t in range(T2):
                    ins = v.bn_aggr(n.mv[:, t, :], n.st[:, t, :])
                ins.then_inc(n.mean, 1)
                v.wait_ge(n.mean, ks + 1)
                v.tensor_scalar(n.ve[:], n.mv[:, :, 1], EPS, None, ALU.add).then_inc(n.var, 1)

            def squares(n, k, src, junk):
                for t in range(T2):
                    ins = v.tensor_tensor_reduce(junk[:, t, :], src[:, t, :], src[:, t, :], 1.0, 0.0, ALU.mult, ALU.add,
                                                 n.st[:, t, 0:1])
                ins.then_inc(n.stats, 1)
                v.wait_ge(n.stats, k + 1)
                v.tensor_scalar(n.ve[:], n.st[:, :, 0], 1.0 / D, EPS, ALU.mult, ALU.add).then_inc(n.var, 1)

            def max_of(u, k):
                v.wait_ge(scores, u + 1)
                v.tensor_reduce(nmax[:, k % 4, :], sc_ps[k % 2][:], AX.X, ALU.max, negate=True).then_inc(smax, 1)

            def masked_max(u, k, mask, scale, src, dst):
                v.wait_ge(scores, u + 1)
                apart(v)
                for t in range(T2):
                    ins = v.tensor_tensor_reduce(dst[:, t, :], src[:, t, :], mask(t), -scale, BIG, ALU.add, ALU.min,
                                                 nmax[:, k % 4, t:t + 1])
                ins.then_inc(smax, 1)

            def copy_turned(u, k, used=None, ring=None):
                v.wait_ge(turned, u + 1)
                if used:
                    used()
                dst = probsT[k % 2][:] if ring is None else ring[k % len(ring)]
                v.tensor_copy(dst, pt_ps[k % 2][:]).then_inc(turned_sb, 1)

            def copy_ring(W, b, i0, u, k, ring):
                n = len(ring)
                copy_turned(u, k, (lambda: W.full(v, b, i0 + 2 * ((k - n) // 4))) if k >= n else None, ring)

            def head_out(W, b, i0, g, n, ue):
                v.wait_ge(expd, ue)
                hs = slice(4 * g, 4 * g + 4)
                v.reciprocal(rrm[:, :, hs], rsm[:, :, hs]).then_inc(inv_m, 1)
                v.wait_ge(inv_m, 4 * n + (g + 1))
                i = i0 + 2 * g + 1
                W.full(v, b, i)
                for t in range(T2):
                    ins = v.tensor_tensor(On[:, t, 64 * g:64 * g + 64].rearrange("p (h n) -> p h n", n=HD),
                                          W.ps(i)[:, t, 0:P].rearrange("p (h n) -> p h n", n=32)[:, :, 0:HD],
                                          rrm[:, t, hs].unsqueeze(2).broadcast_to([P, 4, HD]), ALU.mult)
                W.copy(ins, i)

            RT = 8

            def end_sum(b):
                W, c = FA(b), b - 1
                W.full(v, b, PROJ)
                ins = v.tensor_tensor(h[:], W.ps(PROJ)[:], x2[:], ALU.add)
                W.copy(ins, PROJ)
                W.out(v, b, PROJ)
                need(v, scattered, 64 * c)
                squares(nA, 4 * c + 3, h, n2)

            def end_norm(b):
                c = b - 1
                v.wait_ge(nA.root, 4 * c + 4)
                for t in range(T2):
                    ins = v.scalar_tensor_tensor(n2[:, t, :], h[:, t, :], nA.rstd[:, t:t + 1], ln2w[:], ALU.mult, ALU.mult)
                ins.then_inc(n2_ok, 1)

            def end_choice(b):
                W, c = FA(b), b - 1
                W.full(v, b, LOGIT)
                W.copy(v.tensor_copy(lg[:], W.ps(LOGIT)[:, :, 0:E]), LOGIT)
                W.out(v, b, LOGIT)
                apart(v)
                for t in range(T2):
                    ins = v.max(mx[:, t, :], lg[:, t, :])
                ins.then_inc(rt, 1)
                v.wait_ge(rt, RT * c + 1)
                apart(v)
                for t in range(T2):
                    ins = v.max_index(mi[:, t, :], mx[:, t, :], lg[:, t, :])
                ins.then_inc(rt, 1)
                v.tensor_tensor(dl[:], mx[:, :, 1], mx[:, :, 0], ALU.subtract).then_inc(dl_ok, 1)
                v.wait_ge(rt, RT * c + 2)
                v.tensor_copy(mf[:], mi[:, :, 0:2]).then_inc(rt, 1)
                v.wait_ge(rt, RT * c + 3)
                for t in range(T2):
                    for k in range(2):
                        ins = v.tensor_scalar(sel[:, t, k, :], ei[:], mf[:, t, k:k + 1], None, ALU.is_equal)
                ins.then_inc(rt, 1)
                v.wait_ge(rt, RT * c + 4)
                v.tensor_tensor(cnt[:], sel[:, :, 0, :], sel[:, :, 1, :], ALU.add).then_inc(cnt_ok, 1)
                v.tensor_copy(sel_all[:, bass.ds(c, 1), :].rearrange("p b n -> p (b n)"),
                              sel[:].rearrange("p t k e -> p (t k e)"))

            def end_rows(b):
                W, c = FA(b), b - 1
                v.wait_ge(el_ok, c + 1)
                v.tensor_scalar(e1[:], el[:], 1.0, None, ALU.add).then_inc(rt, 1)
                v.wait_ge(rt, RT * c + 5)
                v.reciprocal(pk[:, :, 0], e1[:]).then_inc(rt, 1)
                v.wait_ge(rt, RT * c + 6)
                v.tensor_tensor(pk[:, :, 1], pk[:, :, 0], el[:], ALU.mult).then_inc(rt, 1)
                W.full(v, b, RANK)
                v.tensor_tensor(rank[:], W.ps(RANK)[:, 0, 0:2 * E].rearrange("p (t e) -> p t e", t=2),
                                run[:].unsqueeze(1).broadcast_to([P, T2, E]), ALU.add).then_inc(route_pos, 1)
                v.wait_ge(route_pos, 3 * c + 1)
                W.copy(v.tensor_tensor(run[:], W.ps(RANK)[:, 0, 2 * E:3 * E], run[:], ALU.add), RANK)
                W.out(v, b, RANK)
                v.wait_ge(rt, RT * c + 7)
                v.tensor_copy(pk_all[:, bass.ds(c, 1), :].rearrange("p b n -> p (b n)"), pk[:].rearrange("p t k -> p (t k)"))
                v.tensor_copy(rank_all[:, bass.ds(c, 1), :].rearrange("p b n -> p (b n)"), rank[:].rearrange("p t e -> p (t e)"))
                v.tensor_tensor(rowat[:], rank[:], ebase[:].unsqueeze(1).broadcast_to([P, T2, E]), ALU.add).then_inc(rt, 1)
                v.wait_ge(rt, RT * c + 8)
                for k in range(2):
                    ins = v.tensor_tensor(rowsel[:, :, k, :], sel[:, :, k, :], rowat[:], ALU.mult)
                ins.then_inc(route_pos, 1)
                v.wait_ge(route_pos, 3 * c + 2)
                v.tensor_reduce(posf[:], rowsel[:].rearrange("p t k e -> p (t k) e"), AX.X, ALU.add).then_inc(route_pos, 1)
                v.wait_ge(route_pos, 3 * c + 3)
                v.tensor_copy(posu[:], posf[:]).then_inc(pos_ok, 1)

            def layer0(b, first):
                def u(k):
                    return U_A * b + k
                for i in range(H0 + 1):
                    if i < H0:
                        max_of(u(i), i)
                    if 1 <= i <= H0:
                        k = i - 1
                        v.wait_ge(expd, u(k) + 1)
                        v.reciprocal(rr0[:, k % 3, :], rs0[:, k % 3, :]).then_inc(sums_inv, 1)
                        v.wait_ge(sums_inv, (H0 + 1) * b + k + 1)
                        for t in range(T2):
                            ins = v.tensor_scalar(probs[k % 3][:, t, :], probs[k % 3][:, t, :],
                                                  rr0[:, k % 3, t:t + 1], None, ALU.mult)
                        ins.then_inc(normed, 1)
                    if not first and i == 3:
                        end_sum(b)
                    if not first and i == 4:
                        end_norm(b)
                if not first:
                    end_choice(b)
                    end_rows(b)
                v.wait_ge(x_in, 16 * (b + 1))
                WA.full(v, b, ATTN0)
                ins = v.tensor_tensor(r[:], WA.ps(ATTN0)[:], x[:], ALU.add)
                WA.copy(ins, ATTN0)
                WA.out(v, b, ATTN0)
                stats(nA, 4 * b, 2 * b, r)
                finish_norm(nA, 4 * b, r, x1, x1_ok)
                v.wait_ge(mask_ok, b + 1)
                masked_max(u(H0), 0, lambda t: mask0[:, t, :], 1.0 / SQ0, sc_ps[0], probs[2])
                copy_turned(u(H0), 0)
                v.wait_ge(expd, u(H0) + 1)
                v.reciprocal(rr0[:, 0, :], rs0[:, 0, :]).then_inc(sums_inv, 1)
                v.wait_ge(sums_inv, (H0 + 1) * b + H0 + 1)
                v.wait_ge(xb_ok, b + 1)
                WA.full(v, b, XATT)
                for t in range(T2):
                    ins = v.scalar_tensor_tensor(r[:, t, :], WA.ps(XATT)[:, t, :], rr0[:, 0, t:t + 1], xb[:, t, :],
                                                 ALU.mult, ALU.add)
                WA.copy(ins, XATT)
                WA.out(v, b, XATT)
                stats(nA, 4 * b + 1, 2 * b + 1, r)
                finish_norm(nA, 4 * b + 1, r, x2, x2_ok)
                v.wait_ge(x2_ok, b + 1)
                squares(nA, 4 * b + 2, x2, r)
                finish_norm(nA, 4 * b + 2, x2, r, n1_ok, mean=False)
                WA.full(v, b, VM)
                WA.copy(v.tensor_copy(Vm, WA.ps(VM)[:]), VM)
                for i in range(HM + 2):
                    if i < HM:
                        max_of(u(H0 + 1 + i), i)
                    if i >= 2:
                        k = i - 2
                        copy_ring(WA, b, HEADS0, u(H0 + 1 + k), k, ring0)
                    if i >= 9 and i % 4 == 1:
                        g = (i - 9) // 4
                        head_out(WA, b, HEADS0, g, b, u(H0 + 1 + 4 * g + 3) + 1)
                head_out(WA, b, HEADS0, HM // 4 - 1, b, u(U_A))
            layer0(0, True)
            layer0(1, False)
            with v.Fori(2, B) as b:
                layer0(b, False)
            end_sum(B)
            end_norm(B)
            end_choice(B)
            end_rows(B)

            step = [0]

            def link(ins):
                step[0] += 1
                ins.then_inc(plan, 1)
                v.wait_ge(plan, step[0])

            link(v.tensor_tensor(tcmp[:], run[:].unsqueeze(2).broadcast_to([P, E, TOK // P]),
                                 thr[:].unsqueeze(1).broadcast_to([P, E, TOK // P]), ALU.is_gt))
            link(v.tensor_reduce(tiles[:], tcmp[:], AX.X, ALU.add))
            link(v.tensor_tensor_scan(tend[:], ones[:, 0:E], tiles[:], 0.0, ALU.mult, ALU.add))
            link(v.tensor_tensor(tbeg[:], tend[:], tiles[:], ALU.subtract))
            link(v.tensor_tensor(padf[:], run[:], ebase[:], ALU.add))
            link(v.tensor_scalar(padf[:], padf[:], pidx[:, 0:1], None, ALU.add))
            link(v.tensor_copy(padu[:], padf[:]))
            sl = si[:].unsqueeze(2).broadcast_to([P, SLOTS, E])
            v.tensor_tensor(inA[:], tbeg[:].unsqueeze(1).broadcast_to([P, SLOTS, E]), sl, ALU.is_le)
            link(v.tensor_tensor(inB[:], tend[:].unsqueeze(1).broadcast_to([P, SLOTS, E]), sl, ALU.is_gt))
            link(v.tensor_tensor(inA[:], inA[:], inB[:], ALU.mult))
            v.scalar_tensor_tensor(rbase[:], tbeg[:], -float(P), ebase[:], ALU.mult, ALU.add)
            link(v.tensor_tensor(inB[:], inA[:], ei[:].unsqueeze(1).broadcast_to([P, SLOTS, E]), ALU.mult))
            link(v.tensor_reduce(slf[:, 0, :], inB[:], AX.X, ALU.add))
            link(v.scalar_tensor_tensor(inB[:], sl, float(P), rbase[:].unsqueeze(1).broadcast_to([P, SLOTS, E]), ALU.mult, ALU.add))
            link(v.tensor_tensor(inB[:], inB[:], inA[:], ALU.mult))
            v.tensor_copy(slot_e[:], slf[:, 0, :])
            v.tensor_reduce(slf[:, 1, :], inB[:], AX.X, ALU.add).then_inc(route_pos, 1)
            v.wait_ge(route_pos, 3 * B + 1)
            link(v.tensor_copy(slot_r[:], slf[:, 1, :]))
            assert step[0] == 14
            v.tensor_scalar(ybase[:], tbeg[:], float(P), None, ALU.mult).then_inc(route_pos, 1)
            v.wait_ge(route_pos, 3 * B + 2)
            ra = rank_all[:].rearrange("p b (t e) -> p (b t) e", e=E)
            link(v.tensor_tensor(ra, ra, ybase[:].unsqueeze(1).broadcast_to([P, B * T2, E]), ALU.add))
            sa = sel_all[:].rearrange("p b (t k e) -> p (b t) k e", k=2, e=E)
            for k in range(2):
                ins = v.tensor_tensor(ymul[:, :, k, :], sa[:, :, k, :], ra, ALU.mult)
            link(ins)
            v.tensor_reduce(yf[:], ymul[:].rearrange("p t k e -> p (t k) e"), AX.X, ALU.add).then_inc(route_pos, 1)
            v.wait_ge(route_pos, 3 * B + 3)
            link(v.tensor_copy(yu_all[:].rearrange("p b n -> p (b n)"), yf[:]))

            def slot(s, p, first):
                v.wait_ge(b_gate, s + 1)
                if not first:
                    v.wait_ge(b_t, s - 1)
                v.tensor_tensor(hid[p], bank[3 + 2 * p][:].rearrange("p a b -> p (a b)"), gate[p], ALU.mult).then_inc(b_hid, 1)

            def slot_y(t, p, first):
                s = 2 * t + p
                v.wait_ge(b_y, s + 1)
                if not first:
                    need(v, y_out[p], 16 * t)
                v.tensor_copy(yo[p], bank[7][:, 0, :]).then_inc(b_ys, 1)

            slot(0, 0, True)
            slot(1, 1, True)
            slot_y(0, 0, True)

            def slots(t):
                slot(2 * t, 0, False)
                slot_y(t - 1, 1, False)
                slot(2 * t + 1, 1, False)
                slot_y(t, 0, False)

            slots(1)
            with v.Fori(2, SLOTS // 2) as t:
                slots(t)
            slot_y(SLOTS // 2 - 1, 1, False)

            def combine(b):
                v.wait_ge(yk_in, 64 * (b + 1))
                v.wait_ge(hx_in, 16 * (b + 1))
                v.tensor_copy(pk[:].rearrange("p t k -> p (t k)"), pk_all[:, bass.ds(b, 1), :].rearrange("p b n -> p (b n)")).then_inc(comb1, 1)
                v.wait_ge(comb1, 2 * b + 1)
                for t in range(T2):
                    ins = v.scalar_tensor_tensor(r[:, t, :], yk[0][:, t, :], pk[:, t, 0:1], x[:, t, :], ALU.mult, ALU.add)
                ins.then_inc(comb1, 1)
                v.wait_ge(comb1, 2 * b + 2)
                for t in range(T2):
                    ins = v.scalar_tensor_tensor(r[:, t, :], yk[1][:, t, :], pk[:, t, 1:2], r[:, t, :], ALU.mult, ALU.add)
                ins.then_inc(comb, 1)
                v.wait_ge(comb, b + 1)
                stats(nC, 2 * b, 2 * b, r)

            def finish_expert(b):
                need(v, out_done, 16 * b)
                finish_norm(nF, b, rF, xF, f_out)

            def mask_of(b):
                v.wait_ge(smax, U_C * b + U0)
                v.wait_ge(mi_in, 16 * (b + 1))
                v.tensor_scalar(mask1[:], mask_i[:], 0.0, NEG1, ALU.is_equal, ALU.mult).then_inc(mask1_ok, 1)

            def between(b, i, begin, end, expert):
                if i == 0 and begin:
                    combine(b + 1)
                if expert and i == DOWN_AT[1] + 1:
                    FC.full(v, b, DOWN)
                    v.wait_ge(f_r, b - 1)
                    FC.copy(v.tensor_tensor(rF[:], FC.ps(DOWN)[:], rF[:], ALU.add), DOWN)
                    FC.out(v, b, DOWN)
                    stats(nF, b - 2, b - 2, rF)
                if expert and i == DOWN_AT[1] + 2:
                    finish_expert(b - 2)
                if i == 1 and begin:
                    finish_norm(nC, 2 * (b + 1), r, x3, x3_ok)
                if i == 3 and end:
                    v.wait_ge(x4b_ok, b)
                    FC.full(v, b, PROJ1)
                    FC.copy(v.tensor_tensor(r5, FC.ps(PROJ1)[:], x4b, ALU.add), PROJ1)
                    FC.out(v, b, PROJ1)
                    stats(nA, b + (4 * B - 1), b + (2 * B - 1), r5)
                if i == 4 and end:
                    need(v, f_r, b - 1)
                    finish_norm(nA, b + (4 * B - 1), r5, x5, x5_ok)
                if i == 4 and begin:
                    FC.out(v, b, X3T)
                    for t in range(D2):
                        ins = v.tensor_tensor_scan(yT[:, t, :], ah[:, t:t + 1].broadcast_to([P, S]), x3T[:, t, :], 0.0,
                                                   ALU.mult, ALU.add)
                    ins.then_inc(scan_ok, 1)
                if i == 6 and begin:
                    FC.full(v, b, SSM)
                    v.wait_ge(x3b_ok, b + 2)
                    FC.copy(v.tensor_tensor(r[:], FC.ps(SSM)[:], xb[:], ALU.add), SSM)
                    FC.out(v, b, SSM)
                    stats(nC, 2 * (b + 1) + 1, 2 * (b + 1) + 1, r)
                if i == 7 and begin:
                    need(v, x4b_ok, b + 1)
                    finish_norm(nC, 2 * (b + 1) + 1, r, x4, x4_ok)
                if i == 9 and end:
                    FC.full(v, b, ROUTE)
                    FC.copy(v.scalar_tensor_tensor(lr[:], FC.ps(ROUTE)[0:1, 0, 0:E], 1.0 / S, br1[:], ALU.mult, ALU.add), ROUTE)
                    FC.out(v, b, ROUTE)
                    apart(v)
                    v.max(lmx[:], lr[:]).then_inc(rt1, 1)
                    v.wait_ge(rt1, b)
                    apart(v)
                    v.max_index(lmi[:], lmx[:], lr[:]).then_inc(pick_ok, 1)
                if i == 16 and begin:
                    mask_of(b + 1)

            def values(b):
                FC.full(v, b, V1)
                FC.copy(v.tensor_tensor(vF, FC.ps(V1)[:], bv1[:].unsqueeze(1).broadcast_to([P, 2, D]), ALU.add), V1)

            def body(b, begin, heads, end, expert):
                if heads:
                    v.wait_ge(mask1_ok, b + 1)
                for i in range(HM + 2):
                    if heads and i < HM:
                        uu = U_C * b + (U0 + i)
                        if i >= 3:
                            v.wait_ge(turned, uu - 2)
                        masked_max(uu, i, lambda t: mask1[:], 1.0 / SQM, sc_ps[i % 2], probs[i % 3])
                    if heads and i >= 2:
                        k = i - 2
                        copy_ring(WC, b, HEADS1, U_C * b + (U0 + k), k, ring1)
                    if heads and i >= 9 and i % 4 == 1:
                        g = (i - 9) // 4
                        head_out(WC, b, HEADS1, g, b + B, U_C * b + (U0 + 4 * g + 4))
                    between(b, i, begin, end, expert)
                if heads:
                    head_out(WC, b, HEADS1, HM // 4 - 1, b + B, U_C * b + (U0 + HM))
                if begin and heads:
                    values(b)

            v.wait_ge(consts, 16)
            values(-1)
            body(-1, True, False, False, False)
            body(0, True, True, False, False)
            body(1, True, True, True, False)
            body(2, True, True, True, True)
            with v.Fori(3, B - 1) as b:
                body(b, True, True, True, True)
            body(B - 1, False, True, True, True)
            body(B, False, False, True, True)
            body(B + 1, False, False, False, True)


def lay(inputs):
    import numpy as np

    def tiled(w):
        return np.asarray(w).reshape(2, P, -1).transpose(1, 0, 2)

    def a(name):
        return np.asarray(inputs[name])

    def turned(x):
        return x.reshape(B, S, 2, P).transpose(0, 3, 2, 1)

    x, c = a("x"), a("ctx_1024")
    d = {
        "x": x.reshape(B, 2, P, D).transpose(0, 2, 1, 3),
        "xT": turned(x),
        "cT": turned(c),
        "lens": a("_lenS2"),
        "mask": a("mask_Bx1x1xS2_if1").reshape(B, S),
        "wq0": tiled(a("L0_attn_proj_q").transpose(1, 0, 2).reshape(D, H0 * P)),
        "wk0": tiled(a("L0_attn_proj_k")),
        "wv0": tiled(a("L0_attn_proj_v")),
        "wo0": a("L0_attn_proj_o").transpose(2, 0, 1),
        "wx": tiled(a("L0_xattn_W")),
        "bx": a("L0_xattn_b"),
        "ln1w": a("L0_ffn_ln1_w").reshape(2, P).T,
        "ln2w": a("L0_ffn_ln2_w"),
        "wqm": tiled(a("L0_ffn_wq").T),
        "wkm": tiled(a("L0_ffn_wk").T),
        "wvm": tiled(a("L0_ffn_wv").T),
        "wom": tiled(a("L0_ffn_wo").T),
        "wg": tiled(a("L0_ffn_gate_w").T),
        "w1": a("L0_ffn_w1").transpose(0, 2, 1).reshape(E, 2, P, F0).transpose(0, 2, 1, 3).reshape(E, P, 1, 2 * F0),
        "w3": a("L0_ffn_w3").transpose(0, 2, 1).reshape(E, 2, P, F0).transpose(0, 2, 1, 3).reshape(E, P, 1, 2 * F0),
        "w2": a("L0_ffn_w2").transpose(0, 2, 1).reshape(E, FT0, P, D).transpose(0, 2, 1, 3).reshape(E, P, 1, FT0 * D),
        "a": a("L1_attn_a").reshape(2, P).T,
        "b": a("L1_attn_b").reshape(2, P).T,
        "wout": tiled(a("L1_attn_w_out").T),
        "bout": a("L1_attn_b_out"),
        "wv1": tiled(a("L1_xattn_Wv")),
        "wk1": tiled(a("L1_xattn_Wk")),
        "wq1": tiled(a("L1_xattn_Wq")),
        "wo1": tiled(a("L1_xattn_Wo")),
        "bv1": a("L1_xattn_bv"),
        "bk1": a("L1_xattn_bk").reshape(2, P).T,
        "bq1": a("L1_xattn_bq").reshape(2, P).T,
        "bo1": a("L1_xattn_bo"),
        "wr": tiled(a("L1_ffn_Wr")),
        "br1": a("L1_ffn_br").reshape(1, E),
        "W1": a("L1_ffn_W1").reshape(E, 2, P, F1).transpose(0, 2, 1, 3),
        "b1": a("L1_ffn_b1").reshape(E, FT1, P).transpose(0, 2, 1),
        "W2": a("L1_ffn_W2").reshape(E, FT1, P, D).transpose(0, 2, 1, 3),
        "b2": a("L1_ffn_b2"),
    }
    return {k: np.ascontiguousarray(v) for k, v in d.items()}


def kernel(**inputs):
    import concourse.bacc as _bacc
    from concourse.bass_utils import run_bass_kernel_spmd as _run

    nc = _bacc.Bacc("TRN2", target_bir_lowering=False, num_devices=1)
    arrays, A = {}, {}
    for name, v in lay(inputs).items():
        arrays[f"in_{name}"] = v
        A[name] = nc.dram_tensor(f"in_{name}", v.shape, mybir.dt.from_np(v.dtype), kind="ExternalInput").ap()
    out = nc.dram_tensor("out_0", [B, S, D], F32, kind="ExternalOutput").ap()
    build(nc, A, out)
    r = _run(nc, [arrays], core_ids=[0])
    return r.results[0]["out_0"]
```
